# Optimizing a Trainium2 kernel written in Bass

```python
import numpy as np
import jax
import jax.numpy as jnp

def _softmax(x, axis=-1):
    return jax.nn.softmax(x, axis=axis)

def _gelu(x):
    return jax.nn.gelu(x, approximate=True)

def _silu(x):
    return jax.nn.silu(x)

def _sigmoid(x):
    return jax.nn.sigmoid(x)

def _layernorm(x, axis=-1, eps=1e-05):
    m = jnp.mean(x, axis=axis, keepdims=True)
    v = jnp.var(x, axis=axis, keepdims=True)
    return (x - m) / jnp.sqrt(v + eps)

def _scatter_add(tgt, idx, src, axis=0):
    return tgt.at[idx].add(src)

def _segment_sum(src, seg, n):
    return jax.ops.segment_sum(src, seg, n)
kernel_name = 'mk_xattn_ffn_d4_seqx_r8_7cae56'

def setup_inputs(seed: int=0):
    np.random.seed(seed)
    _w = jnp.asarray

    def _rec_inputs():
        import jax
        import jax.numpy as jnp
        _rk = jax.random.key(seed)
        x = -0.0002928 + 1 * jax.random.normal(jax.random.fold_in(_rk, 1), (128, 64, 128), jnp.float32)
        _lenS = 64 - jax.random.randint(jax.random.fold_in(_rk, 7), (128,), 0, max(1, 64 // 4) + 1, jnp.int32)
        _lenS2 = 64 - jax.random.randint(jax.random.fold_in(_rk, 8), (128,), 0, max(1, 64 // 4) + 1, jnp.int32)
        _ctx_1024P = jax.random.normal(jax.random.fold_in(_rk, 11), (128, 16, 128), jnp.float32)
        _ctx_1024c = jax.random.dirichlet(jax.random.fold_in(_rk, 511), 0.3 * jnp.ones((16,), jnp.float32), (128, 64))
        _ctx_1024t = jnp.einsum('bsk,bkd->bsd', _ctx_1024c, _ctx_1024P)
        _ctx_1024t = _ctx_1024t * jax.lax.rsqrt(jnp.mean(jnp.square(_ctx_1024t)) + 1e-12) * 0.953939
        ctx_1024 = -1.39393e-06 + 0.999914 * (_ctx_1024t + 0.3 * jax.random.normal(jax.random.fold_in(_rk, 611), (128, 64, 128), jnp.float32))
        fside_BxSx4_0 = jax.random.uniform(jax.random.fold_in(_rk, 13), (128, 64, 4), jnp.float32, 0.0, 0.999884)
        _validS = jnp.arange(64)[None, :] < _lenS[:, None]
        _validS2 = jnp.arange(64)[None, :] < _lenS2[:, None]
        _causal = jnp.tril(jnp.ones((64, 64), dtype=bool))
        mask_BxS2_ik0 = jnp.where(jnp.broadcast_to(_validS2[:, :], (128, 64)), 0, 1).astype(jnp.int32)
        mask_1x1xSxS2_ff0 = jnp.where(jnp.ones((1, 1, 64, 64), dtype=bool), 0.0, -1000000000.0).astype(jnp.float32)
        return (x, ctx_1024, fside_BxSx4_0, mask_BxS2_ik0, mask_1x1xSxS2_ff0)
    x, ctx_1024, fside_BxSx4_0, mask_BxS2_ik0, mask_1x1xSxS2_ff0 = _rec_inputs()

    def _L0_xattn_setup():
        import jax, jax.numpy as jnp
        import numpy as np
        D = 128
        H = 16
        HD = D // H

        def _split_heads(x):
            B, L, _ = x.shape
            return x.reshape(B, L, H, HD).transpose(0, 2, 1, 3)
        key = jax.random.key(seed)
        ks = jax.random.split(key, 12)
        B, Lq, Lk = (2, 256, 256)
        scale = 1.0 / np.sqrt(D)
        inp = {'query_input': jax.random.normal(ks[0], (B, Lq, D), jnp.float32), 'key_input': jax.random.normal(ks[1], (B, Lk, D), jnp.float32), 'value_input': jax.random.normal(ks[2], (B, Lk, D), jnp.float32), 'key_mask': jax.random.randint(ks[3], (B, Lk), 0, 2, jnp.int32), 'Wq': jax.random.normal(ks[4], (D, D), jnp.float32) * scale, 'bq': jnp.zeros((D,), jnp.float32), 'Wk': jax.random.normal(ks[5], (D, D), jnp.float32) * scale, 'bk': jnp.zeros((D,), jnp.float32), 'Wv': jax.random.normal(ks[6], (D, D), jnp.float32) * scale, 'bv': jnp.zeros((D,), jnp.float32), 'Wo': jax.random.normal(ks[7], (D, D), jnp.float32) * scale, 'bo': jnp.zeros((D,), jnp.float32)}
        return inp
    _L0_xattn_all = _L0_xattn_setup()
    _L0_xattn_in = {k: v for k, v in _L0_xattn_all.items() if k in ('Wq', 'bq', 'Wk', 'bk', 'Wv', 'bv', 'Wo', 'bo')}
    del _L0_xattn_all

    def _L0_ffn_setup():
        import jax, jax.numpy as jnp
        import numpy as np
        EPS = 1e-05
        key = jax.random.key(seed)
        kx, kw, kb = jax.random.split(key, 3)
        B, S, K, N = (8, 1024, 128, 128)
        x = jax.random.normal(kx, (B, S, K), dtype=jnp.float32)
        W = jax.random.normal(kw, (N, K), dtype=jnp.float32) * 0.02
        weight_scale = jnp.maximum(jnp.max(jnp.abs(W), axis=1, keepdims=True) / 127.0, EPS)
        weight_int8 = jnp.clip(jnp.round(W / weight_scale), -128, 127).astype(jnp.int8)
        bias = jax.random.normal(kb, (N,), dtype=jnp.float32) * 0.01
        return {'x': x, 'weight_int8': weight_int8, 'weight_scale': weight_scale, 'bias': bias}
    _L0_ffn_all = _L0_ffn_setup()
    _L0_ffn_in = {k: v for k, v in _L0_ffn_all.items() if k in ('weight_int8', 'weight_scale', 'bias')}
    del _L0_ffn_all

    def _L1_xattn_setup():
        import jax, jax.numpy as jnp
        import numpy as np
        B, S, D, H = (2, 256, 128, 16)
        key = jax.random.key(seed)
        kq, kk, kv, kw = jax.random.split(key, 4)
        Q = jax.random.normal(kq, (B, S, D), dtype=jnp.float32)
        K = jax.random.normal(kk, (B, S, D), dtype=jnp.float32)
        V = jax.random.normal(kv, (B, S, D), dtype=jnp.float32)
        Wo = jax.random.normal(kw, (D, D), dtype=jnp.float32) * (1.0 / np.sqrt(D))
        return {'Q': Q, 'K': K, 'V': V, 'Wo': Wo, 'num_heads': H}
    _L1_xattn_all = _L1_xattn_setup()
    _L1_xattn_in = {k: v for k, v in _L1_xattn_all.items() if k in ('Wo',)}
    del _L1_xattn_all

    def _L1_ffn_setup():
        import jax, jax.numpy as jnp
        import numpy as np
        EPS_NORM = 1e-08
        EPS_Q = 1e-05

        def rmsnorm(x, w):
            v = jnp.mean(jnp.square(x.astype(jnp.float32)), axis=-1, keepdims=True)
            x_hat = x * jax.lax.rsqrt(v + EPS_NORM)
            return (x_hat * w).astype(x.dtype)

        def activation_quant(x):
            scale = 127.0 / jnp.clip(jnp.max(jnp.abs(x), axis=-1, keepdims=True), EPS_Q, None)
            return jnp.clip(jnp.round(x * scale), -128, 127) / scale

        def weight_quant(w):
            scale = 1.0 / jnp.clip(jnp.mean(jnp.abs(w)), EPS_Q, None)
            return jnp.clip(jnp.round(w * scale), -1, 1) / scale

        def bitlinear(x, norm_w, w):
            x_norm = rmsnorm(x, norm_w)
            x_q = x_norm + jax.lax.stop_gradient(activation_quant(x_norm) - x_norm)
            w_q = w + jax.lax.stop_gradient(weight_quant(w) - w)
            return jnp.einsum('bsd,hd->bsh', x_q, w_q)
        key = jax.random.key(seed)
        k1, k2, k3 = jax.random.split(key, 3)
        dim, hidden = (128, 512)
        return {'x': jax.random.normal(k1, (4, 256, dim), dtype=jnp.float32), 'norm1_w': jnp.ones((dim,), jnp.float32), 'w1': jax.random.normal(k2, (hidden, dim), jnp.float32) * 0.02, 'act_scale': jnp.ones((1,), jnp.float32), 'act_bias': jnp.zeros((1,), jnp.float32), 'norm2_w': jnp.ones((hidden,), jnp.float32), 'w2': jax.random.normal(k3, (dim, hidden), jnp.float32) * 0.02}
    _L1_ffn_all = _L1_ffn_setup()
    _L1_ffn_in = {k: v for k, v in _L1_ffn_all.items() if k in ('norm1_w', 'w1', 'act_scale', 'act_bias', 'norm2_w', 'w2')}
    del _L1_ffn_all

    def _L2_xattn_setup():
        import jax, jax.numpy as jnp
        import numpy as np
        D_MODEL = 128
        H = 16
        D_K = 64
        D_V = 64
        D_G = D_MODEL // H
        WAVE_LEN = 1000.0
        B = 8
        N = 64

        def box_relational_embedding(boxes, dim_g=D_G):
            x_min, y_min, x_max, y_max = jnp.split(boxes, 4, axis=-1)
            cx = (x_min + x_max) * 0.5
            cy = (y_min + y_max) * 0.5
            w = x_max - x_min + 1.0
            h = y_max - y_min + 1.0
            delta_x = jnp.log(jnp.clip(jnp.abs((cx - jnp.swapaxes(cx, 1, 2)) / w), 0.001, None))
            delta_y = jnp.log(jnp.clip(jnp.abs((cy - jnp.swapaxes(cy, 1, 2)) / h), 0.001, None))
            delta_w = jnp.log(w / jnp.swapaxes(w, 1, 2))
            delta_h = jnp.log(h / jnp.swapaxes(h, 1, 2))
            pos = jnp.stack([delta_x, delta_y, delta_w, delta_h], axis=-1)
            n_freq = dim_g // 8
            feat_range = jnp.arange(n_freq, dtype=jnp.float32)
            dim_mat = 1.0 / WAVE_LEN ** (feat_range / n_freq)
            mul = (100.0 * pos)[..., None] * dim_mat
            b, n = (pos.shape[0], pos.shape[1])
            mul = mul.reshape(b, n, n, 4 * n_freq)
            return jnp.concatenate([jnp.sin(mul), jnp.cos(mul)], axis=-1)
        key = jax.random.key(seed)
        ks = jax.random.split(key, 12)
        s = 0.02
        inp = {'queries': jax.random.normal(ks[0], (B, N, D_MODEL), jnp.float32), 'keys': jax.random.normal(ks[1], (B, N, D_MODEL), jnp.float32), 'values': jax.random.normal(ks[2], (B, N, D_MODEL), jnp.float32), 'boxes': jax.random.uniform(ks[3], (B, N, 4), jnp.float32), 'Wq': jax.random.normal(ks[4], (H * D_K, D_MODEL), jnp.float32) * s, 'bq': jnp.zeros((H * D_K,), jnp.float32), 'Wk': jax.random.normal(ks[5], (H * D_K, D_MODEL), jnp.float32) * s, 'bk': jnp.zeros((H * D_K,), jnp.float32), 'Wv': jax.random.normal(ks[6], (H * D_V, D_MODEL), jnp.float32) * s, 'bv': jnp.zeros((H * D_V,), jnp.float32), 'Wo': jax.random.normal(ks[7], (D_MODEL, H * D_V), jnp.float32) * s, 'bo': jnp.zeros((D_MODEL,), jnp.float32), 'Wg': jax.random.normal(ks[8], (H, D_G), jnp.float32) * s, 'bg': jnp.zeros((H,), jnp.float32)}
        return inp
    _L2_xattn_all = _L2_xattn_setup()
    _L2_xattn_in = {k: v for k, v in _L2_xattn_all.items() if k in ('Wq', 'bq', 'Wk', 'bk', 'Wv', 'bv', 'Wo', 'bo', 'Wg', 'bg')}
    del _L2_xattn_all

    def _L2_ffn_setup():
        import jax, jax.numpy as jnp
        import numpy as np
        E = 8
        K = 2
        D = 128
        H = 512
        CAP_FACTOR = 1.0
        key = jax.random.key(seed)
        ks = jax.random.split(key, 5)
        x = jax.random.normal(ks[0], (4, 256, D), jnp.float32)
        gate_w = jax.random.normal(ks[1], (E, D), jnp.float32) * 0.02
        fc1_w = jax.random.normal(ks[2], (E, H, D), jnp.float32) * 0.02
        fc1_b = jnp.zeros((E, 1, H), jnp.float32)
        fc2_w = jax.random.normal(ks[3], (E, H, D), jnp.float32) * 0.02
        fc2_b = jnp.zeros((E, 1, D), jnp.float32)
        return {'x': x, 'gate_w': gate_w, 'fc1_w': fc1_w, 'fc1_b': fc1_b, 'fc2_w': fc2_w, 'fc2_b': fc2_b}
    _L2_ffn_all = _L2_ffn_setup()
    _L2_ffn_in = {k: v for k, v in _L2_ffn_all.items() if k in ('gate_w', 'fc1_w', 'fc1_b', 'fc2_w', 'fc2_b')}
    del _L2_ffn_all

    def _L3_xattn_setup():
        import jax, jax.numpy as jnp
        import numpy as np
        D_MODEL = 128
        N_HEADS = 16
        HEAD_DIM = D_MODEL // N_HEADS
        key = jax.random.key(seed)
        ks = jax.random.split(key, 12)
        B, S = (2, 256)
        s = 1.0 / np.sqrt(D_MODEL)
        return {'Q': jax.random.normal(ks[0], (B, S, D_MODEL), jnp.float32), 'K': jax.random.normal(ks[1], (B, S, D_MODEL), jnp.float32), 'V': jax.random.normal(ks[2], (B, S, D_MODEL), jnp.float32), 'mask': jnp.zeros((1, 1, S, S), jnp.float32), 'Wq': jax.random.normal(ks[3], (D_MODEL, D_MODEL), jnp.float32) * s, 'bq': jnp.zeros((D_MODEL,), jnp.float32), 'Wk': jax.random.normal(ks[4], (D_MODEL, D_MODEL), jnp.float32) * s, 'bk': jnp.zeros((D_MODEL,), jnp.float32), 'Wv': jax.random.normal(ks[5], (D_MODEL, D_MODEL), jnp.float32) * s, 'bv': jnp.zeros((D_MODEL,), jnp.float32), 'Wo': jax.random.normal(ks[6], (D_MODEL, D_MODEL), jnp.float32) * s, 'bo': jnp.zeros((D_MODEL,), jnp.float32)}
    _L3_xattn_all = _L3_xattn_setup()
    _L3_xattn_in = {k: v for k, v in _L3_xattn_all.items() if k in ('Wq', 'bq', 'Wk', 'bk', 'Wv', 'bv', 'Wo', 'bo')}
    del _L3_xattn_all

    def _L3_ffn_setup():
        import jax, jax.numpy as jnp
        import numpy as np
        EMB = 128
        HID = 256
        HEADS = 16
        HEAD_DIM = EMB // HEADS
        EXPERTS = 8
        TOPK = 2
        EPS = 1e-05

        def layernorm(x, scale, shift):
            mean = jnp.mean(x, axis=-1, keepdims=True)
            var = jnp.mean((x - mean) ** 2, axis=-1, keepdims=True)
            return scale * (x - mean) / jnp.sqrt(var + EPS) + shift

        def attention(x, wq, wk, wv, wo, bo):
            b, t, _ = x.shape
            q = (x @ wq).reshape(b, t, HEADS, HEAD_DIM)
            k = (x @ wk).reshape(b, t, HEADS, HEAD_DIM)
            v = (x @ wv).reshape(b, t, HEADS, HEAD_DIM)
            scores = jnp.einsum('bqhd,bkhd->bhqk', q, k)
            mask = jnp.arange(t)[:, None] < jnp.arange(t)[None, :]
            scores = jnp.where(mask, -jnp.inf, scores)
            attn = jax.nn.softmax(scores / np.sqrt(HEAD_DIM), axis=-1)
            ctx = jnp.einsum('bhqk,bkhd->bqhd', attn, v).reshape(b, t, EMB)
            return ctx @ wo + bo

        def moe_ff(x, gate_w, w1, w2, w3):
            b, t, d = x.shape
            xf = x.reshape(b * t, d)
            scores = xf @ gate_w
            topk_scores, topk_idx = jax.lax.top_k(scores, TOPK)
            topk_probs = jax.nn.softmax(topk_scores, axis=-1)
            weight = jnp.sum(jax.nn.one_hot(topk_idx, EXPERTS, dtype=xf.dtype) * topk_probs[..., None], axis=1)
            h = jax.nn.silu(jnp.einsum('td,edh->eth', xf, w1)) * jnp.einsum('td,edh->eth', xf, w2)
            out_e = jnp.einsum('eth,ehd->etd', h, w3)
            out = jnp.einsum('etd,te->td', out_e, weight)
            return out.reshape(b, t, d)
        key = jax.random.key(seed)
        ks = jax.random.split(key, 12)
        s = lambda k, shape, fan: jax.random.normal(k, shape, jnp.float32) / np.sqrt(fan)
        return {'x': jax.random.normal(ks[0], (2, 256, EMB), jnp.float32), 'ln1_scale': jnp.ones((EMB,), jnp.float32), 'ln1_shift': jnp.zeros((EMB,), jnp.float32), 'wq': s(ks[1], (EMB, EMB), EMB), 'wk': s(ks[2], (EMB, EMB), EMB), 'wv': s(ks[3], (EMB, EMB), EMB), 'wo': s(ks[4], (EMB, EMB), EMB), 'bo': jnp.zeros((EMB,), jnp.float32), 'ln2_scale': jnp.ones((EMB,), jnp.float32), 'ln2_shift': jnp.zeros((EMB,), jnp.float32), 'gate_w': s(ks[5], (EMB, EXPERTS), EMB), 'w1': s(ks[6], (EXPERTS, EMB, HID), EMB), 'w2': s(ks[7], (EXPERTS, EMB, HID), EMB), 'w3': s(ks[8], (EXPERTS, HID, EMB), HID)}
    _L3_ffn_all = _L3_ffn_setup()
    _L3_ffn_in = {k: v for k, v in _L3_ffn_all.items() if k in ('ln1_scale', 'ln1_shift', 'wq', 'wk', 'wv', 'wo', 'bo', 'ln2_scale', 'ln2_shift', 'gate_w', 'w1', 'w2', 'w3')}
    del _L3_ffn_all
    return {'x': x, 'ctx_1024': ctx_1024, 'fside_BxSx4_0': fside_BxSx4_0, 'mask_BxS2_ik0': mask_BxS2_ik0, 'mask_1x1xSxS2_ff0': mask_1x1xSxS2_ff0, 'L0_xattn_Wq': _L0_xattn_in['Wq'], 'L0_xattn_bq': _L0_xattn_in['bq'], 'L0_xattn_Wk': _L0_xattn_in['Wk'], 'L0_xattn_bk': _L0_xattn_in['bk'], 'L0_xattn_Wv': _L0_xattn_in['Wv'], 'L0_xattn_bv': _L0_xattn_in['bv'], 'L0_xattn_Wo': _L0_xattn_in['Wo'], 'L0_xattn_bo': _L0_xattn_in['bo'], 'L0_ffn_weight_int8': _L0_ffn_in['weight_int8'], 'L0_ffn_weight_scale': _L0_ffn_in['weight_scale'], 'L0_ffn_bias': _L0_ffn_in['bias'], 'L1_xattn_Wo': _L1_xattn_in['Wo'], 'L1_ffn_norm1_w': _L1_ffn_in['norm1_w'], 'L1_ffn_w1': _L1_ffn_in['w1'], 'L1_ffn_act_scale': _L1_ffn_in['act_scale'], 'L1_ffn_act_bias': _L1_ffn_in['act_bias'], 'L1_ffn_norm2_w': _L1_ffn_in['norm2_w'], 'L1_ffn_w2': _L1_ffn_in['w2'], 'L2_xattn_Wq': _L2_xattn_in['Wq'], 'L2_xattn_bq': _L2_xattn_in['bq'], 'L2_xattn_Wk': _L2_xattn_in['Wk'], 'L2_xattn_bk': _L2_xattn_in['bk'], 'L2_xattn_Wv': _L2_xattn_in['Wv'], 'L2_xattn_bv': _L2_xattn_in['bv'], 'L2_xattn_Wo': _L2_xattn_in['Wo'], 'L2_xattn_bo': _L2_xattn_in['bo'], 'L2_xattn_Wg': _L2_xattn_in['Wg'], 'L2_xattn_bg': _L2_xattn_in['bg'], 'L2_ffn_gate_w': _L2_ffn_in['gate_w'], 'L2_ffn_fc1_w': _L2_ffn_in['fc1_w'], 'L2_ffn_fc1_b': _L2_ffn_in['fc1_b'], 'L2_ffn_fc2_w': _L2_ffn_in['fc2_w'], 'L2_ffn_fc2_b': _L2_ffn_in['fc2_b'], 'L3_xattn_Wq': _L3_xattn_in['Wq'], 'L3_xattn_bq': _L3_xattn_in['bq'], 'L3_xattn_Wk': _L3_xattn_in['Wk'], 'L3_xattn_bk': _L3_xattn_in['bk'], 'L3_xattn_Wv': _L3_xattn_in['Wv'], 'L3_xattn_bv': _L3_xattn_in['bv'], 'L3_xattn_Wo': _L3_xattn_in['Wo'], 'L3_xattn_bo': _L3_xattn_in['bo'], 'L3_ffn_ln1_scale': _L3_ffn_in['ln1_scale'], 'L3_ffn_ln1_shift': _L3_ffn_in['ln1_shift'], 'L3_ffn_wq': _L3_ffn_in['wq'], 'L3_ffn_wk': _L3_ffn_in['wk'], 'L3_ffn_wv': _L3_ffn_in['wv'], 'L3_ffn_wo': _L3_ffn_in['wo'], 'L3_ffn_bo': _L3_ffn_in['bo'], 'L3_ffn_ln2_scale': _L3_ffn_in['ln2_scale'], 'L3_ffn_ln2_shift': _L3_ffn_in['ln2_shift'], 'L3_ffn_gate_w': _L3_ffn_in['gate_w'], 'L3_ffn_w1': _L3_ffn_in['w1'], 'L3_ffn_w2': _L3_ffn_in['w2'], 'L3_ffn_w3': _L3_ffn_in['w3']}

def reference(x, ctx_1024, fside_BxSx4_0, mask_BxS2_ik0, mask_1x1xSxS2_ff0, L0_xattn_Wq, L0_xattn_bq, L0_xattn_Wk, L0_xattn_bk, L0_xattn_Wv, L0_xattn_bv, L0_xattn_Wo, L0_xattn_bo, L0_ffn_weight_int8, L0_ffn_weight_scale, L0_ffn_bias, L1_xattn_Wo, L1_ffn_norm1_w, L1_ffn_w1, L1_ffn_act_scale, L1_ffn_act_bias, L1_ffn_norm2_w, L1_ffn_w2, L2_xattn_Wq, L2_xattn_bq, L2_xattn_Wk, L2_xattn_bk, L2_xattn_Wv, L2_xattn_bv, L2_xattn_Wo, L2_xattn_bo, L2_xattn_Wg, L2_xattn_bg, L2_ffn_gate_w, L2_ffn_fc1_w, L2_ffn_fc1_b, L2_ffn_fc2_w, L2_ffn_fc2_b, L3_xattn_Wq, L3_xattn_bq, L3_xattn_Wk, L3_xattn_bk, L3_xattn_Wv, L3_xattn_bv, L3_xattn_Wo, L3_xattn_bo, L3_ffn_ln1_scale, L3_ffn_ln1_shift, L3_ffn_wq, L3_ffn_wk, L3_ffn_wv, L3_ffn_wo, L3_ffn_bo, L3_ffn_ln2_scale, L3_ffn_ln2_shift, L3_ffn_gate_w, L3_ffn_w1, L3_ffn_w2, L3_ffn_w3):
    import jax
    import jax.numpy as jnp

    def _L0_xattn_ref(query_input, key_input, value_input, key_mask, Wq, bq, Wk, bk, Wv, bv, Wo, bo):
        import jax, jax.numpy as jnp
        import numpy as np
        D = 128
        H = 16
        HD = D // H

        def _split_heads(x):
            B, L, _ = x.shape
            return x.reshape(B, L, H, HD).transpose(0, 2, 1, 3)
        B = query_input.shape[0]
        q = _split_heads(query_input @ Wq.T + bq)
        k = _split_heads(key_input @ Wk.T + bk)
        v = _split_heads(value_input @ Wv.T + bv)
        scores = jnp.einsum('bhqd,bhkd->bhqk', q, k) / jnp.sqrt(jnp.float32(HD))
        mask = key_mask[:, None, None, :]
        scores = jnp.where(mask == 0, jnp.float32(-1e+30), scores)
        attn = jax.nn.softmax(scores, axis=-1)
        ctx = jnp.einsum('bhqk,bhkd->bhqd', attn, v)
        ctx = ctx.transpose(0, 2, 1, 3).reshape(B, -1, D)
        return ctx @ Wo.T + bo

    def _L0_ffn_ref(x, weight_int8, weight_scale, bias):
        import jax, jax.numpy as jnp
        import numpy as np
        EPS = 1e-05
        B, S, K = x.shape
        x2 = x.reshape(-1, K)
        x_scale = jnp.maximum(jnp.abs(x2).max() / 127.0, EPS)
        x_int8 = jnp.clip(jnp.round(x2 / x_scale), -128, 127).astype(jnp.int8)
        acc_i32 = jax.lax.dot_general(x_int8, weight_int8.T, dimension_numbers=(((1,), (0,)), ((), ())), preferred_element_type=jnp.int32)
        out = acc_i32.astype(jnp.float32) * x_scale * weight_scale.T
        out = out + bias
        return out.reshape(B, S, -1)

    def _L1_xattn_ref(Q, K, V, Wo, num_heads):
        import jax, jax.numpy as jnp
        import numpy as np
        B, S, D, H = (2, 256, 128, 16)
        b, s, d = Q.shape
        dk = d // num_heads
        q = Q.reshape(b, s, num_heads, dk).transpose(0, 2, 1, 3)
        k = K.reshape(b, s, num_heads, dk).transpose(0, 2, 1, 3)
        v = V.reshape(b, s, num_heads, dk).transpose(0, 2, 1, 3)
        scale = 1.0 / jnp.sqrt(jnp.asarray(dk, dtype=q.dtype))
        logits = jnp.einsum('bhqd,bhkd->bhqk', q, k) * scale
        probs = jax.nn.softmax(logits, axis=-1).astype(q.dtype)
        o = jnp.einsum('bhqk,bhkd->bhqd', probs, v)
        o = o.transpose(0, 2, 1, 3).reshape(b, s, d)
        return jnp.einsum('dk,bsk->bsd', Wo, o)

    def _L1_ffn_ref(x, norm1_w, w1, act_scale, act_bias, norm2_w, w2):
        import jax, jax.numpy as jnp
        import numpy as np
        EPS_NORM = 1e-08
        EPS_Q = 1e-05

        def rmsnorm(x, w):
            v = jnp.mean(jnp.square(x.astype(jnp.float32)), axis=-1, keepdims=True)
            x_hat = x * jax.lax.rsqrt(v + EPS_NORM)
            return (x_hat * w).astype(x.dtype)

        def activation_quant(x):
            scale = 127.0 / jnp.clip(jnp.max(jnp.abs(x), axis=-1, keepdims=True), EPS_Q, None)
            return jnp.clip(jnp.round(x * scale), -128, 127) / scale

        def weight_quant(w):
            scale = 1.0 / jnp.clip(jnp.mean(jnp.abs(w)), EPS_Q, None)
            return jnp.clip(jnp.round(w * scale), -1, 1) / scale

        def bitlinear(x, norm_w, w):
            x_norm = rmsnorm(x, norm_w)
            x_q = x_norm + jax.lax.stop_gradient(activation_quant(x_norm) - x_norm)
            w_q = w + jax.lax.stop_gradient(weight_quant(w) - w)
            return jnp.einsum('bsd,hd->bsh', x_q, w_q)
        h = bitlinear(x, norm1_w, w1)
        h = act_scale * jnp.square(jax.nn.relu(h)) + act_bias
        y = bitlinear(h, norm2_w, w2)
        return y

    def _L2_xattn_ref(queries, keys, values, boxes, Wq, bq, Wk, bk, Wv, bv, Wo, bo, Wg, bg):
        import jax, jax.numpy as jnp
        import numpy as np
        D_MODEL = 128
        H = 16
        D_K = 64
        D_V = 64
        D_G = D_MODEL // H
        WAVE_LEN = 1000.0
        B = 8
        N = 64

        def box_relational_embedding(boxes, dim_g=D_G):
            x_min, y_min, x_max, y_max = jnp.split(boxes, 4, axis=-1)
            cx = (x_min + x_max) * 0.5
            cy = (y_min + y_max) * 0.5
            w = x_max - x_min + 1.0
            h = y_max - y_min + 1.0
            delta_x = jnp.log(jnp.clip(jnp.abs((cx - jnp.swapaxes(cx, 1, 2)) / w), 0.001, None))
            delta_y = jnp.log(jnp.clip(jnp.abs((cy - jnp.swapaxes(cy, 1, 2)) / h), 0.001, None))
            delta_w = jnp.log(w / jnp.swapaxes(w, 1, 2))
            delta_h = jnp.log(h / jnp.swapaxes(h, 1, 2))
            pos = jnp.stack([delta_x, delta_y, delta_w, delta_h], axis=-1)
            n_freq = dim_g // 8
            feat_range = jnp.arange(n_freq, dtype=jnp.float32)
            dim_mat = 1.0 / WAVE_LEN ** (feat_range / n_freq)
            mul = (100.0 * pos)[..., None] * dim_mat
            b, n = (pos.shape[0], pos.shape[1])
            mul = mul.reshape(b, n, n, 4 * n_freq)
            return jnp.concatenate([jnp.sin(mul), jnp.cos(mul)], axis=-1)
        b, nq, _ = queries.shape
        nk = keys.shape[1]
        emb = box_relational_embedding(boxes)
        g = jax.nn.relu(jnp.einsum('bnmd,hd->bhnm', emb, Wg) + bg[None, :, None, None])
        q = (queries @ Wq.T + bq).reshape(b, nq, H, D_K).transpose(0, 2, 1, 3)
        k = (keys @ Wk.T + bk).reshape(b, nk, H, D_K).transpose(0, 2, 1, 3)
        v = (values @ Wv.T + bv).reshape(b, nk, H, D_V).transpose(0, 2, 1, 3)
        a = jnp.einsum('bhqd,bhkd->bhqk', q, k) / jnp.sqrt(jnp.float32(D_K))
        mn = jax.nn.softmax(jnp.log(jnp.clip(g, 1e-06, None)) + a, axis=-1)
        out = jnp.einsum('bhqk,bhkd->bqhd', mn, v).reshape(b, nq, H * D_V)
        return out @ Wo.T + bo

    def _L2_ffn_ref(x, gate_w, fc1_w, fc1_b, fc2_w, fc2_b):
        import jax, jax.numpy as jnp
        import numpy as np
        E = 8
        K = 2
        D = 128
        H = 512
        CAP_FACTOR = 1.0
        B, S, Dm = x.shape
        xf = x.reshape(-1, Dm)
        N = xf.shape[0]
        cap = int(K * CAP_FACTOR * ((N + E - 1) // E))
        logits = xf @ gate_w.T
        scores = jax.nn.softmax(logits, axis=-1)
        topv, topi = jax.lax.top_k(scores, K)
        gates = topv / jnp.sum(topv, axis=-1, keepdims=True)
        offset = jnp.zeros((E,), jnp.int32)
        locs = []
        for j in range(K):
            mask = jax.nn.one_hot(topi[:, j], E, dtype=jnp.int32)
            loc_in = jnp.cumsum(mask, axis=0) - 1 + offset[None, :]
            locs.append(jnp.take_along_axis(loc_in, topi[:, j:j + 1], axis=1)[:, 0])
            offset = offset + mask.sum(axis=0)
        loc = jnp.stack(locs, axis=1)
        valid = loc < cap
        flat_idx = jnp.where(valid, topi * cap + loc, 0)
        w = valid.astype(xf.dtype)
        disp = jnp.zeros((E * cap, Dm), xf.dtype)
        disp = disp.at[flat_idx.reshape(-1)].add((xf[:, None, :] * w[:, :, None]).reshape(-1, Dm))
        de = disp.reshape(E, cap, Dm)
        h = jax.nn.relu(jnp.einsum('ecd,ehd->ech', de, fc1_w) + fc1_b)
        eo = jnp.einsum('ech,ehd->ecd', h, fc2_w) + fc2_b
        gathered = eo.reshape(E * cap, Dm)[flat_idx]
        out = jnp.sum(gathered * (gates * w)[:, :, None], axis=1)
        return out.reshape(B, S, Dm)

    def _L3_xattn_ref(Q, K, V, mask, Wq, bq, Wk, bk, Wv, bv, Wo, bo):
        import jax, jax.numpy as jnp
        import numpy as np
        D_MODEL = 128
        N_HEADS = 16
        HEAD_DIM = D_MODEL // N_HEADS
        B, Sq, _ = Q.shape
        Sk = K.shape[1]
        q = (Q @ Wq.T + bq).reshape(B, Sq, N_HEADS, HEAD_DIM).transpose(0, 2, 1, 3)
        k = (K @ Wk.T + bk).reshape(B, Sk, N_HEADS, HEAD_DIM).transpose(0, 2, 1, 3)
        v = (V @ Wv.T + bv).reshape(B, Sk, N_HEADS, HEAD_DIM).transpose(0, 2, 1, 3)
        scores = jnp.einsum('bhqd,bhkd->bhqk', q, k) / jnp.sqrt(jnp.asarray(HEAD_DIM, q.dtype))
        scores = scores + mask
        attn = jax.nn.softmax(scores, axis=-1)
        out = jnp.einsum('bhqk,bhkd->bhqd', attn, v)
        out = out.transpose(0, 2, 1, 3).reshape(B, Sq, D_MODEL)
        return out @ Wo.T + bo

    def _L3_ffn_ref(x, ln1_scale, ln1_shift, wq, wk, wv, wo, bo, ln2_scale, ln2_shift, gate_w, w1, w2, w3):
        import jax, jax.numpy as jnp
        import numpy as np
        EMB = 128
        HID = 256
        HEADS = 16
        HEAD_DIM = EMB // HEADS
        EXPERTS = 8
        TOPK = 2
        EPS = 1e-05

        def layernorm(x, scale, shift):
            mean = jnp.mean(x, axis=-1, keepdims=True)
            var = jnp.mean((x - mean) ** 2, axis=-1, keepdims=True)
            return scale * (x - mean) / jnp.sqrt(var + EPS) + shift

        def attention(x, wq, wk, wv, wo, bo):
            b, t, _ = x.shape
            q = (x @ wq).reshape(b, t, HEADS, HEAD_DIM)
            k = (x @ wk).reshape(b, t, HEADS, HEAD_DIM)
            v = (x @ wv).reshape(b, t, HEADS, HEAD_DIM)
            scores = jnp.einsum('bqhd,bkhd->bhqk', q, k)
            mask = jnp.arange(t)[:, None] < jnp.arange(t)[None, :]
            scores = jnp.where(mask, -jnp.inf, scores)
            attn = jax.nn.softmax(scores / np.sqrt(HEAD_DIM), axis=-1)
            ctx = jnp.einsum('bhqk,bkhd->bqhd', attn, v).reshape(b, t, EMB)
            return ctx @ wo + bo

        def moe_ff(x, gate_w, w1, w2, w3):
            b, t, d = x.shape
            xf = x.reshape(b * t, d)
            scores = xf @ gate_w
            topk_scores, topk_idx = jax.lax.top_k(scores, TOPK)
            topk_probs = jax.nn.softmax(topk_scores, axis=-1)
            weight = jnp.sum(jax.nn.one_hot(topk_idx, EXPERTS, dtype=xf.dtype) * topk_probs[..., None], axis=1)
            h = jax.nn.silu(jnp.einsum('td,edh->eth', xf, w1)) * jnp.einsum('td,edh->eth', xf, w2)
            out_e = jnp.einsum('eth,ehd->etd', h, w3)
            out = jnp.einsum('etd,te->td', out_e, weight)
            return out.reshape(b, t, d)
        h = layernorm(x, ln1_scale, ln1_shift)
        x = x + attention(h, wq, wk, wv, wo, bo)
        h = layernorm(x, ln2_scale, ln2_shift)
        x = x + moe_ff(h, gate_w, w1, w2, w3)
        return x
    x = x + _L0_xattn_ref(_layernorm(x, axis=-1), ctx_1024, ctx_1024, mask_BxS2_ik0, L0_xattn_Wq, L0_xattn_bq, L0_xattn_Wk, L0_xattn_bk, L0_xattn_Wv, L0_xattn_bv, L0_xattn_Wo, L0_xattn_bo)
    x = x + _L0_ffn_ref(_layernorm(x, axis=-1), L0_ffn_weight_int8, L0_ffn_weight_scale, L0_ffn_bias)
    x = x + _L1_xattn_ref(_layernorm(x, axis=-1), ctx_1024, ctx_1024, L1_xattn_Wo, 16)
    x = x + _L1_ffn_ref(_layernorm(x, axis=-1), L1_ffn_norm1_w, L1_ffn_w1, L1_ffn_act_scale, L1_ffn_act_bias, L1_ffn_norm2_w, L1_ffn_w2)
    x = x + _L2_xattn_ref(_layernorm(x, axis=-1), ctx_1024, ctx_1024, fside_BxSx4_0, L2_xattn_Wq, L2_xattn_bq, L2_xattn_Wk, L2_xattn_bk, L2_xattn_Wv, L2_xattn_bv, L2_xattn_Wo, L2_xattn_bo, L2_xattn_Wg, L2_xattn_bg)
    x = x + _L2_ffn_ref(_layernorm(x, axis=-1), L2_ffn_gate_w, L2_ffn_fc1_w, L2_ffn_fc1_b, L2_ffn_fc2_w, L2_ffn_fc2_b)
    x = x + _L3_xattn_ref(_layernorm(x, axis=-1), ctx_1024, ctx_1024, mask_1x1xSxS2_ff0, L3_xattn_Wq, L3_xattn_bq, L3_xattn_Wk, L3_xattn_bk, L3_xattn_Wv, L3_xattn_bv, L3_xattn_Wo, L3_xattn_bo)
    x = x + _L3_ffn_ref(_layernorm(x, axis=-1), L3_ffn_ln1_scale, L3_ffn_ln1_shift, L3_ffn_wq, L3_ffn_wk, L3_ffn_wv, L3_ffn_wo, L3_ffn_bo, L3_ffn_ln2_scale, L3_ffn_ln2_shift, L3_ffn_gate_w, L3_ffn_w1, L3_ffn_w2, L3_ffn_w3)
    return x

_drawn_inputs = setup_inputs


def setup_inputs(seed=0):
    import zlib

    import numpy as np

    out = dict(_drawn_inputs(seed))
    spreads = {'L0_xattn_bq': (0.0, 0.1),
     'L0_xattn_bk': (0.0, 0.8),
     'L0_xattn_bv': (0.0, 0.1),
     'L0_xattn_bo': (0.0, 0.1),
     'L1_ffn_norm1_w': (1.0, 0.2),
     'L1_ffn_norm2_w': (1.0, 0.2),
     'L2_xattn_bq': (0.0, 0.8),
     'L2_xattn_bk': (0.0, 0.8),
     'L2_xattn_bv': (0.0, 0.1),
     'L2_xattn_bo': (0.0, 0.1),
     'L2_xattn_bg': (0.0, 0.277),
     'L2_ffn_fc1_b': (0.0, 0.404),
     'L2_ffn_fc2_b': (0.0, 0.1),
     'L3_xattn_bq': (0.0, 0.314),
     'L3_xattn_bk': (0.0, 0.8),
     'L3_xattn_bv': (0.0, 0.1),
     'L3_xattn_bo': (0.0, 0.1),
     'L3_ffn_ln1_scale': (1.0, 0.2),
     'L3_ffn_ln1_shift': (0.0, 0.1),
     'L3_ffn_bo': (0.0, 0.1),
     'L3_ffn_ln2_scale': (1.0, 0.2),
     'L3_ffn_ln2_shift': (0.0, 0.1)}
    factors = {'L0_ffn_bias': 3.734, 'L2_xattn_Wq': 8.0, 'L2_xattn_Wk': 8.0}
    for name, (base, spread) in spreads.items():
        noise = np.random.default_rng([zlib.crc32(name.encode()), seed]).standard_normal(out[name].shape)
        drawn = base * np.exp(spread * noise) if base else spread * noise
        out[name] = jnp.asarray(drawn.astype(out[name].dtype))
    for name, factor in factors.items():
        out[name] = (out[name] * factor).astype(out[name].dtype)
    return out
```

```python
from contextlib import ExitStack

import concourse.bass as bass
from concourse import mybir

F32 = mybir.dt.float32
BF16 = mybir.dt.bfloat16
I32 = mybir.dt.int32
U32 = mybir.dt.uint32
I8 = mybir.dt.int8
ALU = mybir.AluOpType
ACT = mybir.ActivationFunctionType
X = mybir.AxisListType.X

P = 128
SEQ = 64
PAIR = P // SEQ
HEADS = 16
HD = P // HEADS
GROUP = 32 // HD
STREAMS = 4
LN_EPS = 1e-5
MASKED = -1e30


def bcast(ap, dims):
    return bass.AP(ap.tensor, ap.offset, [list(ap.ap[0])] + [list(d) for d in dims])


def row_on_all(dram, n, parts=P, offset=0):
    return bass.AP(dram.tensor, dram.offset + offset, [[0, parts], [1, n]])


def column(dram, n=P, offset=0):
    return bass.AP(dram.tensor, dram.offset + offset, [[1, n], [1, 1]])


class Resident:

    def __init__(self, sb, tiles):
        self.tiles = tiles
        self.x = sb("x_resident", [P, tiles, P])
        self.ident = sb("ident", [P, P])
        self.ident_bf = sb("ident_bf", [P, P], BF16)
        self.group_mask = sb("group_mask", [P, GROUP])
        self.ones_row = sb("ones_row", [1, P])
        self.ones_full = sb("ones_full", [P, P])
        self.minus_half = sb("minus_half", [P, 2 * STREAMS])


class Phase:

    def __init__(self, nc, name):
        self.nc, self.name, self.stack, self.sems = nc, name, ExitStack(), []

    def sb(self, label, shape, dt=F32):
        return self.stack.enter_context(self.nc.sbuf_tensor(f"{self.name}_{label}", shape, dt))

    def psum(self):
        return self.stack.enter_context(self.nc.psum_tensor(f"{self.name}_psum", [P, 8, 512], F32))

    def sem(self, label):
        self.sems.append(self.nc.alloc_semaphore(f"{self.name}_{label}"))
        return self.sems[-1]

    def end(self):
        self.nc.clear_and_free_semaphores(self.sems)
        self.nc.all_engine_barrier()
        self.stack.close()


def transpose_weights(nc, ph, loads, turned, ident, psum):
    weights_loaded = ph.sem("weights_loaded")
    block_turned = ph.sem("block_turned")
    block_kept = ph.sem("block_kept")
    n_loads = len(loads)
    with nc.Block() as block:
        @block.sync
        def _(sp):
            for tile, source in loads:
                sp.dma_start(tile, source, allow_slow_non_contiguous=True).then_inc(weights_loaded, 16)
            sp.wait_ge(weights_loaded, 16 * n_loads)

        @block.tensor
        def _(pe):
            pe.wait_ge(weights_loaded, 16 * n_loads)
            for n, (dst, src) in enumerate(turned):
                if n >= 8:
                    pe.wait_ge(block_kept, n - 7)
                rows, cols = src.shape
                nc.tensor.transpose(psum[0:cols, n % 8, 0:rows], src, ident[0:rows, 0:rows]).then_inc(block_turned, 1)

        @block.vector
        def _(dve):
            for n, (dst, src) in enumerate(turned):
                rows, cols = src.shape
                dve.wait_ge(block_turned, n + 1)
                nc.vector.tensor_copy(dst, psum[0:cols, n % 8, 0:rows]).then_inc(block_kept, 1)


def tile_of(g, t):
    return g.x[:, bass.ds(t, 1), :].rearrange("p a d -> p (a d)")


class LayernormState:

    def __init__(self, ph, tag="", n=STREAMS):
        self.n = n
        self.stats = ph.sb("stats" + tag, [P, n, 6])
        self.mean_var = ph.sb("mean_var" + tag, [P, n, 2])
        self.var_eps = ph.sb("var_eps" + tag, [P, n])
        self.rstd = ph.sb("rstd" + tag, [P, n])
        self.stats_ready = ph.sem("stats_ready" + tag)
        self.mean_ready = ph.sem("mean_ready" + tag)
        self.var_eps_ready = ph.sem("var_eps_ready" + tag)
        self.rstd_ready = ph.sem("rstd_ready" + tag)


def group_statistics(nc, dve, g, i, c0, ln, t0=None):
    t0 = c0 if t0 is None else t0
    last = ln.n - 1
    nc.vector.bn_stats(ln.stats[:, 0, :], tile_of(g, t0)).then_inc(ln.stats_ready, 1)
    for s in range(1, ln.n):
        dve.wait_ge(ln.stats_ready, c0 + s)
        nc.vector.bn_stats(ln.stats[:, s, :], tile_of(g, t0 + s)).then_inc(ln.stats_ready, 1)
        nc.vector.bn_aggr(ln.mean_var[:, s - 1, :], ln.stats[:, s - 1, :]).then_inc(ln.mean_ready, 1)
    dve.wait_ge(ln.mean_ready, c0 + last)
    dve.wait_ge(ln.stats_ready, c0 + ln.n)
    nc.vector.tensor_scalar(ln.var_eps[:, 0:last], ln.mean_var[:, 0:last, 1], LN_EPS, None, ALU.add)
    nc.vector.bn_aggr(ln.mean_var[:, last, :], ln.stats[:, last, :]).then_inc(ln.mean_ready, 1)
    dve.wait_ge(ln.mean_ready, c0 + ln.n)
    nc.vector.tensor_scalar(ln.var_eps[:, last:], ln.mean_var[:, last, 1:2], LN_EPS, None, ALU.add).then_inc(ln.var_eps_ready, 1)


def group_rstd(nc, pool, g, i, ln):
    pool.wait_ge(ln.var_eps_ready, i + 1)
    nc.gpsimd.tensor_tensor(ln.rstd[:, :], ln.var_eps[:, :], g.minus_half[:, 0:ln.n], ALU.pow).then_inc(ln.rstd_ready, 1)


class Tile:

    def __init__(self, base, offset, load_base):
        self.t = base + offset
        self.stream = offset % STREAMS
        self.loads = load_base + 16 * (offset // STREAMS)


def run_tiles(engine, tiles, step):
    def step_at(n):
        step(*[Tile(0, n + k, 0) if 0 <= n + k < tiles else None for k in (1, 0, -1, -2, -3)])

    for n in range(STREAMS):
        step_at(n)
    with engine.Fori(0, tiles // STREAMS - 2) as i:
        base, load_base = engine.snap(i * STREAMS), engine.snap(i * 16)
        for m in range(STREAMS):
            step(*[Tile(base, STREAMS + m + k, load_base) for k in (1, 0, -1, -2, -3)])
    for n in range(tiles - STREAMS, tiles + 3):
        step_at(n)


def tile_rstd(nc, pool, g, tile, ln):
    pool.wait_ge(ln.var_eps_ready, tile.t + 1)
    nc.gpsimd.tensor_tensor(ln.rstd[:, :], ln.var_eps[:, :], g.minus_half[:, 0:1], ALU.pow).then_inc(ln.rstd_ready, 1)


def attention_phase(nc, name, g, wq=None, bq=None, wk=None, bk=None, wv=None, bv=None, wo=None, bo=None,
                    weights_turned=False, context=None, key_mask=None, score_mask=None, ln_scale=None, ln_shift=None):
    tiles = g.tiles
    own = context is None
    affine = ln_scale is not None
    masked = key_mask is not None or score_mask is not None
    scale = HD ** -0.5
    ph = Phase(nc, name)
    sb, sem = ph.sb, ph.sem
    psum = ph.psum()
    ps = [psum[:, 2 * s:2 * s + 2, :].rearrange("p b n -> p (b n)") for s in range(STREAMS)]
    wqT, wkT, wvT, woT = (sb(n, [P, P]) if w is not None else None
                          for n, w in (("wqT", wq), ("wkT", wk), ("wvT", wv), ("woT", wo)))
    bq_col, bk_col, bv_col = (sb(n, [P, 1]) if b is not None else None
                              for n, b in (("bq", bq), ("bk", bk), ("bv", bv)))
    bo_row = sb("bo", [1, P]) if bo is not None else None
    out_bias = sb("out_bias", [1, P]) if bo is not None else None
    bq_scaled = sb("bq_scaled", [P, 1]) if bq is not None else None
    given = [(w, t) for w, t in ((wq, wqT), (wk, wkT), (wv, wvT), (wo, woT)) if w is not None]
    raw = sb("raw", [P, len(given), P])
    small = [(t[:, :], column(b)) for b, t in ((bq, bq_col), (bk, bk_col), (bv, bv_col)) if b is not None]
    if bo is not None:
        small.append((bo_row[:, :], row_on_all(bo, P, 1)))
    if affine:
        ln_scale_rows, ln_shift_rows = sb("ln_scale", [P, P]), sb("ln_shift", [P, P])
        small += [(ln_scale_rows[:, :], row_on_all(ln_scale, P)), (ln_shift_rows[:, :], row_on_all(ln_shift, P))]
    if score_mask is not None:
        mask_rows = sb("mask_rows", [P, SEQ])
        small += [(mask_rows[SEQ * s:SEQ * s + SEQ, :], score_mask) for s in range(PAIR)]
    if weights_turned:
        transpose_weights(nc, ph, [(t[:, :], w) for w, t in given] + small, [], g.ident, psum)
    else:
        transpose_weights(nc, ph, [(raw[:, n, :], w) for n, (w, t) in enumerate(given)] + small,
                          [(t[:, :], raw[:, n, :]) for n, (w, t) in enumerate(given)], g.ident, psum)

    ln = LayernormState(ph, n=1)
    normed = sb("normed", [P, STREAMS, P])
    scaled = sb("scaled", [P, STREAMS, P]) if affine else None
    shifted_norm = sb("shifted_norm", [P, STREAMS, P]) if affine else None
    context_in = sb("context_in", [P, STREAMS, P])
    normed_T = None if own else sb("normed_T", [P, STREAMS, P])
    source_T = sb("source_T", [P, STREAMS, PAIR, 2, SEQ])
    queries_T = sb("queries_T", [P, STREAMS, P])
    keys_block = sb("keys_block", [P, STREAMS, PAIR, GROUP, SEQ])
    values_block = sb("values_block", [P, STREAMS, PAIR, HEADS // 2, 2, HD + 1])
    probs = sb("probs", [P, STREAMS, HEADS * SEQ])
    probs_T = sb("probs_T", [P, STREAMS, HEADS * SEQ])
    negmax = sb("negmax", [P, STREAMS, HEADS])
    recip = sb("recip", [P, STREAMS, HEADS])
    attended = sb("attended", [P, STREAMS, P])
    attended_T = sb("attended_T", [P, STREAMS, P])
    if key_mask is not None:
        mask_int = sb("mask_int", [P, STREAMS, SEQ], I32)
        mask_add = sb("mask_add", [P, STREAMS, SEQ])

    context_loaded = [sem(f"context_loaded_{n}") for n in range(2)]
    mask_loaded = [sem(f"mask_loaded_{n}") for n in range(2)]
    mask_ready = sem("mask_ready")
    bias_summed = sem("bias_summed")
    constants_ready = sem("constants_ready")
    normed_ready = sem("normed_ready")
    scaled_ready = sem("scaled_ready")
    shifted_ready = sem("shifted_ready")
    inputs_turned = sem("inputs_turned")
    inputs_ready = sem("inputs_ready")
    projected = sem("projected")
    queries_ready = sem("queries_ready")
    keys_ready = sem("keys_ready")
    scores_half = sem("scores_half")
    scores_ready = sem("scores_ready")
    masked_ready = sem("masked_ready")
    negmax_ready = sem("negmax_ready")
    shifted_scores = sem("shifted_scores")
    probs_ready = sem("probs_ready")
    probs_turned = sem("probs_turned")
    turned_kept = sem("turned_kept")
    attended_raw = sem("attended_raw")
    recip_ready = sem("recip_ready")
    attended_ready = sem("attended_ready")
    attended_turned = sem("attended_turned")
    attended_kept = sem("attended_kept")
    output_ready = sem("output_ready")
    tile_done = sem("tile_done")

    norm_out, norm_out_ready = (shifted_norm, shifted_ready) if affine else (normed, normed_ready)
    with nc.Block() as block:
        @block.sync
        def _(sp):
            def load(parity, first):
                pair = slice(2 * parity, 2 * parity + 2)
                sp.dma_start(context_in[:, pair, :],
                             context[bass.ds(first, 2), :, :].rearrange("t p d -> p t d")).then_inc(context_loaded[parity], 16)

            def load_mask(parity, first):
                pair = slice(2 * parity, 2 * parity + 2)
                for s in range(PAIR):
                    source = key_mask[bass.ds(first, 2), s:s + 1, :].rearrange("t a k -> a t k").to_broadcast([SEQ, 2, SEQ])
                    sp.dma_start(mask_int[SEQ * s:SEQ * s + SEQ, pair, :], source).then_inc(mask_loaded[parity], 16)

            for parity in range(2):
                if not own:
                    load(parity, 2 * parity)
                if key_mask is not None:
                    load_mask(parity, 2 * parity)
            if not own:
                with sp.Fori(0, tiles // STREAMS - 1) as i:
                    t0 = sp.snap(i * STREAMS)
                    for parity in range(2):
                        sp.wait_ge(inputs_turned, t0 + (2 * parity + 2))
                        load(parity, t0 + (2 * parity + STREAMS))
                        if key_mask is not None:
                            sp.wait_ge(mask_ready, t0 + (2 * parity + 2))
                            load_mask(parity, t0 + (2 * parity + STREAMS))

        @block.gpsimd
        def _(pool):
            def norm(tile):
                tile_rstd(nc, pool, g, tile, ln)
                if affine:
                    s = tile.stream
                    pool.wait_ge(normed_ready, tile.t + 1)
                    nc.gpsimd.tensor_tensor(scaled[:, s, :], normed[:, s, :], ln_scale_rows[:, :],
                                            ALU.mult).then_inc(scaled_ready, 1)
                    s = tile.stream
                    pool.wait_ge(scaled_ready, tile.t + 1)
                    nc.gpsimd.tensor_tensor(shifted_norm[:, s, :], scaled[:, s, :], ln_shift_rows[:, :],
                                            ALU.add).then_inc(shifted_ready, 1)

            norm(Tile(0, 0, 0))
            run_tiles(pool, tiles, lambda ahead, *others: norm(ahead) if ahead else None)

        @block.tensor
        def _(pe):
            if bo is not None and bv is not None:
                nc.tensor.matmul(ps[0][0:1, 0:P], bv_col[:, 0:1], woT[:, :], start=True, stop=True).then_inc(bias_summed, 1)
            pe.wait_ge(constants_ready, 1)

            def turn_inputs(tile):
                s = tile.stream
                pe.wait_ge(norm_out_ready, tile.t + 1)
                last = nc.tensor.transpose(ps[s][:, 0:P], norm_out[:, s, :], g.ident[:, :])
                if not own:
                    if True:
                        pe.wait_ge(context_loaded[s // 2], tile.loads + 16)
                    last = nc.tensor.transpose(ps[s][:, P:2 * P], context_in[:, s, :], g.ident[:, :])
                last.then_inc(inputs_turned, 1)

            def project(tile):
                s = tile.stream
                pe.wait_ge(inputs_ready, tile.t + 1)
                pe.wait_ge(tile_done, tile.t + 1)
                if wq is not None:
                    nc.tensor.matmul(ps[s][:, 0:P], wqT[:, :], source_T[:, s, :, 0, :] if own else normed_T[:, s, :],
                                     start=True, stop=True)
                    nc.tensor.matmul(ps[s][:, 512:512 + P], wkT[:, :], source_T[:, s, :, 0, :], start=True, stop=True)
                for q in range(PAIR):
                    last = nc.tensor.matmul(ps[s][:, P * (q + 1):P * (q + 2)],
                                            source_T[:, s, q, :, :].rearrange("p a k -> p (a k)"),
                                            wvT[:, :] if wv is not None else g.ident[:, :], start=True, stop=True)
                last.then_inc(projected, 1)

            def score(tile, turn):
                s = tile.stream
                if turn == 0:
                    pe.wait_ge(queries_ready, tile.t + 1)
                    pe.wait_ge(keys_ready, tile.t + 1)
                else:
                    pe.wait_ge(scores_half, tile.t + 1)
                for r in range(HEADS // GROUP):
                    rows, q = slice(32 * r, 32 * r + 32), (r + turn) % PAIR
                    last = nc.tensor.matmul(ps[s][SEQ * q:SEQ * q + SEQ, 256 * r:256 * r + 256],
                                            queries_T[rows, s, SEQ * q:SEQ * q + SEQ],
                                            keys_block[rows, s, q, :, :].rearrange("p a b -> p (a b)"),
                                            start=True, stop=True)
                last.then_inc(scores_ready if turn else scores_half, 1)

            def turn_probs(tile):
                s = tile.stream
                pe.wait_ge(probs_ready, tile.t + 1)
                for c in range(HEADS // 2):
                    last = nc.tensor.transpose(ps[s][:, P * c:P * c + P], probs[:, s, P * c:P * c + P], g.ident[:, :])
                last.then_inc(probs_turned, 1)

            def attend(tile):
                s = tile.stream
                pe.wait_ge(turned_kept, tile.t + 1)
                for c in range(HEADS // 2):
                    last = nc.tensor.matmul(ps[s][:, 36 * c:36 * c + 36], probs_T[:, s, P * c:P * c + P],
                                            values_block[:, s, :, c, :, :].rearrange("p q a b -> p q (a b)"),
                                            start=True, stop=True)
                last.then_inc(attended_raw, 1)

            def turn_attended(tile):
                s = tile.stream
                pe.wait_ge(attended_ready, tile.t + 1)
                nc.tensor.transpose(ps[s][:, 512:512 + P], attended[:, s, :], g.ident[:, :]).then_inc(attended_turned, 1)

            def put_out(tile):
                s = tile.stream
                pe.wait_ge(attended_kept, tile.t + 1)
                if bo is not None:
                    nc.tensor.matmul(ps[s][:, 640:768], g.ones_row[0:1, :], out_bias[0:1, :], start=True, stop=False)
                nc.tensor.matmul(ps[s][:, 640:768], attended_T[:, s, :], woT[:, :],
                                 start=bo is None, stop=True).then_inc(output_ready, 1)

            def step(ahead, a, b, c, d):
                if b:
                    score(b, 0)
                if a:
                    turn_inputs(a)
                if b:
                    score(b, 1)
                if d:
                    turn_attended(d)
                if c:
                    turn_probs(c)
                if a:
                    project(a)
                if c:
                    attend(c)
                if d:
                    put_out(d)

            run_tiles(pe, tiles, step)

        @block.scalar
        def _(act):
            act.wait_ge(constants_ready, 1)

            def keep_inputs(tile):
                s = tile.stream
                act.wait_ge(inputs_turned, tile.t + 1)
                side = ps[s][:, 0:P] if own else ps[s][:, P:2 * P]
                if wq is None:
                    nc.scalar.activation(queries_T[:, s, :], ps[s][:, 0:P], ACT.Copy, scale=scale)
                elif not own:
                    nc.scalar.copy(normed_T[:, s, :], ps[s][:, 0:P])
                nc.scalar.copy(source_T[:, s, :, :, :], bcast(side, [(SEQ, PAIR), (0, 2), (1, SEQ)])).then_inc(inputs_ready, 1)

            def keep_queries_and_values(tile):
                s = tile.stream
                act.wait_ge(projected, tile.t + 1)
                if wq is not None:
                    if bq is not None:
                        nc.scalar.activation(queries_T[:, s, :], ps[s][:, 0:P], ACT.Identity, bias=bq_scaled[:, 0:1], scale=scale)
                    else:
                        nc.scalar.activation(queries_T[:, s, :], ps[s][:, 0:P], ACT.Copy, scale=scale)
                for h in range(2):
                    rows = slice(SEQ * h, SEQ * h + SEQ)
                    last = nc.scalar.copy(values_block[rows, s, :, :, h, 0:HD].rearrange("p q c d -> p (q c) d"),
                                          ps[s][rows, P:3 * P].rearrange("p (c h d) -> p c h d", h=2, d=HD)[:, :, h, :])
                last.then_inc(queries_ready, 1)

            def exponentials(tile):
                s = tile.stream
                act.wait_ge(shifted_scores, tile.t + 1)
                nc.scalar.activation(probs[:, s, :], probs[:, s, :], ACT.Exp).then_inc(probs_ready, 1)

            def keep_turned(tile):
                s = tile.stream
                act.wait_ge(probs_turned, tile.t + 1)
                nc.scalar.copy(probs_T[:, s, :], ps[s]).then_inc(turned_kept, 1)

            def keep_attended(tile):
                s = tile.stream
                act.wait_ge(attended_turned, tile.t + 1)
                nc.scalar.copy(attended_T[:, s, :], ps[s][:, 512:512 + P]).then_inc(attended_kept, 1)

            def step(ahead, a, b, c, d):
                if a:
                    keep_inputs(a)
                if d:
                    keep_attended(d)
                if c:
                    keep_turned(c)
                if a:
                    keep_queries_and_values(a)
                if b:
                    exponentials(b)

            run_tiles(act, tiles, step)

        @block.vector
        def _(dve):
            nc.vector.memset(values_block[:, :, :, :, :, :].rearrange("p s q c h d -> p (s q c h d)"), 0.0).then_inc(bias_summed, 1)
            dve.wait_ge(bias_summed, 1 + (bo is not None and bv is not None))
            if bo is not None and bv is not None:
                nc.vector.tensor_tensor(out_bias[0:1, :], ps[0][0:1, 0:P], bo_row[0:1, :], ALU.add)
            elif bo is not None:
                nc.vector.tensor_copy(out_bias[0:1, :], bo_row[0:1, :])
            if bq is not None:
                nc.vector.tensor_scalar(bq_scaled[:, :], bq_col[:, :], scale, None, ALU.mult)
            for h in range(2):
                last = nc.vector.memset(values_block[SEQ * h:SEQ * h + SEQ, :, :, :, h, HD:HD + 1].rearrange("p s q c d -> p (s q c) d"), 1.0)
            last.then_inc(constants_ready, 1)
            nc.vector.memset(negmax[:, 0, 0:1], 0.0).then_inc(tile_done, STREAMS)

            def statistics(tile):
                nc.vector.bn_stats(ln.stats[:, 0, :], tile_of(g, tile.t)).then_inc(ln.stats_ready, 1)
                if key_mask is not None:
                    dve.wait_ge(mask_loaded[tile.stream // 2], tile.loads * 2 + 32)
                    s = tile.stream
                    nc.vector.tensor_scalar(mask_add[:, s, :], mask_int[:, s, :], 0.0, MASKED,
                                            ALU.is_equal, ALU.mult).then_inc(mask_ready, 1)

            def mean_and_variance(tile):
                dve.wait_ge(ln.stats_ready, tile.t + 1)
                nc.vector.memset(ln.var_eps[:, 0:1], 0.0)
                nc.vector.bn_aggr(ln.mean_var[:, 0, :], ln.stats[:, 0, :]).then_inc(ln.mean_ready, 1)
                dve.wait_ge(ln.mean_ready, tile.t + 1)
                nc.vector.tensor_scalar(ln.var_eps[:, :], ln.mean_var[:, 0, 1:2], LN_EPS, None, ALU.add).then_inc(ln.var_eps_ready, 1)

            def norm(tile):
                s = tile.stream
                dve.wait_ge(ln.rstd_ready, tile.t + 1)
                nc.vector.tensor_scalar(normed[:, s, :], tile_of(g, tile.t), ln.mean_var[:, 0, 0:1],
                                        ln.rstd[:, 0:1], ALU.subtract, ALU.mult).then_inc(normed_ready, 1)

            def block_keys(tile):
                s = tile.stream
                if wq is None:
                    dve.wait_ge(inputs_ready, tile.t + 1)
                dve.wait_ge(projected, tile.t + 1)
                for q in range(PAIR):
                    k = ps[s][:, 512 + SEQ * q:512 + SEQ * q + SEQ] if wq is not None else source_T[:, s, q, 0, :]
                    last = nc.vector.scalar_tensor_tensor(
                        keys_block[:, s, q, :, :], bcast(k, [(0, GROUP), (1, SEQ)]),
                        bk_col[:, 0:1] if bk is not None else 0.0,
                        bcast(g.group_mask[:, :], [(1, GROUP), (0, SEQ)]), ALU.add, ALU.mult)
                last.then_inc(keys_ready, 1)

            def shift_scores(tile):
                s = tile.stream
                dve.wait_ge(scores_ready, tile.t + 1)
                source = ps[s]
                if masked:
                    rows = mask_add[:, s, :] if key_mask is not None else mask_rows[:, :]
                    nc.vector.tensor_tensor(probs[:, s, :].rearrange("p (h k) -> p h k", k=SEQ),
                                            ps[s].rearrange("p (h k) -> p h k", k=SEQ),
                                            bcast(rows, [(0, HEADS), (1, SEQ)]), ALU.add).then_inc(masked_ready, 1)
                    dve.wait_ge(masked_ready, tile.t + 1)
                    source = probs[:, s, :]
                nc.vector.tensor_reduce(negmax[:, s, :], source.rearrange("p (h k) -> p h k", k=SEQ), X, ALU.max,
                                        negate=True).then_inc(negmax_ready, 1)
                dve.wait_ge(negmax_ready, tile.t + 1)
                nc.vector.tensor_tensor(probs[:, s, :].rearrange("p (h k) -> p h k", k=SEQ),
                                        source.rearrange("p (h k) -> p h k", k=SEQ),
                                        bcast(negmax[:, s, :], [(1, HEADS), (0, SEQ)]), ALU.add).then_inc(shifted_scores, 1)

            def divide_by_sums(tile):
                s = tile.stream
                dve.wait_ge(attended_raw, tile.t + 1)
                for q in range(PAIR):
                    part = slice(SEQ * q, SEQ * q + SEQ)
                    got = ps[s][part, 0:288].rearrange("p (c q h d) -> p c q h d", q=PAIR, h=2, d=HD + 1)
                    nc.vector.reciprocal(recip[part, s, :].rearrange("p (c h) -> p c h", h=2),
                                         got[:, :, q, :, HD]).then_inc(recip_ready, 1)
                dve.wait_ge(recip_ready, tile.t * PAIR + PAIR)
                for q in range(PAIR):
                    part = slice(SEQ * q, SEQ * q + SEQ)
                    got = ps[s][part, 0:288].rearrange("p (c q h d) -> p c q h d", q=PAIR, h=2, d=HD + 1)
                    last = nc.vector.tensor_tensor(
                        attended[part, s, :].rearrange("p (c h d) -> p c h d", h=2, d=HD), got[:, :, q, :, 0:HD],
                        bcast(recip[part, s, :], [(2, HEADS // 2), (1, 2), (0, HD)]), ALU.mult)
                last.then_inc(attended_ready, 1)

            def add_output(tile):
                s = tile.stream
                dve.wait_ge(output_ready, tile.t + 1)
                row = tile_of(g, tile.t)
                nc.vector.tensor_tensor(row, row, ps[s][:, 640:768], ALU.add).then_inc(tile_done, 1)

            def step(ahead, a, b, c, d):
                if ahead:
                    statistics(ahead)
                if b:
                    shift_scores(b)
                if a:
                    block_keys(a)
                if ahead:
                    mean_and_variance(ahead)
                if c:
                    divide_by_sums(c)
                if ahead:
                    norm(ahead)
                if d:
                    add_output(d)

            first = Tile(0, 0, 0)
            statistics(first)
            mean_and_variance(first)
            norm(first)
            run_tiles(dve, tiles, step)

    ph.end()
ROUND = 1.5 * 2 ** 23


def int8_ffn_phase(nc, g, weight_int8, weight_scale, bias):
    tiles = g.tiles
    groups = tiles // STREAMS
    ph = Phase(nc, "l0f")
    sb, sem = ph.sb, ph.sem
    psum = ph.psum()
    raw_int = sb("raw_int", [P, P], I32)
    raw = sb("raw", [P, P])
    weight_T = sb("weight_T", [P, P], BF16)
    scale_rows, bias_rows = sb("scale_rows", [P, P]), sb("bias_rows", [P, P])
    normed_all = sb("normed_all", [P, tiles, P])
    token_max = sb("token_max", [P, tiles])
    lane_max = sb("lane_max", [P, 1])
    all_max = sb("all_max", [1, 1])
    scale_one = sb("scale_one", [1, 1])
    x_scale = sb("x_scale", [P, 1])
    x_scale_inv = sb("x_scale_inv", [P, 1])
    ln = LayernormState(ph)
    transpose_weights(nc, ph, [(raw_int[:, :], weight_int8), (scale_rows[:, :], row_on_all(weight_scale, P)),
                               (bias_rows[:, :], row_on_all(bias, P))], [], g.ident, psum)

    normed_ready = sem("normed_ready")
    max_ready = sem("max_ready")
    weight_float = sem("weight_float")
    weight_turned = sem("weight_turned")
    lane_max_ready = sem("lane_max_ready")
    lane_max_turned = sem("lane_max_turned")
    scale_step = sem("scale_step")
    scale_spread = sem("scale_spread")
    with nc.Block() as block:
        @block.vector
        def _(dve):
            nc.vector.tensor_copy(raw[:, :], raw_int[:, :]).then_inc(weight_float, 1)
            dve.wait_ge(weight_turned, 1)
            nc.vector.tensor_copy(weight_T[:, :], psum[:, 0, 0:P])
            with dve.Fori(0, groups) as i:
                t0 = dve.snap(i * STREAMS)
                group_statistics(nc, dve, g, i, t0, ln)
                dve.wait_ge(ln.rstd_ready, i + 1)
                for s in range(STREAMS):
                    nc.vector.tensor_scalar(normed_all[:, bass.ds(t0 + s, 1), :].rearrange("p a d -> p (a d)"), tile_of(g, t0 + s),
                                            ln.mean_var[:, s, 0:1], ln.rstd[:, s:s + 1], ALU.subtract,
                                            ALU.mult).then_inc(normed_ready, 1)
                dve.wait_ge(normed_ready, t0 + STREAMS)
                nc.vector.tensor_reduce(token_max[:, bass.ds(t0, STREAMS)], normed_all[:, bass.ds(t0, STREAMS), :], X, ALU.max,
                                        apply_absolute_value=True).then_inc(max_ready, 1)
            dve.wait_ge(max_ready, groups)
            nc.vector.tensor_reduce(lane_max[:, :], token_max[:, :], X, ALU.max).then_inc(lane_max_ready, 1)
            dve.wait_ge(lane_max_turned, 1)
            nc.vector.tensor_reduce(all_max[0:1, :], psum[0:1, 1, 0:P], X, ALU.max).then_inc(scale_step, 1)
            dve.wait_ge(scale_step, 1)
            nc.vector.tensor_scalar(scale_one[0:1, :], all_max[0:1, :], 1.0 / 127.0, 1e-5, ALU.mult, ALU.max).then_inc(scale_step, 1)
            dve.wait_ge(scale_spread, 1)
            nc.vector.tensor_copy(x_scale[:, :], psum[:, 2, 0:1]).then_inc(scale_step, 1)
            dve.wait_ge(scale_step, 3)
            nc.vector.reciprocal(x_scale_inv[:, :], x_scale[:, :])

        @block.gpsimd
        def _(pool):
            with pool.Fori(0, groups) as i:
                group_rstd(nc, pool, g, i, ln)

        @block.tensor
        def _(pe):
            pe.wait_ge(weight_float, 1)
            nc.tensor.transpose(psum[:, 0, 0:P], raw[:, :], g.ident[:, :]).then_inc(weight_turned, 1)
            pe.wait_ge(lane_max_ready, 1)
            nc.tensor.transpose(psum[0:1, 1, 0:P], lane_max[:, 0:1], g.ident[:, :]).then_inc(lane_max_turned, 1)
            pe.wait_ge(scale_step, 2)
            nc.tensor.matmul(psum[:, 2, 0:1], g.ones_row[0:1, :], scale_one[0:1, 0:1], start=True, stop=True).then_inc(scale_spread, 1)

    width = STREAMS * P
    clipped = sb("clipped", [P, 2, width])
    shifted = sb("shifted", [P, 2, width])
    ints = sb("ints", [P, 2, width], BF16)
    ints_T = sb("ints_T", [P, 2, width], BF16)
    product = sb("product", [P, 2, width])
    biased = sb("biased", [P, 2, width])
    clipped_ready = sem("clipped_ready")
    shifted_ready = sem("shifted_ready")
    ints_ready = sem("ints_ready")
    ints_turned = sem("ints_turned")
    ints_kept = sem("ints_kept")
    dot_ready = sem("dot_ready")
    product_ready = sem("product_ready")
    biased_ready = sem("biased_ready")
    turn = [psum[:, 2 * b, 0:width // 2].bitcast(BF16) for b in range(2)]
    dot = [psum[:, 2 * b + 1, :] for b in range(2)]
    with nc.Block() as block:
        @block.vector
        def _(dve):
            with dve.Fori(0, groups // 2) as i:
                n0 = dve.snap(i * 2)
                for b in range(2):
                    t0 = (n0 + b) * STREAMS
                    source = normed_all[:, bass.ds(t0, STREAMS), :].rearrange("p t d -> p (t d)")
                    nc.vector.tensor_scalar(clipped[:, b, :], source, x_scale_inv[:, 0:1], 127.0, ALU.mult,
                                            ALU.min).then_inc(clipped_ready, 1)
                    dve.wait_ge(clipped_ready, n0 + (b + 1))
                    nc.vector.tensor_scalar(shifted[:, b, :], clipped[:, b, :], -128.0, ROUND, ALU.max,
                                            ALU.add).then_inc(shifted_ready, 1)
                    dve.wait_ge(shifted_ready, n0 + (b + 1))
                    nc.vector.tensor_scalar(ints[:, b, :], shifted[:, b, :], -ROUND, None, ALU.add).then_inc(ints_ready, 1)
                for b in range(2):
                    t0 = (n0 + b) * STREAMS
                    dve.wait_ge(dot_ready, n0 + (b + 1))
                    nc.vector.scalar_tensor_tensor(product[:, b, :].rearrange("p (t d) -> p t d", d=P),
                                                   dot[b].rearrange("p (t d) -> p t d", d=P), x_scale[:, 0:1],
                                                   bcast(scale_rows[:, :], [(0, STREAMS), (1, P)]), ALU.mult,
                                                   ALU.mult).then_inc(product_ready, 1)
                    dve.wait_ge(product_ready, n0 + (b + 1))
                    nc.vector.tensor_tensor(biased[:, b, :].rearrange("p (t d) -> p t d", d=P),
                                            product[:, b, :].rearrange("p (t d) -> p t d", d=P),
                                            bcast(bias_rows[:, :], [(0, STREAMS), (1, P)]), ALU.add).then_inc(biased_ready, 1)
                    dve.wait_ge(biased_ready, n0 + (b + 1))
                    row = g.x[:, bass.ds(t0, STREAMS), :].rearrange("p t d -> p (t d)")
                    nc.vector.tensor_tensor(row, row, biased[:, b, :], ALU.add)

        @block.tensor
        def _(pe):
            with pe.Fori(0, groups // 2) as i:
                n0 = pe.snap(i * 2)
                for b in range(2):
                    pe.wait_ge(ints_ready, n0 + (b + 1))
                    for s in range(STREAMS):
                        last = nc.tensor.transpose(turn[b][:, P * s:P * s + P], ints[:, b, P * s:P * s + P], g.ident_bf[:, :])
                    last.then_inc(ints_turned, 1)
                for b in range(2):
                    pe.wait_ge(ints_kept, n0 + (b + 1))
                    for s in range(STREAMS):
                        last = nc.tensor.matmul(dot[b][:, P * s:P * s + P], ints_T[:, b, P * s:P * s + P], weight_T[:, :],
                                                start=True, stop=True)
                    last.then_inc(dot_ready, 1)

        @block.scalar
        def _(act):
            with act.Fori(0, groups // 2) as i:
                n0 = act.snap(i * 2)
                for b in range(2):
                    act.wait_ge(ints_turned, n0 + (b + 1))
                    nc.scalar.copy(ints_T[:, b, :], turn[b]).then_inc(ints_kept, 1)

    ph.end()


def ternary_ffn_phase(nc, g, norm1_w, w1, act_scale, act_bias, norm2_w, w2):
    tiles = g.tiles
    groups = tiles // STREAMS
    hidden = w1.shape[0]
    chunks = hidden // P
    ph = Phase(nc, "l1f")
    sb, sem = ph.sb, ph.sem
    psum = ph.psum()
    raw = sb("raw", [P, 2, hidden])
    rounded_w = sb("rounded_w", [P, 2, hidden])
    ternary = sb("ternary", [P, 2, hidden], BF16)
    w1T = sb("w1T", [P, hidden], BF16)
    w2T = sb("w2T", [P, chunks, P], BF16)
    norm1_rows, norm2_rows = sb("norm1_rows", [P, P]), sb("norm2_rows", [P, hidden])
    act_scale_col, act_bias_col = sb("act_scale", [P, 1]), sb("act_bias", [P, 1])
    weight_sum = sb("weight_sum", [P, 2])
    weight_mean = sb("weight_mean", [P, 2])
    weight_mean_inv = sb("weight_mean_inv", [P, 2])
    transpose_weights(nc, ph, [(raw[:, 0, :].rearrange("p (c d) -> p c d", d=P), w1.rearrange("(c p) d -> p c d", p=P)),
                               (raw[:, 1, :], w2), (norm1_rows[:, :], row_on_all(norm1_w, P)),
                               (norm2_rows[:, :], row_on_all(norm2_w, hidden)), (act_scale_col[:, :], row_on_all(act_scale, 1)),
                               (act_bias_col[:, :], row_on_all(act_bias, 1))], [], g.ident, psum)
    weight_step = sem("weight_step")
    weight_summed = sem("weight_summed")
    ternary_turned = sem("ternary_turned")
    with nc.Block() as block:
        @block.vector
        def _(dve):
            nc.vector.tensor_reduce(weight_sum[:, :], raw[:, :, :], X, ALU.add, apply_absolute_value=True).then_inc(weight_step, 1)
            dve.wait_ge(weight_summed, 1)
            nc.vector.tensor_scalar(weight_mean[:, :], psum[:, 0, 0:2], 1.0 / (hidden * P), 1e-5, ALU.mult, ALU.max).then_inc(weight_step, 1)
            dve.wait_ge(weight_step, 2)
            nc.vector.reciprocal(weight_mean_inv[:, :], weight_mean[:, :]).then_inc(weight_step, 1)
            dve.wait_ge(weight_step, 3)
            for m in range(2):
                nc.vector.tensor_scalar(rounded_w[:, m, :], raw[:, m, :], weight_mean_inv[:, m:m + 1], ROUND, ALU.mult,
                                        ALU.add).then_inc(weight_step, 1)
            dve.wait_ge(weight_step, 5)
            nc.vector.tensor_scalar(raw[:, :, :], rounded_w[:, :, :], -ROUND, 1.0, ALU.add, ALU.min).then_inc(weight_step, 1)
            dve.wait_ge(weight_step, 6)
            nc.vector.tensor_scalar(ternary[:, :, :], raw[:, :, :], -1.0, None, ALU.max).then_inc(weight_step, 1)
            dve.wait_ge(ternary_turned, 1)
            nc.vector.tensor_copy(w1T[:, :], psum[:, 1, 0:hidden // 2].bitcast(BF16))
            nc.vector.tensor_copy(w2T[:, :, :].rearrange("p c d -> p (c d)"), psum[:, 2, 0:hidden // 2].bitcast(BF16))

        @block.tensor
        def _(pe):
            pe.wait_ge(weight_step, 1)
            nc.tensor.matmul(psum[:, 0, 0:2], g.ones_full[:, :], weight_sum[:, :], start=True, stop=True).then_inc(weight_summed, 1)
            pe.wait_ge(weight_step, 7)
            for m in range(2):
                for c in range(chunks):
                    last = nc.tensor.transpose(psum[:, 1 + m, 0:hidden // 2].bitcast(BF16)[:, P * c:P * c + P],
                                               ternary[:, m, P * c:P * c + P], g.ident_bf[:, :])
            last.then_inc(ternary_turned, 1)

    B = 2
    width = STREAMS * P
    ln = [LayernormState(ph, f"_{b}") for b in range(B)]
    normed = sb("normed", [P, B, STREAMS, P])
    squares = sb("squares", [P, B, STREAMS, P])
    square_sum = sb("square_sum", [P, B, STREAMS])
    mean_square = sb("mean_square", [P, B, STREAMS])
    rms_inv = sb("rms_inv", [P, B, STREAMS])
    rms_normed = sb("rms_normed", [P, B, STREAMS, P])
    top = sb("top", [P, B, STREAMS])
    top_kept = sb("top_kept", [P, B, STREAMS])
    top_inv = sb("top_inv", [P, B, STREAMS])
    to_int = sb("to_int", [P, B, STREAMS])
    from_int = sb("from_int", [P, B, STREAMS])
    rounded = sb("rounded", [P, B, STREAMS, P])
    lowered = sb("lowered", [P, B, STREAMS, P])
    ints = sb("ints", [P, B, width], BF16)
    ints_T = sb("ints_T", [P, B, width], BF16)
    act = sb("act", [P, B, STREAMS, hidden])
    work = sb("work", [P, B, STREAMS, hidden])
    square_sum2 = sb("square_sum2", [P, B, STREAMS])
    mean_square2 = sb("mean_square2", [P, B, STREAMS])
    rms_inv2 = sb("rms_inv2", [P, B, STREAMS])
    top2 = sb("top2", [P, B, STREAMS])
    top_kept2 = sb("top_kept2", [P, B, STREAMS])
    top_inv2 = sb("top_inv2", [P, B, STREAMS])
    to_int2 = sb("to_int2", [P, B, STREAMS])
    from_int2 = sb("from_int2", [P, B, STREAMS])
    hidden_ints = sb("hidden_ints", [P, B, STREAMS, hidden], BF16)
    hidden_T = sb("hidden_T", [P, B, STREAMS, hidden], BF16)
    normed_ready = sem("normed_ready")
    squares_ready = sem("squares_ready")
    mean_square_ready = sem("mean_square_ready")
    rms_ready = sem("rms_ready")
    rms_normed_ready = sem("rms_normed_ready")
    top_ready = sem("top_ready")
    top_kept_ready = sem("top_kept_ready")
    top_inv_ready = sem("top_inv_ready")
    to_int_ready = sem("to_int_ready")
    rounded_ready = sem("rounded_ready")
    lowered_ready = sem("lowered_ready")
    ints_ready = sem("ints_ready")
    ints_turned = sem("ints_turned")
    ints_kept = sem("ints_kept")
    hidden_ready = sem("hidden_ready")
    relu_ready = sem("relu_ready")
    squared_ready = sem("squared_ready")
    activated = sem("activated")
    hidden_squares_ready = sem("hidden_squares_ready")
    mean_square2_ready = sem("mean_square2_ready")
    rms2_ready = sem("rms2_ready")
    hidden_normed = sem("hidden_normed")
    top2_ready = sem("top2_ready")
    top_kept2_ready = sem("top_kept2_ready")
    top_inv2_ready = sem("top_inv2_ready")
    to_int2_ready = sem("to_int2_ready")
    hidden_rounded = sem("hidden_rounded")
    hidden_lowered = sem("hidden_lowered")
    hidden_ints_ready = sem("hidden_ints_ready")
    hidden_turned = sem("hidden_turned")
    hidden_kept = sem("hidden_kept")
    output_ready = sem("output_ready")
    streams, parities = range(STREAMS), range(B)

    def scales(dve, n, b, top, kept, inv, to_int, from_int, which, weight, ready):
        top_ready, kept_ready, inv_ready, scale_ready = ready
        dve.wait_ge(top_ready, which)
        nc.vector.tensor_scalar(kept[:, b, :], top[:, b, :], 1e-5, None, ALU.max).then_inc(kept_ready, 1)
        dve.wait_ge(kept_ready, n + (b + 1))
        nc.vector.reciprocal(inv[:, b, :], kept[:, b, :]).then_inc(inv_ready, 1)
        nc.vector.tensor_scalar(from_int[:, b, :], kept[:, b, :], 1.0 / 127.0, weight, ALU.mult, ALU.mult)
        dve.wait_ge(inv_ready, n + (b + 1))
        nc.vector.tensor_scalar(to_int[:, b, :], inv[:, b, :], 127.0, None, ALU.mult).then_inc(scale_ready, 1)

    with nc.Block() as block:
        @block.vector
        def _(dve):
            with dve.Fori(0, groups // B) as i:
                n0 = dve.snap(i * B)
                c0 = dve.snap(i * STREAMS)
                k0 = dve.snap(i * (B * STREAMS))
                for b in parities:
                    group_statistics(nc, dve, g, i, c0, ln[b], k0 + b * STREAMS)
                for b in parities:
                    dve.wait_ge(ln[b].rstd_ready, i + 1)
                    for s in streams:
                        last = nc.vector.tensor_scalar(normed[:, b, s, :], tile_of(g, k0 + (b * STREAMS + s)), ln[b].mean_var[:, s, 0:1],
                                                       ln[b].rstd[:, s:s + 1], ALU.subtract, ALU.mult)
                    last.then_inc(normed_ready, 1)
                for b in parities:
                    dve.wait_ge(squares_ready, n0 + (b + 1))
                    nc.vector.tensor_scalar(mean_square[:, b, :], square_sum[:, b, :], 1.0 / P, 1e-8, ALU.mult,
                                            ALU.add).then_inc(mean_square_ready, 1)
                for b in parities:
                    dve.wait_ge(rms_ready, n0 + (b + 1))
                    for s in streams:
                        last = nc.vector.scalar_tensor_tensor(rms_normed[:, b, s, :], normed[:, b, s, :], rms_inv[:, b, s:s + 1],
                                                              norm1_rows[:, :], ALU.mult, ALU.mult)
                    last.then_inc(rms_normed_ready, 1)
                    dve.wait_ge(rms_normed_ready, n0 + (b + 1))
                    nc.vector.tensor_reduce(top[:, b, :], rms_normed[:, b, :, :], X, ALU.max, apply_absolute_value=True).then_inc(top_ready, 1)
                    scales(dve, n0, b, top, top_kept, top_inv, to_int, from_int, n0 + (b + 1), weight_mean[:, 0:1],
                           (top_ready, top_kept_ready, top_inv_ready, to_int_ready))
                    dve.wait_ge(to_int_ready, n0 + (b + 1))
                    for s in streams:
                        last = nc.vector.tensor_scalar(rounded[:, b, s, :], rms_normed[:, b, s, :], to_int[:, b, s:s + 1], ROUND,
                                                       ALU.mult, ALU.add)
                    last.then_inc(rounded_ready, 1)
                    dve.wait_ge(rounded_ready, n0 + (b + 1))
                    nc.vector.tensor_scalar(lowered[:, b, :, :], rounded[:, b, :, :], -ROUND, 127.0, ALU.add, ALU.min).then_inc(lowered_ready, 1)
                    dve.wait_ge(lowered_ready, n0 + (b + 1))
                    nc.vector.tensor_scalar(ints[:, b, :], lowered[:, b, :, :].rearrange("p s d -> p (s d)"), -128.0, None,
                                            ALU.max).then_inc(ints_ready, 1)
                for b in parities:
                    for s in streams:
                        dve.wait_ge(hidden_ready, k0 + (b * STREAMS + s + 1))
                        nc.vector.tensor_scalar(act[:, b, s, :], psum[:, STREAMS * b + s, :], from_int[:, b, s:s + 1], 0.0, ALU.mult,
                                                ALU.max).then_inc(relu_ready, 1)
                for b in parities:
                    dve.wait_ge(hidden_squares_ready, n0 + (b + 1))
                    nc.vector.tensor_scalar(mean_square2[:, b, :], square_sum2[:, b, :], 1.0 / hidden, 1e-8, ALU.mult,
                                            ALU.add).then_inc(mean_square2_ready, 1)
                for b in parities:
                    dve.wait_ge(rms2_ready, n0 + (b + 1))
                    for s in streams:
                        last = nc.vector.scalar_tensor_tensor(work[:, b, s, :], act[:, b, s, :], rms_inv2[:, b, s:s + 1],
                                                              norm2_rows[:, :], ALU.mult, ALU.mult)
                    last.then_inc(hidden_normed, 1)
                    dve.wait_ge(hidden_normed, n0 + (b + 1))
                    nc.vector.tensor_reduce(top2[:, b, :], work[:, b, :, :], X, ALU.max, apply_absolute_value=True).then_inc(top2_ready, 1)
                    scales(dve, n0, b, top2, top_kept2, top_inv2, to_int2, from_int2, n0 + (b + 1), weight_mean[:, 1:2],
                           (top2_ready, top_kept2_ready, top_inv2_ready, to_int2_ready))
                    dve.wait_ge(to_int2_ready, n0 + (b + 1))
                    for s in streams:
                        last = nc.vector.tensor_scalar(act[:, b, s, :], work[:, b, s, :], to_int2[:, b, s:s + 1], ROUND,
                                                       ALU.mult, ALU.add)
                    last.then_inc(hidden_rounded, 1)
                    dve.wait_ge(hidden_rounded, n0 + (b + 1))
                    nc.vector.tensor_scalar(work[:, b, :, :], act[:, b, :, :], -ROUND, 127.0, ALU.add, ALU.min).then_inc(hidden_lowered, 1)
                    dve.wait_ge(hidden_lowered, n0 + (b + 1))
                    nc.vector.tensor_scalar(hidden_ints[:, b, :, :], work[:, b, :, :], -128.0, None, ALU.max).then_inc(hidden_ints_ready, 1)
                for b in parities:
                    for s in streams:
                        dve.wait_ge(output_ready, k0 + (b * STREAMS + s + 1))
                        row = tile_of(g, k0 + (b * STREAMS + s))
                        nc.vector.scalar_tensor_tensor(row, psum[:, STREAMS * b + s, 256:256 + P], from_int2[:, b, s:s + 1], row,
                                                       ALU.mult, ALU.add)

        @block.gpsimd
        def _(pool):
            with pool.Fori(0, groups // B) as i:
                n0 = pool.snap(i * B)
                k0 = pool.snap(i * (B * STREAMS))
                for b in parities:
                    group_rstd(nc, pool, g, i, ln[b])
                for b in parities:
                    pool.wait_ge(mean_square_ready, n0 + (b + 1))
                    nc.gpsimd.tensor_tensor(rms_inv[:, b, :], mean_square[:, b, :], g.minus_half[:, 0:STREAMS], ALU.pow).then_inc(rms_ready, 1)
                for b in parities:
                    pool.wait_ge(mean_square2_ready, n0 + (b + 1))
                    nc.gpsimd.tensor_tensor(rms_inv2[:, b, :], mean_square2[:, b, :], g.minus_half[:, 0:STREAMS], ALU.pow).then_inc(rms2_ready, 1)

        @block.tensor
        def _(pe):
            with pe.Fori(0, groups // B) as i:
                n0 = pe.snap(i * B)
                k0 = pe.snap(i * (B * STREAMS))
                for b in parities:
                    turned = psum[:, STREAMS * b, 0:width // 2].bitcast(BF16)
                    pe.wait_ge(ints_ready, n0 + (b + 1))
                    for s in streams:
                        last = nc.tensor.transpose(turned[:, P * s:P * s + P], ints[:, b, P * s:P * s + P], g.ident_bf[:, :])
                    last.then_inc(ints_turned, 1)
                for b in parities:
                    pe.wait_ge(ints_kept, n0 + (b + 1))
                    for s in streams:
                        nc.tensor.matmul(psum[:, STREAMS * b + s, :], ints_T[:, b, P * s:P * s + P], w1T[:, :],
                                         start=True, stop=True).then_inc(hidden_ready, 1)
                for b in parities:
                    pe.wait_ge(hidden_ints_ready, n0 + (b + 1))
                    for s in streams:
                        turned = psum[:, STREAMS * b + s, 0:hidden // 2].bitcast(BF16)
                        for c in range(chunks):
                            last = nc.tensor.transpose(turned[:, P * c:P * c + P], hidden_ints[:, b, s, P * c:P * c + P], g.ident_bf[:, :])
                        last.then_inc(hidden_turned, 1)
                for b in parities:
                    for s in streams:
                        pe.wait_ge(hidden_kept, k0 + (b * STREAMS + s + 1))
                        for c in range(chunks):
                            last = nc.tensor.matmul(psum[:, STREAMS * b + s, 256:256 + P], hidden_T[:, b, s, P * c:P * c + P], w2T[:, c, :],
                                                    start=c == 0, stop=c == chunks - 1)
                        last.then_inc(output_ready, 1)

        @block.scalar
        def _(acte):
            with acte.Fori(0, groups // B) as i:
                n0 = acte.snap(i * B)
                k0 = acte.snap(i * (B * STREAMS))
                for b in parities:
                    acte.wait_ge(normed_ready, n0 + (b + 1))
                    for s in streams:
                        last = nc.scalar.activation(squares[:, b, s, :], normed[:, b, s, :], ACT.Square, accum_out=square_sum[:, b, s:s + 1])
                    last.then_inc(squares_ready, 1)
                for b in parities:
                    acte.wait_ge(ints_turned, n0 + (b + 1))
                    nc.scalar.copy(ints_T[:, b, :], psum[:, STREAMS * b, 0:width // 2].bitcast(BF16)).then_inc(ints_kept, 1)
                for b in parities:
                    for s in streams:
                        acte.wait_ge(relu_ready, k0 + (b * STREAMS + s + 1))
                        nc.scalar.activation(work[:, b, s, :], act[:, b, s, :], ACT.Square).then_inc(squared_ready, 1)
                for b in parities:
                    acte.wait_ge(squared_ready, k0 + (b * STREAMS + STREAMS))
                    for s in streams:
                        nc.scalar.activation(act[:, b, s, :], work[:, b, s, :], ACT.Identity, bias=act_bias_col[:, 0:1],
                                             scale=act_scale_col[:, 0:1]).then_inc(activated, 1)
                for b in parities:
                    acte.wait_ge(activated, k0 + (b * STREAMS + STREAMS))
                    for s in streams:
                        last = nc.scalar.activation(work[:, b, s, :], act[:, b, s, :], ACT.Square, accum_out=square_sum2[:, b, s:s + 1])
                    last.then_inc(hidden_squares_ready, 1)
                for b in parities:
                    for s in streams:
                        acte.wait_ge(hidden_turned, k0 + (b * STREAMS + s + 1))
                        nc.scalar.copy(hidden_T[:, b, s, :], psum[:, STREAMS * b + s, 0:hidden // 2].bitcast(BF16)).then_inc(hidden_kept, 1)

    ph.end()


def takes_the_wait(nc, g, column):
    nc.tensor.matmul(column, g.ones_row[0:1, :], g.ones_row[0:1, 0:1], start=True, stop=True)


def box_attention_phase(nc, g, boxes, context, wq, bq, wk, bk, wv, bv, wo, bo, wg, bg, constants):
    tiles = g.tiles
    wide = wq.shape[0]
    heads_dim = wide // HEADS
    pairs = HEADS // 2
    scale = heads_dim ** -0.5
    kinds, trigs = 4, 2
    features = kinds * trigs
    keys_at_once = P // features
    blocks = SEQ // keys_at_once
    turns = 100.0 / (2 * 3.141592653589793)
    T = 2
    ph = Phase(nc, "l2x")
    sb, sem = ph.sb, ph.sem
    psum = ph.psum()
    ps = [psum[:, 4 * b:4 * b + 4, :].rearrange("p b n -> p (b n)") for b in range(T)]
    wqT, wkT, wvT = sb("wqT", [P, wide]), sb("wkT", [P, wide]), sb("wvT", [P, wide])
    woT = sb("woT", [P, pairs, P])
    raw = sb("raw", [P, 4, wide])
    bq_cols, bk_cols, bv_cols = sb("bq", [P, pairs]), sb("bk", [P, pairs]), sb("bv", [P, pairs])
    bo_row, out_bias = sb("bo", [1, P]), sb("out_bias", [1, P])
    boxes_all = sb("boxes_all", [P, tiles, 4])
    box_features = sb("box_features", [P, tiles, 4, kinds])
    gate_cols = sb("gate_cols", [P, HEADS])
    gate_weights = sb("gate_weights", [P, HEADS, keys_at_once])
    bg_row, gate_bias = sb("bg", [1, HEADS]), sb("gate_bias", [1, HEADS, keys_at_once])
    same_key, block_of, diagonal, floor_phase = (sb("same_key", [P, P]), sb("block_of", [P, PAIR * blocks]),
                                                 sb("diagonal", [P, keys_at_once]), sb("floor_phase", [P, 2]))
    loads = [(raw[:, m, :].rearrange("p (c d) -> p c d", d=P), w.rearrange("(c p) d -> p c d", p=P)) for m, w in enumerate((wq, wk, wv))]
    loads += [(raw[:, 3, :], wo)]
    loads += [(t[:, :], bass.AP(b.tensor, b.offset, [[1, P], [P, pairs]])) for t, b in ((bq_cols, bq), (bk_cols, bk), (bv_cols, bv))]
    loads += [(bo_row[:, :], row_on_all(bo, P, 1)), (bg_row[:, :], row_on_all(bg, HEADS, 1))]
    loads += [(boxes_all[:, :, :], boxes)]
    loads += [(gate_cols[features * k:features * (k + 1), :], wg.rearrange("h d -> d h")) for k in range(keys_at_once)]
    loads += [(same_key[:, :], constants["same_key"]), (block_of[:, :], constants["block_of"]),
              (diagonal[:, :], constants["diagonal"]), (floor_phase[:, :], constants["floor_phase"])]
    turned = [(dst[:, P * c:P * c + P], raw[:, m, P * c:P * c + P]) for m, dst in enumerate((wqT, wkT, wvT)) for c in range(pairs)]
    turned += [(woT[:, c, :], raw[:, 3, P * c:P * c + P]) for c in range(pairs)]
    transpose_weights(nc, ph, loads, turned, g.ident, psum)

    prepare = sem("prepare")
    bias_summed = sem("bias_summed")
    with nc.Block() as block:
        @block.vector
        def _(dve):
            size, center = box_features[:, :, 0, 2:4], box_features[:, :, 0, 0:2]
            nc.vector.memset(box_features[:, :, 1:4, :].rearrange("p t m k -> p t (m k)"), 1.0).then_inc(prepare, 1)
            nc.vector.tensor_tensor(center, boxes_all[:, :, 0:2], boxes_all[:, :, 2:4], ALU.add)
            nc.vector.tensor_tensor(size, boxes_all[:, :, 2:4], boxes_all[:, :, 0:2], ALU.subtract).then_inc(prepare, 1)
            dve.wait_ge(prepare, 2)
            nc.vector.tensor_scalar(size, size, 1.0, None, ALU.add)
            nc.vector.tensor_scalar(center, center, 0.5, None, ALU.mult).then_inc(prepare, 1)
            dve.wait_ge(prepare, 3)
            nc.vector.reciprocal(box_features[:, :, 1, 0:2], size)
            nc.vector.memset(box_features[:, :, 2, 2:4], 0.0)
            nc.vector.tensor_copy(box_features[:, :, 2, 0:2], center).then_inc(prepare, 1)
            dve.wait_ge(prepare, 4)
            nc.vector.tensor_copy(box_features[:, :, 3, 2:4], box_features[:, :, 1, 0:2])
            nc.vector.tensor_tensor(gate_weights[:, :, :], bcast(gate_cols[:, :], [(1, HEADS), (0, keys_at_once)]),
                                    bcast(diagonal[:, :], [(0, HEADS), (1, keys_at_once)]), ALU.mult)
            nc.vector.tensor_copy(gate_bias[:, :, :], bcast(bg_row[:, :], [(1, HEADS), (0, keys_at_once)]))
            dve.wait_ge(bias_summed, 1)
            nc.vector.tensor_tensor(out_bias[:, :], psum[0:1, 0, 0:P], bo_row[:, :], ALU.add)

        @block.tensor
        def _(pe):
            for c in range(pairs):
                last = nc.tensor.matmul(psum[0:1, 0, 0:P], bv_cols[:, c:c + 1], woT[:, c, :], start=c == 0, stop=c == pairs - 1)
            last.then_inc(bias_summed, 1)

    ln = LayernormState(ph, n=T)
    normed = sb("normed", [P, T, P])
    context_in = sb("context_in", [P, T, P])
    inputs_T = sb("inputs_T", [P, T, 2, P])
    query_boxes = sb("query_boxes", [P, T, 2, P])
    key_boxes = sb("key_boxes", [P, T, 2, P])
    spread = sb("spread", [P, T, 2 * P + 2 * PAIR * blocks])
    relation = sb("relation", [P, T, 2, blocks * P])
    embedding = sb("embedding", [P, T, blocks * P])
    queries_T = sb("queries_T", [P, T, pairs, P])
    keys_T = sb("keys_T", [P, T, pairs, P])
    values = sb("values", [P, T, PAIR, pairs, heads_dim])
    probs = sb("probs", [P, T, HEADS * SEQ])
    gated = sb("gated", [P, T, HEADS * SEQ])
    probs_T = sb("probs_T", [P, T, pairs, P])
    attended_T = sb("attended_T", [P, T, pairs, P])
    negmax = sb("negmax", [P, T, HEADS])
    total = sb("total", [P, T, HEADS])
    recip = sb("recip", [P, T, HEADS])
    context_loaded = sem("context_loaded")
    normed_ready = sem("normed_ready")
    boxes_spread = sem("boxes_spread")
    inputs_turned = sem("inputs_turned")
    inputs_ready = sem("inputs_ready")
    spread_ready = sem("spread_ready")
    difference_ready = sem("difference_ready")
    scaled_once = sem("scaled_once")
    relation_ready = sem("relation_ready")
    magnitude_ready = sem("magnitude_ready")
    floored_ready = sem("floored_ready")
    logs_ready = sem("logs_ready")
    turns_ready = sem("turns_ready")
    rounded_ready = sem("rounded_ready")
    fraction_ready = sem("fraction_ready")
    embedding_ready = sem("embedding_ready")
    queries_projected = sem("queries_projected")
    keys_projected = sem("keys_projected")
    queries_ready = sem("queries_ready")
    keys_ready = sem("keys_ready")
    values_projected = sem("values_projected")
    values_ready = sem("values_ready")
    gates_ready = sem("gates_ready")
    scores_half = sem("scores_half")
    scores_ready = sem("scores_ready")
    negmax_ready = sem("negmax_ready")
    shifted_scores = sem("shifted_scores")
    exp_ready = sem("exp_ready")
    gated_ready = sem("gated_ready")
    total_ready = sem("total_ready")
    recip_ready = sem("recip_ready")
    probs_ready = sem("probs_ready")
    probs_turned = sem("probs_turned")
    probs_kept = sem("probs_kept")
    attended_ready = sem("attended_ready")
    attended_kept = sem("attended_kept")
    output_ready = sem("output_ready")
    both = range(T)
    with nc.Block() as block:
        @block.sync
        def _(sp):
            def load(group):
                sp.dma_start(context_in[:, :, :], context[bass.ds(group, 1), :, :, :].rearrange("o t p d -> p (o t) d")).then_inc(context_loaded, 16)

            load(0)
            with sp.Fori(0, tiles // T - 1) as i:
                sp.wait_ge(inputs_turned, i * T + T)
                load(i + 1)

        @block.gpsimd
        def _(pool):
            with pool.Fori(0, tiles // T) as i:
                t0 = pool.snap(i * T)
                for b in both:
                    f = box_features[:, bass.ds(t0 + b, 1), :, :].rearrange("p a m k -> p (a m k)")
                    nc.gpsimd.tensor_copy(query_boxes[:, b, :, :].rearrange("p m (r k) -> p m r k", k=kinds),
                                          bcast(f[:, 0:2 * kinds], [(kinds, 2), (0, P // kinds), (1, kinds)]))
                    nc.gpsimd.tensor_tensor(key_boxes[:, b, :, :].rearrange("p m (r k) -> p m r k", k=kinds),
                                            bcast(f[:, 2 * kinds:4 * kinds], [(kinds, 2), (0, P // kinds), (1, kinds)]),
                                            bcast(same_key[:, :], [(0, 2), (kinds, P // kinds), (1, kinds)]), ALU.mult).then_inc(boxes_spread, 1)
                group_rstd(nc, pool, g, i, ln)

                def grid(ap, dims):
                    return bcast(ap, dims)

                for b in both:
                    pool.wait_ge(spread_ready, t0 + (b + 1))
                    nc.gpsimd.tensor_tensor(relation[:, b, 0, :].rearrange("p (c s n) -> p c s n", s=PAIR, n=SEQ),
                                            grid(spread[:, b, 0:P], [(0, blocks), (SEQ, PAIR), (1, SEQ)]),
                                            grid(spread[:, b, 2 * P:2 * P + 8], [(1, blocks), (blocks, PAIR), (0, SEQ)]),
                                            ALU.subtract).then_inc(difference_ready, 1)
                for b in both:
                    pool.wait_ge(difference_ready, t0 + (b + 1))
                    nc.gpsimd.tensor_tensor(relation[:, b, 1, :].rearrange("p (c n) -> p c n", n=P),
                                            relation[:, b, 0, :].rearrange("p (c n) -> p c n", n=P),
                                            grid(spread[:, b, P:2 * P], [(0, blocks), (1, P)]), ALU.mult).then_inc(scaled_once, 1)
                for b in both:
                    pool.wait_ge(scaled_once, t0 + (b + 1))
                    nc.gpsimd.tensor_tensor(relation[:, b, 0, :].rearrange("p (c s n) -> p c s n", s=PAIR, n=SEQ),
                                            relation[:, b, 1, :].rearrange("p (c s n) -> p c s n", s=PAIR, n=SEQ),
                                            grid(spread[:, b, 2 * P + 8:2 * P + 16], [(1, blocks), (blocks, PAIR), (0, SEQ)]),
                                            ALU.mult).then_inc(relation_ready, 1)
                for b in both:
                    pool.wait_ge(rounded_ready, t0 + (b + 1))
                    nc.gpsimd.tensor_tensor(embedding[:, b, :], relation[:, b, 0, :], relation[:, b, 1, :],
                                            ALU.subtract).then_inc(fraction_ready, 1)
                for b in both:
                    pool.wait_ge(recip_ready, t0 + (b + 1))
                    nc.gpsimd.tensor_tensor(probs[:, b, :].rearrange("p (h k) -> p h k", k=SEQ),
                                            gated[:, b, :].rearrange("p (h k) -> p h k", k=SEQ),
                                            bcast(recip[:, b, :], [(1, HEADS), (0, SEQ)]), ALU.mult).then_inc(probs_ready, 1)

        @block.vector
        def _(dve):
            with dve.Fori(0, tiles // T) as i:
                t0 = dve.snap(i * T)
                group_statistics(nc, dve, g, i, t0, ln)
                for b in both:
                    dve.wait_ge(ln.rstd_ready, i + 1)
                    nc.vector.tensor_scalar(normed[:, b, :], tile_of(g, t0 + b), ln.mean_var[:, b, 0:1], ln.rstd[:, b:b + 1],
                                            ALU.subtract, ALU.mult).then_inc(normed_ready, 1)
                for b in both:
                    dve.wait_ge(queries_projected, t0 + (b + 1))
                    nc.vector.tensor_tensor(queries_T[:, b, :, :], ps[b][:, 0:1024].rearrange("p (c n) -> p c n", n=P),
                                            bcast(bq_cols[:, :], [(1, pairs), (0, P)]), ALU.add).then_inc(queries_ready, 1)
                    dve.wait_ge(keys_projected, t0 + (b + 1))
                    nc.vector.tensor_tensor(keys_T[:, b, :, :], ps[b][:, 1024:2048].rearrange("p (c n) -> p c n", n=P),
                                            bcast(bk_cols[:, :], [(1, pairs), (0, P)]), ALU.add).then_inc(keys_ready, 1)
                for b in both:
                    dve.wait_ge(magnitude_ready, t0 + (b + 1))
                    nc.vector.tensor_scalar(relation[:, b, 1, :], relation[:, b, 0, :], floor_phase[:, 0:1], None,
                                            ALU.max).then_inc(floored_ready, 1)
                for b in both:
                    dve.wait_ge(logs_ready, t0 + (b + 1))
                    nc.vector.tensor_scalar(relation[:, b, 0, :], relation[:, b, 1, :], turns, floor_phase[:, 1:2], ALU.mult,
                                            ALU.add).then_inc(turns_ready, 1)
                    dve.wait_ge(turns_ready, t0 + (b + 1))
                    nc.vector.tensor_scalar(relation[:, b, 1, :], relation[:, b, 0, :], ROUND, -ROUND, ALU.add,
                                            ALU.add).then_inc(rounded_ready, 1)
                for b in both:
                    dve.wait_ge(scores_ready, t0 + (b + 1))
                    scores = ps[b][:, 0:1024].rearrange("p (h k) -> p h k", k=SEQ)
                    nc.vector.tensor_reduce(negmax[:, b, :], scores, X, ALU.max, negate=True).then_inc(negmax_ready, 1)
                    dve.wait_ge(negmax_ready, t0 + (b + 1))
                    nc.vector.tensor_tensor(probs[:, b, :].rearrange("p (h k) -> p h k", k=SEQ), scores,
                                            bcast(negmax[:, b, :], [(1, HEADS), (0, SEQ)]), ALU.add).then_inc(shifted_scores, 1)
                for b in both:
                    dve.wait_ge(exp_ready, t0 + (b + 1))
                    dve.wait_ge(gates_ready, t0 + (b + 1))
                    nc.vector.scalar_tensor_tensor(gated[:, b, :], ps[b][:, 1024:2048], 1e-6, probs[:, b, :], ALU.max,
                                                   ALU.mult).then_inc(gated_ready, 1)
                    dve.wait_ge(gated_ready, t0 + (b + 1))
                    nc.vector.tensor_reduce(total[:, b, :], gated[:, b, :].rearrange("p (h k) -> p h k", k=SEQ), X,
                                            ALU.add).then_inc(total_ready, 1)
                    dve.wait_ge(total_ready, t0 + (b + 1))
                    nc.vector.reciprocal(recip[:, b, :], total[:, b, :]).then_inc(recip_ready, 1)
                for b in both:
                    dve.wait_ge(output_ready, t0 + (b + 1))
                    row = tile_of(g, t0 + b)
                    nc.vector.tensor_tensor(row, row, ps[b][:, 1024:1024 + P], ALU.add)

        @block.scalar
        def _(act):
            with act.Fori(0, tiles // T) as i:
                t0 = act.snap(i * T)
                for b in both:
                    act.wait_ge(inputs_turned, t0 + (b + 1))
                    nc.scalar.copy(inputs_T[:, b, :, :].rearrange("p a n -> p (a n)"), ps[b][:, 0:2 * P]).then_inc(inputs_ready, 1)
                    nc.scalar.copy(spread[:, b, :], ps[b][:, 512:512 + 2 * P + 16]).then_inc(spread_ready, 1)
                for b in both:
                    act.wait_ge(values_projected, t0 + (b + 1))
                    for s in range(PAIR):
                        for h in range(2):
                            last = nc.scalar.copy(values[SEQ * h:SEQ * h + SEQ, b, s, :, :],
                                                  ps[b][SEQ * s:SEQ * s + SEQ, 0:1024].rearrange("p (c h d) -> p c h d", h=2, d=heads_dim)[:, :, h, :])
                    last.then_inc(values_ready, 1)
                for b in both:
                    act.wait_ge(relation_ready, t0 + (b + 1))
                    nc.scalar.activation(relation[:, b, 0, :], relation[:, b, 0, :], ACT.Abs).then_inc(magnitude_ready, 1)
                for b in both:
                    act.wait_ge(floored_ready, t0 + (b + 1))
                    nc.scalar.activation(relation[:, b, 1, :], relation[:, b, 1, :], ACT.Ln).then_inc(logs_ready, 1)
                for b in both:
                    act.wait_ge(fraction_ready, t0 + (b + 1))
                    nc.scalar.activation(embedding[:, b, :], embedding[:, b, :], ACT.Sin, scale=6.283185).then_inc(embedding_ready, 1)
                for b in both:
                    act.wait_ge(shifted_scores, t0 + (b + 1))
                    nc.scalar.activation(probs[:, b, :], probs[:, b, :], ACT.Exp, scale=scale).then_inc(exp_ready, 1)
                for b in both:
                    act.wait_ge(probs_turned, t0 + (b + 1))
                    nc.scalar.copy(probs_T[:, b, :, :].rearrange("p c n -> p (c n)"), ps[b][:, 1024:2048]).then_inc(probs_kept, 1)
                for b in both:
                    act.wait_ge(attended_ready, t0 + (b + 1))
                    nc.scalar.copy(attended_T[:, b, :, :].rearrange("p c n -> p (c n)"), ps[b][:, 0:1024]).then_inc(attended_kept, 1)

        @block.tensor
        def _(pe):
            with pe.Fori(0, tiles // T) as i:
                t0 = pe.snap(i * T)
                for b in both:
                    pe.wait_ge(normed_ready, t0 + (b + 1))
                    nc.tensor.transpose(ps[b][:, 0:P], normed[:, b, :], g.ident[:, :])
                    if b == 0:
                        pe.wait_ge(context_loaded, i * 16 + 16)
                    nc.tensor.transpose(ps[b][:, P:2 * P], context_in[:, b, :], g.ident[:, :])
                    pe.wait_ge(boxes_spread, t0 + (b + 1))
                    for m in range(2):
                        nc.tensor.transpose(ps[b][:, 512 + P * m:512 + P * m + P], query_boxes[:, b, m, :], g.ident[:, :])
                    for m in range(2):
                        last = nc.tensor.matmul(ps[b][:, 768 + 8 * m:768 + 8 * m + 8], key_boxes[:, b, m, :], block_of[:, :],
                                                start=True, stop=True)
                    last.then_inc(inputs_turned, 1)
                for b in both:
                    pe.wait_ge(inputs_ready, t0 + (b + 1))
                    pe.wait_ge(spread_ready, t0 + (b + 1))
                    for c in range(pairs):
                        last = nc.tensor.matmul(ps[b][:, P * c:P * c + P], wqT[:, P * c:P * c + P], inputs_T[:, b, 0, :], start=True, stop=True)
                    last.then_inc(queries_projected, 1)
                    for c in range(pairs):
                        last = nc.tensor.matmul(ps[b][:, 1024 + P * c:1024 + P * c + P], wkT[:, P * c:P * c + P], inputs_T[:, b, 1, :],
                                                start=True, stop=True)
                    last.then_inc(keys_projected, 1)
                for b in both:
                    pe.wait_ge(queries_ready, t0 + (b + 1))
                    for c in range(2):
                        last = nc.tensor.matmul(ps[b][:, 512 * c:512 * c + 512], inputs_T[:, b, 1, :], wvT[:, 512 * c:512 * c + 512],
                                                start=True, stop=True)
                    last.then_inc(values_projected, 1)
                for turn, turn_done in enumerate((scores_half, scores_ready)):
                    for b in both:
                        if turn == 0:
                            pe.wait_ge(keys_ready, t0 + (b + 1))
                            pe.wait_ge(values_ready, t0 + (b + 1))
                        else:
                            pe.wait_ge(scores_half, t0 + (b + 1))
                        takes_the_wait(nc, g, ps[b][:, 0:1])
                        for c in range(pairs):
                            for h in range(2):
                                rows, s = slice(SEQ * h, SEQ * h + SEQ), (h + turn) % PAIR
                                cols = slice(SEQ * s, SEQ * s + SEQ)
                                last = nc.tensor.matmul(ps[b][cols, P * c + SEQ * h:P * c + SEQ * h + SEQ], queries_T[rows, b, c, cols],
                                                        keys_T[rows, b, c, cols], start=True, stop=True)
                        last.then_inc(turn_done, 1)
                for b in both:
                    pe.wait_ge(embedding_ready, t0 + (b + 1))
                    gates = ps[b][:, 1024:2048].rearrange("p (h k) -> p h k", k=SEQ)
                    for c in range(blocks):
                        for half in range(2):
                            hs = slice(8 * half, 8 * half + 8)
                            out = gates[:, hs, keys_at_once * c:keys_at_once * (c + 1)]
                            nc.tensor.matmul(out, g.ones_row[0:1, :], gate_bias[0:1, hs, :], start=True, stop=False, skip_group_check=True)
                            last = nc.tensor.matmul(out, embedding[:, b, P * c:P * c + P], gate_weights[:, hs, :], start=False, stop=True,
                                                    skip_group_check=True)
                    last.then_inc(gates_ready, 1)
                for b in both:
                    pe.wait_ge(probs_ready, t0 + (b + 1))
                    for c in range(pairs):
                        last = nc.tensor.transpose(ps[b][:, 1024 + P * c:1024 + P * c + P], probs[:, b, P * c:P * c + P], g.ident[:, :])
                    last.then_inc(probs_turned, 1)
                for b in both:
                    pe.wait_ge(probs_kept, t0 + (b + 1))
                    takes_the_wait(nc, g, ps[b][:, 0:1])
                    for c in range(pairs):
                        for s in range(PAIR):
                            for h in range(2):
                                rows, cols = slice(SEQ * h, SEQ * h + SEQ), slice(SEQ * s, SEQ * s + SEQ)
                                last = nc.tensor.matmul(ps[b][rows, P * c + SEQ * s:P * c + SEQ * s + SEQ], values[rows, b, s, c, :],
                                                        probs_T[rows, b, c, cols], start=True, stop=True)
                    last.then_inc(attended_ready, 1)
                for b in both:
                    pe.wait_ge(attended_kept, t0 + (b + 1))
                    out = ps[b][:, 1024:1024 + P]
                    nc.tensor.matmul(out, g.ones_row[0:1, :], out_bias[0:1, :], start=True, stop=False)
                    for c in range(pairs):
                        last = nc.tensor.matmul(out, attended_T[:, b, c, :], woT[:, c, :], start=False, stop=c == pairs - 1)
                    last.then_inc(output_ready, 1)

    ph.end()


EXPERTS = 8


def route(nc, ph, g, psum, normed_T, weights, gate_T, capacity, constants, ln_rows=None):
    sb, sem = ph.sb, ph.sem
    tiles = g.tiles
    groups = tiles // STREAMS
    affine = ln_rows is not None
    ln = LayernormState(ph)
    normed = sb("normed", [P, 2, STREAMS, P])
    route_T = sb("route_T", [P, 2, STREAMS, P])
    logits = sb("logits", [P, tiles, EXPERTS])
    normed_ready = sem("normed_ready")
    scaled_ready = sem("scaled_ready")
    shifted_ready = sem("shifted_ready")
    tokens_turned = sem("tokens_turned")
    tokens_kept = sem("tokens_kept")
    logits_ready = sem("logits_ready")
    logits_kept = sem("logits_kept")
    norm_ready = shifted_ready if affine else normed_ready
    turned = [psum[:, b, :] for b in range(2)]
    logit_bank = [psum[:, 2 + b, 0:STREAMS * EXPERTS] for b in range(2)]
    with nc.Block() as block:
        @block.vector
        def _(dve):
            def keep_logits(n, b):
                dve.wait_ge(logits_ready, n + (b + 1))
                nc.vector.tensor_copy(logits[:, bass.ds((n + b) * STREAMS, STREAMS), :].rearrange("p t e -> p (t e)"),
                                      logit_bank[b]).then_inc(logits_kept, 1)

            with dve.Fori(0, groups // 2) as i:
                n0 = dve.snap(i * 2)
                for b in range(2):
                    c0 = (n0 + b) * STREAMS
                    group_statistics(nc, dve, g, n0 + b, c0, ln)
                    dve.wait_ge(ln.rstd_ready, n0 + (b + 1))
                    for s in range(STREAMS):
                        last = nc.vector.tensor_scalar(normed[:, b, s, :], tile_of(g, c0 + s), ln.mean_var[:, s, 0:1],
                                                       ln.rstd[:, s:s + 1], ALU.subtract, ALU.mult)
                    last.then_inc(normed_ready, 1)
                for b in range(2):
                    keep_logits(n0, b)

        @block.gpsimd
        def _(pool):
            with pool.Fori(0, groups // 2) as i:
                n0 = pool.snap(i * 2)
                for b in range(2):
                    group_rstd(nc, pool, g, n0 + b, ln)
                    if affine:
                        pool.wait_ge(normed_ready, n0 + (b + 1))
                        nc.gpsimd.tensor_tensor(normed[:, b, :, :], normed[:, b, :, :], bcast(ln_rows[0][:, :], [(0, STREAMS), (1, P)]),
                                                ALU.mult).then_inc(scaled_ready, 1)
                        pool.wait_ge(scaled_ready, n0 + (b + 1))
                        nc.gpsimd.tensor_tensor(normed[:, b, :, :], normed[:, b, :, :], bcast(ln_rows[1][:, :], [(0, STREAMS), (1, P)]),
                                                ALU.add).then_inc(shifted_ready, 1)

        @block.tensor
        def _(pe):
            with pe.Fori(0, groups // 2) as i:
                n0 = pe.snap(i * 2)
                for b in range(2):
                    pe.wait_ge(norm_ready, n0 + (b + 1))
                    for s in range(STREAMS):
                        last = nc.tensor.transpose(turned[b][:, P * s:P * s + P], normed[:, b, s, :], g.ident[:, :])
                    last.then_inc(tokens_turned, 1)
                for b in range(2):
                    pe.wait_ge(tokens_kept, n0 + (b + 1))
                    for s in range(STREAMS):
                        last = nc.tensor.matmul(logit_bank[b][:, EXPERTS * s:EXPERTS * s + EXPERTS],
                                                route_T[:, b, s, :], gate_T[:, :], start=True, stop=True)
                    last.then_inc(logits_ready, 1)

        @block.scalar
        def _(act):
            with act.Fori(0, groups // 2) as i:
                n0 = act.snap(i * 2)
                for b in range(2):
                    act.wait_ge(tokens_turned, n0 + (b + 1))
                    nc.scalar.copy(route_T[:, b, :, :].rearrange("p s n -> p (s n)"), turned[b])
                    nc.scalar.copy(normed_T[:, bass.ds((n0 + b) * STREAMS, STREAMS), :].rearrange("p s n -> p (s n)"),
                                   turned[b]).then_inc(tokens_kept, 1)

    order = sb("order", [P, EXPERTS])
    before = sb("before", [P, P])
    loaded, step, exp_step, counted = sem("rank_loaded"), sem("rank_step"), sem("rank_exp"), sem("rank_counted")
    best = [sb(f"best_{j}", [P, tiles]) for j in range(2)]
    first = [sb(f"first_{j}", [P, tiles]) for j in range(2)]
    chosen = [sb(f"chosen_{j}", [P, tiles, EXPERTS]) for j in range(2)]
    hit = sb("hit", [P, tiles, EXPERTS])
    ranked = sb("ranked", [P, tiles, EXPERTS])
    gap = sb("gap", [P, tiles])
    gate = [sb(f"gate_{j}", [P, tiles]) for j in range(2)]
    ones_row = sb("scan_ones", [P, tiles])
    counts = sb("counts", [P, tiles, EXPERTS])
    passed = [sb(f"passed_{j}", [P, tiles + 1, EXPERTS]) for j in range(2)]
    place = sb("place", [P, tiles, EXPERTS])
    flat = lambda t: t[:, :, :].rearrange("p t e -> p (t e)")
    over = lambda t: bcast(t[:, :], [(1, tiles), (0, EXPERTS)])
    with nc.Block() as block:
        @block.sync
        def _(sp):
            sp.dma_start(order[:, :], constants["order"]).then_inc(loaded, 16)
            sp.dma_start(before[:, :], constants["before"]).then_inc(loaded, 16)
            sp.wait_ge(loaded, 32)

        @block.scalar
        def _(act):
            act.wait_ge(exp_step, 1)
            nc.scalar.activation(gap[:, :], gap[:, :], ACT.Exp).then_inc(exp_step, 1)

        @block.tensor
        def _(pe):
            if capacity is not None:
                pe.wait_ge(loaded, 32)
                pe.wait_ge(counted, 1)
                for j in range(2):
                    nc.tensor.matmul(psum[:, 2 * j, 0:tiles * EXPERTS], before[:, :], flat(chosen[j]), start=True, stop=True)
                    last = nc.tensor.matmul(psum[:, 2 * j + 1, 0:tiles * EXPERTS], g.ones_full[:, :], flat(chosen[j]), start=True, stop=True)
                last.then_inc(counted, 1)

        @block.vector
        def _(dve):
            done = [0]

            def then(instruction):
                done[0] += 1
                instruction.then_inc(step, 1)
                dve.wait_ge(step, done[0])

            dve.wait_ge(loaded, 32)
            source = logits
            for j in range(2):
                then(nc.vector.tensor_reduce(best[j][:, :], source[:, :, :], X, ALU.max))
                then(nc.vector.tensor_tensor(hit[:, :, :], source[:, :, :], over(best[j]), ALU.is_equal))
                then(nc.vector.tensor_tensor(hit[:, :, :], hit[:, :, :], bcast(order[:, :], [(0, tiles), (1, EXPERTS)]), ALU.mult))
                then(nc.vector.tensor_reduce(first[j][:, :], hit[:, :, :], X, ALU.max))
                then(nc.vector.tensor_tensor(chosen[j][:, :, :], hit[:, :, :], over(first[j]), ALU.is_equal))
                if j == 0:
                    then(nc.vector.scalar_tensor_tensor(flat(ranked), flat(chosen[0]), MASKED, flat(logits), ALU.mult, ALU.add))
                    source = ranked
            nc.vector.tensor_tensor(gap[:, :], best[1][:, :], best[0][:, :], ALU.subtract).then_inc(exp_step, 1)
            dve.wait_ge(exp_step, 2)
            then(nc.vector.tensor_scalar(gate[0][:, :], gap[:, :], 1.0, None, ALU.add))
            then(nc.vector.reciprocal(gate[0][:, :], gate[0][:, :]))
            then(nc.vector.tensor_tensor(gate[1][:, :], gate[0][:, :], gap[:, :], ALU.mult))
            if capacity is not None:
                then(nc.vector.memset(ones_row[:, :], 1.0))
                nc.vector.memset(passed[0][:, 0:1, :], 0.0).then_inc(counted, 1)
                dve.wait_ge(counted, 2)
                for j in range(2):
                    then(nc.vector.tensor_copy(flat(counts), psum[:, 2 * j + 1, 0:tiles * EXPERTS]))
                    if j == 1:
                        then(nc.vector.tensor_copy(passed[1][:, 0:1, :], passed[0][:, tiles:tiles + 1, :]))
                    for e in range(EXPERTS):
                        last = nc.vector.tensor_tensor_scan(passed[j][:, 1:tiles + 1, e], ones_row[:, :], counts[:, :, e],
                                                            passed[j][:, 0:1, e], ALU.mult, ALU.add)
                    then(last)
                    then(nc.vector.tensor_tensor(flat(place), psum[:, 2 * j, 0:tiles * EXPERTS],
                                                 passed[j][:, 0:tiles, :].rearrange("p t e -> p (t e)"), ALU.add))
                    then(nc.vector.scalar_tensor_tensor(flat(chosen[j]), flat(place), float(capacity), flat(chosen[j]), ALU.is_lt, ALU.mult))
            then(nc.vector.tensor_tensor(hit[:, :, :], chosen[0][:, :, :], over(gate[0]), ALU.mult))
            then(nc.vector.tensor_tensor(ranked[:, :, :], chosen[1][:, :, :], over(gate[1]), ALU.mult))
            nc.vector.tensor_tensor(weights[:, :, :], hit[:, :, :], ranked[:, :, :], ALU.add)


def capacity_experts_phase(nc, g, gate_w, fc1_w, fc1_b, fc2_w, fc2_b, constants):
    tiles = g.tiles
    groups = tiles // STREAMS
    hidden = fc1_w.shape[1]
    chunks = hidden // P
    tokens = tiles * P
    capacity = 2 * ((tokens + EXPERTS - 1) // EXPERTS)
    width = STREAMS * P
    ph = Phase(nc, "l2f")
    sb, sem = ph.sb, ph.sem
    psum = ph.psum()
    normed_T = sb("normed_T", [P, tiles, P])
    weights = sb("weights", [P, tiles, EXPERTS])
    fc1_T = sb("fc1_T", [P, EXPERTS, chunks, P])
    fc2 = sb("fc2", [P, EXPERTS, chunks, P])
    raw = sb("raw", [P, EXPERTS, chunks, P])
    fc1_bias = sb("fc1_bias", [P, EXPERTS, chunks])
    gate_raw, gate_T = sb("gate_raw", [EXPERTS, P]), sb("gate_T", [P, EXPERTS])
    out_bias = sb("out_bias", [STREAMS * EXPERTS, STREAMS, P])
    spread_bias = sb("spread_bias", [STREAMS * EXPERTS, STREAMS, P])
    own_tile = sb("own_tile", [STREAMS * EXPERTS, STREAMS])
    loads = [(raw[:, :, :, :].rearrange("p e c d -> p (e c) d"), fc1_w.rearrange("e (c p) d -> p (e c) d", p=P)),
             (fc2[:, :, :, :].rearrange("p e c d -> p (e c) d"), fc2_w.rearrange("e (c p) d -> p (e c) d", p=P)),
             (fc1_bias[:, :, :].rearrange("p e c -> p (e c)"), fc1_b.rearrange("e o (c p) -> p (e o c)", p=P)),
             (gate_raw[:, :], gate_w), (own_tile[:, :], constants["own_tile"])]
    for s in range(STREAMS):
        for r in range(STREAMS):
            loads.append((out_bias[EXPERTS * s:EXPERTS * s + EXPERTS, r, :], fc2_b.rearrange("e o d -> (e o) d")))
    turned = [(fc1_T[:, e, c, :], raw[:, e, c, :]) for e in range(EXPERTS) for c in range(chunks)]
    turned.append((gate_T[:, :], gate_raw[:, :]))
    transpose_weights(nc, ph, loads, turned, g.ident, psum)
    route(nc, ph, g, psum, normed_T, weights, gate_T, capacity, constants)

    items = EXPERTS * chunks
    hidden_buf = sb("hidden_buf", [P, 4, width])
    group_weights = sb("group_weights", [P, STREAMS * EXPERTS])
    group_weights_T = sb("group_weights_T", [STREAMS * EXPERTS, P])
    bias_spread = sem("bias_spread")
    banks_free = sem("banks_free")
    group_weights_ready = sem("group_weights_ready")
    weights_turned = sem("weights_turned")
    weights_kept = sem("weights_kept")
    bias_ready = sem("bias_ready")
    bias_added = sem("bias_added")
    hidden_raw = sem("hidden_raw")
    hidden_ready = sem("hidden_ready")
    expert_ready = sem("expert_ready")
    raw_bank = [psum[:, n, :] for n in range(4)]
    sum_bank = [psum[:, 4 + n, :] for n in range(2)]
    bias_bank, turn_bank = psum[:, 6, :], psum[:, 7, :]
    rows = slice(0, STREAMS * EXPERTS)
    with nc.Block() as block:
        @block.vector
        def _(dve):
            nc.vector.tensor_tensor(spread_bias[:, :, :], out_bias[:, :, :], bcast(own_tile[:, :], [(1, STREAMS), (0, P)]),
                                    ALU.mult).then_inc(bias_spread, 1)
            dve.wait_ge(bias_spread, 1)
            nc.vector.memset(group_weights[:, :], 0.0).then_inc(banks_free, 2)
            dve.wait_ge(banks_free, 2)
            with dve.Fori(0, groups) as i:
                t0 = dve.snap(i * STREAMS)
                e0 = dve.snap(i * EXPERTS)
                dve.wait_ge(banks_free, e0 + 2)
                nc.vector.tensor_copy(group_weights[:, :], weights[:, bass.ds(t0, STREAMS), :].rearrange("p t e -> p (t e)")).then_inc(group_weights_ready, 1)
                dve.wait_ge(bias_ready, i + 1)
                row = g.x[:, bass.ds(t0, STREAMS), :].rearrange("p t d -> p (t d)")
                nc.vector.tensor_tensor(row, row, bias_bank, ALU.add).then_inc(bias_added, 1)
                dve.wait_ge(bias_added, i + 1)
                for e in range(EXPERTS):
                    dve.wait_ge(expert_ready, e0 + (e + 1))
                    dve.wait_ge(banks_free, e0 + (e + 2))
                    for s in range(STREAMS):
                        row = tile_of(g, t0 + s)
                        c = EXPERTS * s + e
                        last = nc.vector.scalar_tensor_tensor(row, sum_bank[e % 2][:, P * s:P * s + P], group_weights[:, c:c + 1], row,
                                                              ALU.mult, ALU.add)
                    last.then_inc(banks_free, 1)

        @block.scalar
        def _(act):
            with act.Fori(0, groups) as i:
                n0 = act.snap(i * items)
                act.wait_ge(weights_turned, i + 1)
                nc.scalar.copy(group_weights_T[:, :], turn_bank[rows, 0:P]).then_inc(weights_kept, 1)
                for n in range(items):
                    e, c = n // chunks, n % chunks
                    act.wait_ge(hidden_raw, n0 + (n + 1))
                    nc.scalar.activation(hidden_buf[:, n % 4, :], raw_bank[n % 4], ACT.Relu, bias=fc1_bias[:, e, c:c + 1]).then_inc(hidden_ready, 1)

        @block.tensor
        def _(pe):
            pe.wait_ge(bias_spread, 1)
            with pe.Fori(0, groups) as i:
                t0 = pe.snap(i * STREAMS)
                n0 = pe.snap(i * items)
                e0 = pe.snap(i * EXPERTS)
                tokens_T = normed_T[:, bass.ds(t0, STREAMS), :].rearrange("p t n -> p (t n)")
                pe.wait_ge(group_weights_ready, i + 1)
                nc.tensor.transpose(turn_bank[rows, 0:P], group_weights[:, :], g.ident[:, :]).then_inc(weights_turned, 1)
                for n in range(items + 2):
                    if n < items:
                        nc.tensor.matmul(raw_bank[n % 4], fc1_T[:, n // chunks, n % chunks, :], tokens_T, start=True, stop=True).then_inc(hidden_raw, 1)
                    if n == 0:
                        pe.wait_ge(weights_kept, i + 1)
                        nc.tensor.matmul(bias_bank, group_weights_T[:, :], spread_bias[:, :, :].rearrange("p s d -> p (s d)"),
                                         start=True, stop=True).then_inc(bias_ready, 1)
                    if n >= 2:
                        m = n - 2
                        e, c = m // chunks, m % chunks
                        pe.wait_ge(hidden_ready, n0 + (m + 1))
                        if c == 0:
                            pe.wait_ge(banks_free, e0 + (e + 1))
                        for s in range(STREAMS):
                            last = nc.tensor.matmul(sum_bank[e % 2][:, P * s:P * s + P], hidden_buf[:, m % 4, P * s:P * s + P], fc2[:, e, c, :],
                                                    start=c == 0 and s == 0, stop=c == chunks - 1, skip_group_check=True)
                        if c == chunks - 1:
                            last.then_inc(expert_ready, 1)

    ph.end()


def normalize_phase(nc, g):
    ph = Phase(nc, "norm")
    ln = LayernormState(ph, n=8)
    x_normed = ph.sem("x_normed")
    with nc.Block() as block:
        @block.gpsimd
        def _(pool):
            with pool.Fori(0, g.tiles // ln.n) as i:
                group_rstd(nc, pool, g, i, ln)

        @block.vector
        def _(dve):
            with dve.Fori(0, g.tiles // ln.n) as i:
                t0 = dve.snap(i * ln.n)
                group_statistics(nc, dve, g, i, t0, ln)
                dve.wait_ge(ln.rstd_ready, i + 1)
                for s in range(ln.n):
                    row = tile_of(g, t0 + s)
                    nc.vector.tensor_scalar(row, row, ln.mean_var[:, s, 0:1], ln.rstd[:, s:s + 1],
                                            ALU.subtract, ALU.mult).then_inc(x_normed, 1)

    ph.end()


def gated_experts_phase(nc, g, x_before, ln_scale, ln_shift, gate_w, w1, w2, w3, constants):
    tiles = g.tiles
    groups = tiles // STREAMS
    hidden = w1.shape[2]
    chunks = hidden // P
    width = STREAMS * P
    ph = Phase(nc, "l3e")
    sb, sem = ph.sb, ph.sem
    psum = ph.psum()
    normed_T = sb("normed_T", [P, tiles, P])
    weights = sb("weights", [P, tiles, EXPERTS])
    w1_in, w2_in = sb("w1_in", [P, EXPERTS, hidden]), sb("w2_in", [P, EXPERTS, hidden])
    w3_in = sb("w3_in", [P, EXPERTS, chunks, P])
    gate_T = sb("gate_T", [P, EXPERTS])
    ln_rows = (sb("ln_scale", [P, P]), sb("ln_shift", [P, P]))
    loads = [(w1_in[:, :, :], w1.rearrange("e d h -> d e h")), (w2_in[:, :, :], w2.rearrange("e d h -> d e h")),
             (w3_in[:, :, :, :].rearrange("p e c d -> p (e c) d"), w3.rearrange("e (c p) d -> p (e c) d", p=P)), (gate_T[:, :], gate_w),
             (ln_rows[0][:, :], row_on_all(ln_scale, P)), (ln_rows[1][:, :], row_on_all(ln_shift, P))]
    transpose_weights(nc, ph, loads, [], g.ident, psum)
    route(nc, ph, g, psum, normed_T, weights, gate_T, None, constants, ln_rows)

    items = EXPERTS * chunks
    act_buf = sb("act_buf", [P, 2, width])
    hidden_buf = sb("hidden_buf", [P, 2, width])
    before_added = sem("before_added")
    banks_free = sem("banks_free")
    gate_raw = sem("gate_raw")
    up_raw = sem("up_raw")
    act_ready = sem("act_ready")
    hidden_ready = sem("hidden_ready")
    expert_ready = sem("expert_ready")
    gate_bank = [psum[:, n, :] for n in range(2)]
    up_bank = [psum[:, 2 + n, :] for n in range(2)]
    sum_bank = [psum[:, 4 + n, :] for n in range(2)]
    with nc.Block() as block:
        @block.vector
        def _(dve):
            nc.vector.memset(act_buf[:, 0, 0:1], 0.0).then_inc(banks_free, 2)
            with dve.Fori(0, groups) as i:
                t0 = dve.snap(i * STREAMS)
                e0 = dve.snap(i * EXPERTS)
                n0 = dve.snap(i * items)

                row = g.x[:, bass.ds(t0, STREAMS), :].rearrange("p t d -> p (t d)")
                nc.vector.tensor_tensor(row, row, x_before[:, bass.ds(t0, STREAMS), :].rearrange("p t d -> p (t d)"),
                                        ALU.add).then_inc(before_added, 1)
                dve.wait_ge(before_added, i + 1)

                def add(e):
                    dve.wait_ge(expert_ready, e0 + (e + 1))
                    dve.wait_ge(banks_free, e0 + (e + 2))
                    for s in range(STREAMS):
                        row = tile_of(g, t0 + s)
                        last = nc.vector.scalar_tensor_tensor(row, sum_bank[e % 2][:, P * s:P * s + P],
                                                              weights[:, bass.ds(t0 + s, 1), e:e + 1].rearrange("p a e -> p (a e)"), row,
                                                              ALU.mult, ALU.add)
                    last.then_inc(banks_free, 1)

                for n in range(items):
                    dve.wait_ge(act_ready, n0 + (n + 1))
                    dve.wait_ge(up_raw, n0 + (n + 1))
                    nc.vector.tensor_tensor(hidden_buf[:, n % 2, :], act_buf[:, n % 2, :], up_bank[n % 2], ALU.mult).then_inc(hidden_ready, 1)
                    if n % chunks == 1 and n >= chunks:
                        add(n // chunks - 1)
                add(EXPERTS - 1)

        @block.scalar
        def _(act):
            act.wait_ge(banks_free, 2)
            with act.Fori(0, groups) as i:
                n0 = act.snap(i * items)
                for n in range(items):
                    act.wait_ge(gate_raw, n0 + (n + 1))
                    nc.scalar.activation(act_buf[:, n % 2, :], gate_bank[n % 2], ACT.Silu).then_inc(act_ready, 1)

        @block.tensor
        def _(pe):
            with pe.Fori(0, groups) as i:
                t0 = pe.snap(i * STREAMS)
                n0 = pe.snap(i * items)
                e0 = pe.snap(i * EXPERTS)
                tokens_T = normed_T[:, bass.ds(t0, STREAMS), :].rearrange("p t n -> p (t n)")
                for n in range(items + 1):
                    if n < items:
                        cols = slice(P * (n % chunks), P * (n % chunks) + P)
                        nc.tensor.matmul(gate_bank[n % 2], w1_in[:, n // chunks, cols], tokens_T, start=True, stop=True).then_inc(gate_raw, 1)
                        nc.tensor.matmul(up_bank[n % 2], w2_in[:, n // chunks, cols], tokens_T, start=True, stop=True).then_inc(up_raw, 1)
                    if n >= 1:
                        m = n - 1
                        e, c = m // chunks, m % chunks
                        pe.wait_ge(hidden_ready, n0 + (m + 1))
                        if c == 0:
                            pe.wait_ge(banks_free, e0 + (e + 1))
                        for s in range(STREAMS):
                            last = nc.tensor.matmul(sum_bank[e % 2][:, P * s:P * s + P], hidden_buf[:, m % 2, P * s:P * s + P], w3_in[:, e, c, :],
                                                    start=c == 0 and s == 0, stop=c == chunks - 1, skip_group_check=True)
                        if c == chunks - 1:
                            last.then_inc(expert_ready, 1)

    ph.end()



def program(nc, d, out, stages):
    tokens, width = d["x"].shape[0] * d["x"].shape[1], d["x"].shape[2]
    tiles = tokens // P
    x_tiles = d["x"].rearrange("(t a) s d -> (a s) t d", a=PAIR)
    out_tiles = out.rearrange("(t a) s d -> (a s) t d", a=PAIR)
    context = d["ctx_1024"].rearrange("(t a) s d -> t (a s) d", a=PAIR)
    key_mask = d["mask_BxS2_ik0"].rearrange("(t a) k -> t a k", a=PAIR)
    with ExitStack() as ctx:
        def sb(label, shape, dt=F32):
            return ctx.enter_context(nc.sbuf_tensor(label, shape, dt))

        g = Resident(sb, tiles)
        x_loaded = ctx.enter_context(nc.semaphore("x_loaded"))
        ident_ready = ctx.enter_context(nc.semaphore("ident_ready"))
        out_stored = ctx.enter_context(nc.semaphore("out_stored"))
        with nc.Block() as block:
            @block.sync
            def _(sp):
                sp.dma_start(g.ident[:, :], d["const_ident"]).then_inc(ident_ready, 16)
                sp.dma_start(g.group_mask[:, :], d["const_group_mask"]).then_inc(x_loaded, 16)
                sp.dma_start(g.x[:, :, :], x_tiles).then_inc(x_loaded, 16)
                sp.wait_ge(x_loaded, 32)

            @block.vector
            def _(dve):
                nc.vector.memset(g.ones_row[:, :], 1.0)
                nc.vector.memset(g.ones_full[:, :], 1.0)
                nc.vector.memset(g.minus_half[:, :], -0.5)
                dve.wait_ge(ident_ready, 16)
                nc.vector.tensor_copy(g.ident_bf[:, :], g.ident[:, :])

        def w(layer, key):
            return d[f"{layer}_{key}"]

        if stages >= 1:
            attention_phase(nc, "l0x", g, *[w("L0_xattn", k) for k in ("Wq", "bq", "Wk", "bk", "Wv", "bv", "Wo", "bo")],
                            context=context, key_mask=key_mask)
        if stages >= 2:
            int8_ffn_phase(nc, g, *[w("L0_ffn", k) for k in ("weight_int8", "weight_scale", "bias")])
        if stages >= 3:
            attention_phase(nc, "l1x", g, wo=w("L1_xattn", "Wo"), context=context)

        if stages >= 4:
            ternary_ffn_phase(nc, g, *[w("L1_ffn", k) for k in ("norm1_w", "w1", "act_scale", "act_bias", "norm2_w", "w2")])

        if stages >= 5:
            box_attention_phase(nc, g, d["fside_BxSx4_0"].rearrange("(t a) s d -> (a s) t d", a=PAIR),
                                context.rearrange("(n t) p d -> n t p d", t=2),
                                *[w("L2_xattn", k) for k in ("Wq", "bq", "Wk", "bk", "Wv", "bv", "Wo", "bo", "Wg", "bg")],
                                {k: d["const_" + k] for k in ("same_key", "block_of", "diagonal", "floor_phase")})

        ranking = {k: d["const_" + k] for k in ("order", "before", "own_tile")}
        if stages >= 6:
            capacity_experts_phase(nc, g, *[w("L2_ffn", k) for k in ("gate_w", "fc1_w", "fc1_b", "fc2_w", "fc2_b")], ranking)
        if stages >= 7:
            attention_phase(nc, "l3x", g, *[w("L3_xattn", k) for k in ("Wq", "bq", "Wk", "bk", "Wv", "bv", "Wo", "bo")],
                            context=context, score_mask=d["mask_1x1xSxS2_ff0"].rearrange("a b q k -> (a b q) k"))
        if stages >= 8:
            x_before = sb("x_before", [P, tiles, P])
            with nc.Block() as block:
                @block.vector
                def _(dve):
                    nc.vector.tensor_copy(x_before[:, :, :], g.x[:, :, :])
            normalize_phase(nc, g)

            attention_phase(nc, "l3a", g, wq=w("L3_ffn", "wq"), wk=w("L3_ffn", "wk"), wv=w("L3_ffn", "wv"), wo=w("L3_ffn", "wo"),
                            bo=w("L3_ffn", "bo"), weights_turned=True, score_mask=d["const_causal"],
                            ln_scale=w("L3_ffn", "ln1_scale"), ln_shift=w("L3_ffn", "ln1_shift"))
            gated_experts_phase(nc, g, x_before, *[w("L3_ffn", k) for k in ("ln2_scale", "ln2_shift", "gate_w", "w1", "w2", "w3")],
                                ranking)

        with nc.Block() as block:
            @block.sync
            def _(sp):
                sp.dma_start(out_tiles, g.x[:, :, :]).then_inc(out_stored, 16)
                sp.wait_ge(out_stored, 16)


STAGES = 9


def kernel(**inputs):
    import numpy as np
    import concourse.bacc as bacc
    from concourse.bass_utils import run_bass_kernel_spmd

    p = np.arange(P)
    constants = {
        "const_ident": np.eye(P, dtype=np.float32),
        "const_group_mask": (p[:, None] % 32 // HD == np.arange(GROUP)[None, :]).astype(np.float32),
    }
    key, feature = p // 8, p % 8
    constants["const_same_key"] = (p[:, None] % 16 == key[None, :]).astype(np.float32)
    constants["const_block_of"] = (p[:, None] // 16 == np.arange(8)[None, :]).astype(np.float32)
    constants["const_diagonal"] = (key[:, None] == np.arange(16)[None, :]).astype(np.float32)
    constants["const_floor_phase"] = np.stack([np.where(feature % 4 < 2, 1e-3, 0.0), np.where(feature < 4, 0.0, 0.25)], 1).astype(np.float32)
    constants["const_causal"] = np.where(np.arange(SEQ)[:, None] < np.arange(SEQ)[None, :], MASKED, 0.0).astype(np.float32)
    constants["const_order"] = np.broadcast_to(np.arange(EXPERTS, 0, -1, dtype=np.float32), (P, EXPERTS)).copy()
    constants["const_before"] = (p[:, None] < p[None, :]).astype(np.float32)
    constants["const_own_tile"] = (np.arange(STREAMS * EXPERTS)[:, None] // EXPERTS == np.arange(STREAMS)[None, :]).astype(np.float32)
    nc = bacc.Bacc("TRN2", target_bir_lowering=False, num_devices=1)
    arrays, d = {}, {}
    for name, a in list(inputs.items()) + list(constants.items()):
        a = np.ascontiguousarray(a)
        if a.dtype.kind in "iu":
            a = a.astype(np.int32)
        arrays[name] = a
        d[name] = nc.dram_tensor(name, a.shape, mybir.dt.from_np(a.dtype), kind="ExternalInput").ap()
    out = nc.dram_tensor("out", inputs["x"].shape, F32, kind="ExternalOutput").ap()
    program(nc, d, out, STAGES)
    result = run_bass_kernel_spmd(nc, [arrays], core_ids=[0])
    return result.results[0]["out"]
```

```python
from contextlib import ExitStack

import concourse.bass as bass
from concourse import mybir

F32 = mybir.dt.float32
BF16 = mybir.dt.bfloat16
I32 = mybir.dt.int32
ALU = mybir.AluOpType
ACT = mybir.ActivationFunctionType
X = mybir.AxisListType.X

P = 128
SEQ = 64
PAIR = P // SEQ
HEADS = 16
HD = P // HEADS
GROUP = 32 // HD
STREAMS = 4
LN_EPS = 1e-5
PARTS = (1, 0, -1, -2, -3)
MASKED = -1e30


def bcast(ap, dims):
    return bass.AP(ap.tensor, ap.offset, [list(ap.ap[0])] + [list(d) for d in dims])


def row_on_all(dram, n, parts=P, offset=0):
    return bass.AP(dram.tensor, dram.offset + offset, [[0, parts], [1, n]])


def column(dram, n=P, offset=0):
    return bass.AP(dram.tensor, dram.offset + offset, [[1, n], [1, 1]])


class Resident:

    def __init__(self, sb, tiles):
        self.tiles = tiles
        self.x = sb("x_resident", [P, tiles, P])
        self.ident = sb("ident", [P, P])
        self.ident_bf = sb("ident_bf", [P, P], BF16)
        self.group_mask = sb("group_mask", [P, GROUP])
        self.ones_bf = sb("ones_bf", [P, P], BF16)
        self.ones_full = sb("ones_full", [P, P])
        self.minus_half = sb("minus_half", [P, 2 * STREAMS])


class Phase:

    def __init__(self, nc, name):
        self.nc, self.name, self.stack, self.sems = nc, name, ExitStack(), []

    def sb(self, label, shape, dt=F32):
        return self.stack.enter_context(self.nc.sbuf_tensor(f"{self.name}_{label}", shape, dt))

    def psum(self):
        return self.stack.enter_context(self.nc.psum_tensor(f"{self.name}_psum", [P, 8, 512], F32))

    def sem(self, label):
        self.sems.append(self.nc.alloc_semaphore(f"{self.name}_{label}"))
        return self.sems[-1]

    def end(self):
        self.nc.clear_and_free_semaphores(self.sems)
        self.nc.all_engine_barrier()
        self.stack.close()


class ExactParts:

    def __init__(self, ph, label, n):
        self.rows = ph.sb(label + "_parts", [3 * 32, n], BF16)
        self.rest = ph.sb(label + "_rest", [1, 2, n])
        self.step = ph.sem(label + "_step")

    def split(self, nc, dve, row):
        nc.vector.memset(self.rows[:, :], 0.0).then_inc(self.step, 1)
        dve.wait_ge(self.step, 2)
        nc.vector.tensor_copy(self.rows[0:1, :], row).then_inc(self.step, 1)
        dve.wait_ge(self.step, 3)
        nc.vector.tensor_tensor(self.rest[0:1, 0, :], row, self.rows[0:1, :], ALU.subtract).then_inc(self.step, 1)
        dve.wait_ge(self.step, 4)
        nc.vector.tensor_copy(self.rows[32:33, :], self.rest[0:1, 0, :]).then_inc(self.step, 1)
        dve.wait_ge(self.step, 5)
        nc.vector.tensor_tensor(self.rest[0:1, 1, :], self.rest[0:1, 0, :], self.rows[32:33, :], ALU.subtract).then_inc(self.step, 1)
        dve.wait_ge(self.step, 6)
        nc.vector.tensor_copy(self.rows[64:65, :], self.rest[0:1, 1, :]).then_inc(self.step, 1)
        dve.wait_ge(self.step, 7)


def transpose_weights(nc, ph, loads, turned, ident, psum):
    weights_loaded = ph.sem("weights_loaded")
    block_turned = ph.sem("block_turned")
    block_kept = ph.sem("block_kept")
    n_loads = len(loads)
    with nc.Block() as block:
        @block.sync
        def _(sp):
            for tile, source in loads:
                sp.dma_start(tile, source, allow_slow_non_contiguous=True).then_inc(weights_loaded, 16)
            sp.wait_ge(weights_loaded, 16 * n_loads)

        @block.tensor
        def _(pe):
            pe.wait_ge(weights_loaded, 16 * n_loads)
            for n, (dst, src) in enumerate(turned):
                if n >= 8:
                    pe.wait_ge(block_kept, n - 7)
                rows, cols = src.shape
                nc.tensor.transpose(psum[0:cols, n % 8, 0:rows], src, ident[0:rows, 0:rows]).then_inc(block_turned, 1)

        @block.vector
        def _(dve):
            for n, (dst, src) in enumerate(turned):
                rows, cols = src.shape
                dve.wait_ge(block_turned, n + 1)
                nc.vector.tensor_copy(dst, psum[0:cols, n % 8, 0:rows]).then_inc(block_kept, 1)


def tile_of(g, t):
    return g.x[:, bass.ds(t, 1), :].rearrange("p a d -> p (a d)")


class LayernormState:

    def __init__(self, ph, tag="", n=STREAMS):
        self.n = n
        self.stats = ph.sb("stats" + tag, [P, n, 6])
        self.mean_var = ph.sb("mean_var" + tag, [P, n, 2])
        self.var_eps = ph.sb("var_eps" + tag, [P, n])
        self.rstd = ph.sb("rstd" + tag, [P, n])
        self.stats_ready = ph.sem("stats_ready" + tag)
        self.mean_ready = ph.sem("mean_ready" + tag)
        self.var_eps_ready = ph.sem("var_eps_ready" + tag)
        self.rstd_ready = ph.sem("rstd_ready" + tag)


def group_statistics(nc, dve, g, i, c0, ln, t0=None):
    t0 = c0 if t0 is None else t0
    last = ln.n - 1
    nc.vector.bn_stats(ln.stats[:, 0, :], tile_of(g, t0)).then_inc(ln.stats_ready, 1)
    for s in range(1, ln.n):
        dve.wait_ge(ln.stats_ready, c0 + s)
        nc.vector.bn_stats(ln.stats[:, s, :], tile_of(g, t0 + s)).then_inc(ln.stats_ready, 1)
        nc.vector.bn_aggr(ln.mean_var[:, s - 1, :], ln.stats[:, s - 1, :]).then_inc(ln.mean_ready, 1)
    dve.wait_ge(ln.mean_ready, c0 + last)
    dve.wait_ge(ln.stats_ready, c0 + ln.n)
    nc.vector.tensor_scalar(ln.var_eps[:, 0:last], ln.mean_var[:, 0:last, 1], LN_EPS, None, ALU.add)
    nc.vector.bn_aggr(ln.mean_var[:, last, :], ln.stats[:, last, :]).then_inc(ln.mean_ready, 1)
    dve.wait_ge(ln.mean_ready, c0 + ln.n)
    nc.vector.tensor_scalar(ln.var_eps[:, last:], ln.mean_var[:, last, 1:2], LN_EPS, None, ALU.add).then_inc(ln.var_eps_ready, 1)


def group_rstd(nc, pool, g, i, ln):
    pool.wait_ge(ln.var_eps_ready, i + 1)
    nc.gpsimd.tensor_tensor(ln.rstd[:, :], ln.var_eps[:, :], g.minus_half[:, 0:ln.n], ALU.pow).then_inc(ln.rstd_ready, 1)


class Tile:

    def __init__(self, base, offset, load_base, streams):
        self.t = base + offset
        self.stream = offset % streams
        self.loads = load_base + 16 * (offset // streams)


def run_tiles(engine, tiles, streams, parts, step):
    deepest = -min(parts)
    peeled = streams * -(-deepest // streams)

    def step_at(n):
        step(*[Tile(0, n + k, 0, streams) if 0 <= n + k < tiles else None for k in parts])

    for n in range(peeled):
        step_at(n)
    with engine.Fori(0, (tiles - peeled) // streams - 1) as i:
        base, load_base = engine.snap(i * streams), engine.snap(i * 16)
        for m in range(streams):
            step(*[Tile(base, peeled + m + k, load_base, streams) for k in parts])
    for n in range(tiles - streams, tiles + deepest):
        step_at(n)


def tile_statistics(nc, g, tile, ln):
    nc.vector.bn_stats(ln.stats[:, 0, :], tile_of(g, tile.t)).then_inc(ln.stats_ready, 1)


def tile_moments(nc, dve, tile, ln):
    dve.wait_ge(ln.stats_ready, tile.t + 1)
    nc.vector.memset(ln.var_eps[:, 0:1], 0.0)
    nc.vector.bn_aggr(ln.mean_var[:, 0, :], ln.stats[:, 0, :]).then_inc(ln.mean_ready, 1)
    dve.wait_ge(ln.mean_ready, tile.t + 1)
    nc.vector.tensor_scalar(ln.var_eps[:, :], ln.mean_var[:, 0, 1:2], LN_EPS, None, ALU.add).then_inc(ln.var_eps_ready, 1)


def norm_tile(nc, dve, g, tile, ln, normed, normed_ready):
    dve.wait_ge(ln.rstd_ready, tile.t + 1)
    nc.vector.tensor_scalar(normed[:, tile.stream, :], tile_of(g, tile.t), ln.mean_var[:, 0, 0:1], ln.rstd[:, 0:1],
                            ALU.subtract, ALU.mult).then_inc(normed_ready, 1)


def tile_rstd(nc, pool, g, tile, ln):
    pool.wait_ge(ln.var_eps_ready, tile.t + 1)
    nc.gpsimd.tensor_tensor(ln.rstd[:, :], ln.var_eps[:, :], g.minus_half[:, 0:1], ALU.pow).then_inc(ln.rstd_ready, 1)


def norm_groups(nc, dve, g, lns, norm):
    def statistics(i, b):
        group_statistics(nc, dve, g, i, i * STREAMS, lns[b], (i * 2 + b) * STREAMS)

    rounds = g.tiles // STREAMS // 2
    statistics(0, 0)
    with dve.Fori(0, rounds - 1) as i:
        statistics(i, 1)
        norm(i, 0)
        statistics(i + 1, 0)
        norm(i, 1)
    statistics(rounds - 1, 1)
    norm(rounds - 1, 0)
    norm(rounds - 1, 1)


def attention_phase(nc, name, g, wq=None, bq=None, wk=None, bk=None, wv=None, bv=None, wo=None, bo=None,
                    weights_turned=False, context=None, key_mask=None, score_mask=None, ln_scale=None, ln_shift=None):
    tiles = g.tiles
    own = context is None
    affine = ln_scale is not None
    masked = key_mask is not None or score_mask is not None
    scale = HD ** -0.5
    ph = Phase(nc, name)
    sb, sem = ph.sb, ph.sem
    psum = ph.psum()
    ps = [psum[:, 2 * s:2 * s + 2, :].rearrange("p b n -> p (b n)") for s in range(STREAMS)]
    wqT, wkT, wvT, woT = (sb(n, [P, P]) if w is not None else None
                          for n, w in (("wqT", wq), ("wkT", wk), ("wvT", wv), ("woT", wo)))
    bq_col, bk_col, bv_col = (sb(n, [P, 1]) if b is not None else None
                              for n, b in (("bq", bq), ("bk", bk), ("bv", bv)))
    bo_row = sb("bo", [1, P]) if bo is not None else None
    out_bias = sb("out_bias", [1, P]) if bo is not None else None
    bias_parts = ExactParts(ph, "out_bias", P) if bo is not None else None
    bq_scaled = sb("bq_scaled", [P, 1]) if bq is not None else None
    given = [(w, t) for w, t in ((wq, wqT), (wk, wkT), (wv, wvT), (wo, woT)) if w is not None]
    raw = sb("raw", [P, len(given), P])
    small = [(t[:, :], column(b)) for b, t in ((bq, bq_col), (bk, bk_col), (bv, bv_col)) if b is not None]
    if bo is not None:
        small.append((bo_row[:, :], row_on_all(bo, P, 1)))
    if affine:
        ln_scale_rows, ln_shift_rows = sb("ln_scale", [P, P]), sb("ln_shift", [P, P])
        small += [(ln_scale_rows[:, :], row_on_all(ln_scale, P)), (ln_shift_rows[:, :], row_on_all(ln_shift, P))]
    if score_mask is not None:
        mask_rows = sb("mask_rows", [P, SEQ])
        small += [(mask_rows[SEQ * s:SEQ * s + SEQ, :], score_mask) for s in range(PAIR)]
    if weights_turned:
        transpose_weights(nc, ph, [(t[:, :], w) for w, t in given] + small, [], g.ident, psum)
    else:
        transpose_weights(nc, ph, [(raw[:, n, :], w) for n, (w, t) in enumerate(given)] + small,
                          [(t[:, :], raw[:, n, :]) for n, (w, t) in enumerate(given)], g.ident, psum)

    ln = LayernormState(ph, n=1)
    normed = sb("normed", [P, STREAMS, P])
    scaled = sb("scaled", [P, STREAMS, P]) if affine else None
    shifted_norm = sb("shifted_norm", [P, STREAMS, P]) if affine else None
    context_in = sb("context_in", [P, STREAMS, P])
    inputs_T = sb("inputs_T", [P, STREAMS, 2, P])
    query_side, key_side = (1, 1) if own else (0, 1)
    queries_T = sb("queries_T", [P, STREAMS, P])
    keys_block = sb("keys_block", [P, STREAMS, PAIR, GROUP, SEQ])
    values_block = sb("values_block", [P, STREAMS, PAIR, HEADS // 2, 2, HD + 1])
    probs = sb("probs", [P, STREAMS, HEADS * SEQ])
    probs_T = sb("probs_T", [P, STREAMS, HEADS * SEQ])
    negmax = sb("negmax", [P, STREAMS, HEADS])
    recip = sb("recip", [P, STREAMS, HEADS])
    attended = sb("attended", [P, STREAMS, P])
    attended_T = sb("attended_T", [P, STREAMS, P])
    if key_mask is not None:
        mask_int = sb("mask_int", [P, STREAMS, SEQ], I32)
        mask_add = sb("mask_add", [P, STREAMS, SEQ])

    context_loaded = [sem(f"context_loaded_{n}") for n in range(2)]
    mask_loaded = [sem(f"mask_loaded_{n}") for n in range(2)]
    mask_ready = sem("mask_ready")
    bias_summed = sem("bias_summed")
    constants_ready = sem("constants_ready")
    normed_ready = sem("normed_ready")
    scaled_ready = sem("scaled_ready")
    shifted_ready = sem("shifted_ready")
    inputs_turned = sem("inputs_turned")
    inputs_ready = sem("inputs_ready")
    projected = sem("projected")
    queries_ready = sem("queries_ready")
    keys_ready = sem("keys_ready")
    scores_half = sem("scores_half")
    scores_ready = sem("scores_ready")
    masked_ready = sem("masked_ready")
    negmax_ready = sem("negmax_ready")
    shifted_scores = sem("shifted_scores")
    probs_ready = sem("probs_ready")
    probs_turned = sem("probs_turned")
    turned_kept = sem("turned_kept")
    attended_raw = sem("attended_raw")
    recip_ready = sem("recip_ready")
    attended_ready = sem("attended_ready")
    attended_turned = sem("attended_turned")
    attended_kept = sem("attended_kept")
    output_ready = sem("output_ready")
    tile_done = sem("tile_done")

    norm_out, norm_out_ready = (shifted_norm, shifted_ready) if affine else (normed, normed_ready)
    with nc.Block() as block:
        @block.sync
        def _(sp):
            def load(parity, first):
                pair = slice(2 * parity, 2 * parity + 2)
                sp.dma_start(context_in[:, pair, :],
                             context[bass.ds(first, 2), :, :].rearrange("t p d -> p t d")).then_inc(context_loaded[parity], 16)

            def load_mask(parity, first):
                pair = slice(2 * parity, 2 * parity + 2)
                for s in range(PAIR):
                    source = key_mask[bass.ds(first, 2), s:s + 1, :].rearrange("t a k -> a t k").to_broadcast([SEQ, 2, SEQ])
                    sp.dma_start(mask_int[SEQ * s:SEQ * s + SEQ, pair, :], source).then_inc(mask_loaded[parity], 16)

            for parity in range(2):
                if not own:
                    load(parity, 2 * parity)
                if key_mask is not None:
                    load_mask(parity, 2 * parity)
            if not own:
                with sp.Fori(0, tiles // STREAMS - 1) as i:
                    t0 = sp.snap(i * STREAMS)
                    for parity in range(2):
                        sp.wait_ge(queries_ready, t0 + (2 * parity + 2))
                        load(parity, t0 + (2 * parity + STREAMS))
                        if key_mask is not None:
                            sp.wait_ge(mask_ready, t0 + (2 * parity + 2))
                            load_mask(parity, t0 + (2 * parity + STREAMS))

        @block.gpsimd
        def _(pool):
            def norm(tile):
                tile_rstd(nc, pool, g, tile, ln)
                if affine:
                    s = tile.stream
                    pool.wait_ge(normed_ready, tile.t + 1)
                    nc.gpsimd.tensor_tensor(scaled[:, s, :], normed[:, s, :], ln_scale_rows[:, :],
                                            ALU.mult).then_inc(scaled_ready, 1)
                    s = tile.stream
                    pool.wait_ge(scaled_ready, tile.t + 1)
                    nc.gpsimd.tensor_tensor(shifted_norm[:, s, :], scaled[:, s, :], ln_shift_rows[:, :],
                                            ALU.add).then_inc(shifted_ready, 1)

            norm(Tile(0, 0, 0, STREAMS))
            run_tiles(pool, tiles, STREAMS, PARTS, lambda ahead, *others: norm(ahead) if ahead else None)

        @block.tensor
        def _(pe):
            if bo is not None and bv is not None:
                nc.tensor.matmul(ps[0][0:1, 0:P], bv_col[:, 0:1], woT[:, :], start=True, stop=True).then_inc(bias_summed, 1)
            pe.wait_ge(constants_ready, 1)

            def turn_inputs(tile):
                s = tile.stream
                pe.wait_ge(norm_out_ready, tile.t + 1)
                last = nc.tensor.transpose(ps[s][:, 0:P], norm_out[:, s, :], g.ident[:, :])
                if not own:
                    if True:
                        pe.wait_ge(context_loaded[s // 2], tile.loads + 16)
                    last = nc.tensor.transpose(ps[s][:, P:2 * P], context_in[:, s, :], g.ident[:, :])
                last.then_inc(inputs_turned, 1)

            def project(tile):
                if wq is None:
                    return
                s = tile.stream
                pe.wait_ge(inputs_ready, tile.t + 1)
                pe.wait_ge(tile_done, tile.t + 1)
                nc.tensor.matmul(ps[s][:, 0:P], wqT[:, :], inputs_T[:, s, query_side, :], start=True, stop=True)
                nc.tensor.matmul(ps[s][:, 512:512 + P], wkT[:, :], inputs_T[:, s, key_side, :], start=True, stop=True)
                nc.tensor.matmul(ps[s][:, P:2 * P], inputs_T[:, s, key_side, :], wvT[:, :], start=True, stop=True).then_inc(projected, 1)

            def score(tile, turn):
                s = tile.stream
                if turn == 0:
                    if wq is None:
                        pe.wait_ge(tile_done, tile.t + 1)
                    pe.wait_ge(queries_ready, tile.t + 1)
                    pe.wait_ge(keys_ready, tile.t + 1)
                else:
                    pe.wait_ge(scores_half, tile.t + 1)
                for r in range(HEADS // GROUP):
                    rows, q = slice(32 * r, 32 * r + 32), (r + turn) % PAIR
                    last = nc.tensor.matmul(ps[s][SEQ * q:SEQ * q + SEQ, 256 * r:256 * r + 256],
                                            queries_T[rows, s, SEQ * q:SEQ * q + SEQ],
                                            keys_block[rows, s, q, :, :].rearrange("p a b -> p (a b)"),
                                            start=True, stop=True)
                last.then_inc(scores_ready if turn else scores_half, 1)

            def turn_probs(tile):
                s = tile.stream
                pe.wait_ge(probs_ready, tile.t + 1)
                for c in range(HEADS // 2):
                    last = nc.tensor.transpose(ps[s][:, P * c:P * c + P], probs[:, s, P * c:P * c + P], g.ident[:, :])
                last.then_inc(probs_turned, 1)

            def attend(tile):
                s = tile.stream
                pe.wait_ge(turned_kept, tile.t + 1)
                for c in range(HEADS // 2):
                    last = nc.tensor.matmul(ps[s][:, 36 * c:36 * c + 36], probs_T[:, s, P * c:P * c + P],
                                            values_block[:, s, :, c, :, :].rearrange("p q a b -> p q (a b)"),
                                            start=True, stop=True)
                last.then_inc(attended_raw, 1)

            def turn_attended(tile):
                s = tile.stream
                pe.wait_ge(attended_ready, tile.t + 1)
                nc.tensor.transpose(ps[s][:, 512:512 + P], attended[:, s, :], g.ident[:, :]).then_inc(attended_turned, 1)

            def put_out(tile):
                s = tile.stream
                pe.wait_ge(attended_kept, tile.t + 1)
                if bo is not None:
                    nc.tensor.matmul(ps[s][:, 640:768], g.ones_bf[0:3 * 32, :], bias_parts.rows[:, :], start=True, stop=False)
                nc.tensor.matmul(ps[s][:, 640:768], attended_T[:, s, :], woT[:, :],
                                 start=bo is None, stop=True).then_inc(output_ready, 1)

            def step(ahead, a, b, c, d):
                if wq is None:
                    if b:
                        score(b, 0)
                    if a:
                        turn_inputs(a)
                    if c:
                        turn_probs(c)
                    if b:
                        score(b, 1)
                    if d:
                        turn_attended(d)
                    if c:
                        attend(c)
                    if d:
                        put_out(d)
                    return
                if b:
                    score(b, 0)
                if a:
                    turn_inputs(a)
                if b:
                    score(b, 1)
                if d:
                    turn_attended(d)
                if c:
                    turn_probs(c)
                if a:
                    project(a)
                if c:
                    attend(c)
                if d:
                    put_out(d)

            run_tiles(pe, tiles, STREAMS, PARTS, step)

        @block.scalar
        def _(act):
            act.wait_ge(constants_ready, 1)

            def keep_inputs(tile):
                s = tile.stream
                act.wait_ge(inputs_turned, tile.t + 1)
                if wq is None:
                    nc.scalar.activation(queries_T[:, s, :], ps[s][:, 0:P], ACT.Copy, scale=scale)
                    nc.scalar.copy(inputs_T[:, s, 1, :], ps[s][:, P:2 * P]).then_inc(inputs_ready, 1)
                elif own:
                    nc.scalar.copy(inputs_T[:, s, 1, :], ps[s][:, 0:P]).then_inc(inputs_ready, 1)
                else:
                    nc.scalar.copy(inputs_T[:, s, :, :].rearrange("p a n -> p (a n)"), ps[s][:, 0:2 * P]).then_inc(inputs_ready, 1)

            def keep_queries_and_values(tile):
                s = tile.stream
                if wq is not None:
                    act.wait_ge(projected, tile.t + 1)
                    if bq is not None:
                        nc.scalar.activation(queries_T[:, s, :], ps[s][:, 0:P], ACT.Identity, bias=bq_scaled[:, 0:1], scale=scale)
                    else:
                        nc.scalar.activation(queries_T[:, s, :], ps[s][:, 0:P], ACT.Copy, scale=scale)
                for q in range(PAIR):
                    part = slice(SEQ * q, SEQ * q + SEQ)
                    got = ps[s][part, P:2 * P] if wv is not None else context_in[part, s, :]
                    for h in range(2):
                        last = nc.scalar.copy(values_block[SEQ * h:SEQ * h + SEQ, s, q, :, h, 0:HD],
                                              got.rearrange("p (c h d) -> p c h d", h=2, d=HD)[:, :, h, :])
                last.then_inc(queries_ready, 1)

            def exponentials(tile):
                s = tile.stream
                act.wait_ge(shifted_scores, tile.t + 1)
                nc.scalar.activation(probs[:, s, :], probs[:, s, :], ACT.Exp).then_inc(probs_ready, 1)

            def keep_turned(tile):
                s = tile.stream
                act.wait_ge(probs_turned, tile.t + 1)
                nc.scalar.copy(probs_T[:, s, :], ps[s]).then_inc(turned_kept, 1)

            def keep_attended(tile):
                s = tile.stream
                act.wait_ge(attended_turned, tile.t + 1)
                nc.scalar.copy(attended_T[:, s, :], ps[s][:, 512:512 + P]).then_inc(attended_kept, 1)

            def step(ahead, a, b, c, d):
                if wq is None:
                    if a:
                        keep_inputs(a)
                    if c:
                        keep_turned(c)
                    if d:
                        keep_attended(d)
                    if a:
                        keep_queries_and_values(a)
                    if b:
                        exponentials(b)
                    return
                if a:
                    keep_inputs(a)
                if d:
                    keep_attended(d)
                if c:
                    keep_turned(c)
                if a:
                    keep_queries_and_values(a)
                if b:
                    exponentials(b)

            run_tiles(act, tiles, STREAMS, PARTS, step)

        @block.vector
        def _(dve):
            nc.vector.memset(values_block[:, :, :, :, :, :].rearrange("p s q c h d -> p (s q c h d)"), 0.0).then_inc(bias_summed, 1)
            dve.wait_ge(bias_summed, 1 + (bo is not None and bv is not None))
            if bo is not None and bv is not None:
                nc.vector.tensor_tensor(out_bias[0:1, :], ps[0][0:1, 0:P], bo_row[0:1, :], ALU.add).then_inc(bias_parts.step, 1)
            elif bo is not None:
                nc.vector.tensor_copy(out_bias[0:1, :], bo_row[0:1, :]).then_inc(bias_parts.step, 1)
            if bo is not None:
                bias_parts.split(nc, dve, out_bias[0:1, :])
            if bq is not None:
                nc.vector.tensor_scalar(bq_scaled[:, :], bq_col[:, :], scale, None, ALU.mult)
            for h in range(2):
                last = nc.vector.memset(values_block[SEQ * h:SEQ * h + SEQ, :, :, :, h, HD:HD + 1].rearrange("p s q c d -> p (s q c) d"), 1.0)
            last.then_inc(constants_ready, 1)
            nc.vector.memset(negmax[:, 0, 0:1], 0.0).then_inc(tile_done, STREAMS)

            def statistics(tile):
                tile_statistics(nc, g, tile, ln)
                if key_mask is not None:
                    dve.wait_ge(mask_loaded[tile.stream // 2], tile.loads * 2 + 32)
                    s = tile.stream
                    nc.vector.tensor_scalar(mask_add[:, s, :], mask_int[:, s, :], 0.0, MASKED,
                                            ALU.is_equal, ALU.mult).then_inc(mask_ready, 1)

            def block_keys(tile):
                s = tile.stream
                dve.wait_ge(inputs_ready if wq is None else projected, tile.t + 1)
                for q in range(PAIR):
                    part = slice(SEQ * q, SEQ * q + SEQ)
                    k = inputs_T[:, s, 1, part] if wq is None else ps[s][:, 512:512 + P][:, part]
                    last = nc.vector.scalar_tensor_tensor(
                        keys_block[:, s, q, :, :], bcast(k, [(0, GROUP), (1, SEQ)]),
                        bk_col[:, 0:1] if bk is not None else 0.0,
                        bcast(g.group_mask[:, :], [(1, GROUP), (0, SEQ)]), ALU.add, ALU.mult)
                last.then_inc(keys_ready, 1)

            def shift_scores(tile):
                s = tile.stream
                dve.wait_ge(scores_ready, tile.t + 1)
                source = ps[s]
                if masked:
                    rows = mask_add[:, s, :] if key_mask is not None else mask_rows[:, :]
                    nc.vector.tensor_tensor(probs[:, s, :].rearrange("p (h k) -> p h k", k=SEQ),
                                            ps[s].rearrange("p (h k) -> p h k", k=SEQ),
                                            bcast(rows, [(0, HEADS), (1, SEQ)]), ALU.add).then_inc(masked_ready, 1)
                    dve.wait_ge(masked_ready, tile.t + 1)
                    source = probs[:, s, :]
                nc.vector.tensor_reduce(negmax[:, s, :], source.rearrange("p (h k) -> p h k", k=SEQ), X, ALU.max,
                                        negate=True).then_inc(negmax_ready, 1)
                dve.wait_ge(negmax_ready, tile.t + 1)
                nc.vector.tensor_tensor(probs[:, s, :].rearrange("p (h k) -> p h k", k=SEQ),
                                        source.rearrange("p (h k) -> p h k", k=SEQ),
                                        bcast(negmax[:, s, :], [(1, HEADS), (0, SEQ)]), ALU.add).then_inc(shifted_scores, 1)

            def divide_by_sums(tile):
                s = tile.stream
                dve.wait_ge(attended_raw, tile.t + 1)
                for q in range(PAIR):
                    part = slice(SEQ * q, SEQ * q + SEQ)
                    got = ps[s][part, 0:288].rearrange("p (c q h d) -> p c q h d", q=PAIR, h=2, d=HD + 1)
                    nc.vector.reciprocal(recip[part, s, :].rearrange("p (c h) -> p c h", h=2),
                                         got[:, :, q, :, HD]).then_inc(recip_ready, 1)
                dve.wait_ge(recip_ready, tile.t * PAIR + PAIR)
                for q in range(PAIR):
                    part = slice(SEQ * q, SEQ * q + SEQ)
                    got = ps[s][part, 0:288].rearrange("p (c q h d) -> p c q h d", q=PAIR, h=2, d=HD + 1)
                    last = nc.vector.tensor_tensor(
                        attended[part, s, :].rearrange("p (c h d) -> p c h d", h=2, d=HD), got[:, :, q, :, 0:HD],
                        bcast(recip[part, s, :], [(2, HEADS // 2), (1, 2), (0, HD)]), ALU.mult)
                last.then_inc(attended_ready, 1)

            def add_output(tile):
                s = tile.stream
                dve.wait_ge(output_ready, tile.t + 1)
                row = tile_of(g, tile.t)
                nc.vector.tensor_tensor(row, row, ps[s][:, 640:768], ALU.add).then_inc(tile_done, 1)

            def step(ahead, a, b, c, d):
                if ahead:
                    dve.wait_ge(normed_ready, ahead.t)
                    statistics(ahead)
                    tile_moments(nc, dve, ahead, ln)
                if b:
                    shift_scores(b)
                if a:
                    block_keys(a)
                if ahead:
                    norm_tile(nc, dve, g, ahead, ln, normed, normed_ready)
                if c:
                    divide_by_sums(c)
                if d:
                    add_output(d)

            first = Tile(0, 0, 0, STREAMS)
            statistics(first)
            tile_moments(nc, dve, first, ln)
            norm_tile(nc, dve, g, first, ln, normed, normed_ready)
            run_tiles(dve, tiles, STREAMS, PARTS, step)

    ph.end()
ROUND = 1.5 * 2 ** 23


def int8_ffn_phase(nc, g, weight_int8, weight_scale, bias):
    tiles = g.tiles
    groups = tiles // STREAMS
    ph = Phase(nc, "l0f")
    sb, sem = ph.sb, ph.sem
    psum = ph.psum()
    raw_int = sb("raw_int", [P, P], I32)
    raw = sb("raw", [P, P])
    weight_T = sb("weight_T", [P, P], BF16)
    scale_rows, bias_rows = sb("scale_rows", [P, P]), sb("bias_rows", [P, P])
    normed_all = sb("normed_all", [P, tiles, P])
    token_max = sb("token_max", [P, tiles])
    lane_max = sb("lane_max", [P, 1])
    all_max = sb("all_max", [1, 1])
    scale_one = sb("scale_one", [1, 1])
    x_scale = sb("x_scale", [P, 1])
    x_scale_inv = sb("x_scale_inv", [P, 1])
    lns = [LayernormState(ph, f"_{n}") for n in range(2)]
    transpose_weights(nc, ph, [(raw_int[:, :], weight_int8), (scale_rows[:, :], row_on_all(weight_scale, P)),
                               (bias_rows[:, :], row_on_all(bias, P))], [], g.ident, psum)

    normed_ready = sem("normed_ready")
    max_ready = sem("max_ready")
    weight_float = sem("weight_float")
    weight_turned = sem("weight_turned")
    lane_max_ready = sem("lane_max_ready")
    lane_max_turned = sem("lane_max_turned")
    scale_step = sem("scale_step")
    scale_spread = sem("scale_spread")
    with nc.Block() as block:
        @block.vector
        def _(dve):
            nc.vector.tensor_copy(raw[:, :], raw_int[:, :]).then_inc(weight_float, 1)
            dve.wait_ge(weight_turned, 1)
            nc.vector.tensor_copy(weight_T[:, :], psum[:, 0, 0:P])
            def norm(i, n):
                dve.wait_ge(lns[n].rstd_ready, i + 1)
                t0 = (i * 2 + n) * STREAMS
                for s in range(STREAMS):
                    nc.vector.tensor_scalar(normed_all[:, bass.ds(t0 + s, 1), :].rearrange("p a d -> p (a d)"), tile_of(g, t0 + s),
                                            lns[n].mean_var[:, s, 0:1], lns[n].rstd[:, s:s + 1], ALU.subtract,
                                            ALU.mult).then_inc(normed_ready, 1)
                dve.wait_ge(normed_ready, t0 + STREAMS)
                nc.vector.tensor_reduce(token_max[:, bass.ds(t0, STREAMS)], normed_all[:, bass.ds(t0, STREAMS), :], X, ALU.max,
                                        apply_absolute_value=True).then_inc(max_ready, 1)

            norm_groups(nc, dve, g, lns, norm)
            dve.wait_ge(max_ready, groups)
            nc.vector.tensor_reduce(lane_max[:, :], token_max[:, :], X, ALU.max).then_inc(lane_max_ready, 1)
            dve.wait_ge(lane_max_turned, 1)
            nc.vector.tensor_reduce(all_max[0:1, :], psum[0:1, 1, 0:P], X, ALU.max).then_inc(scale_step, 1)
            dve.wait_ge(scale_step, 1)
            nc.vector.tensor_scalar(scale_one[0:1, :], all_max[0:1, :], 1.0 / 127.0, 1e-5, ALU.mult, ALU.max).then_inc(scale_step, 1)
            dve.wait_ge(scale_spread, 1)
            nc.vector.tensor_copy(x_scale[:, :], psum[:, 2, 0:1]).then_inc(scale_step, 1)
            dve.wait_ge(scale_step, 3)
            nc.vector.reciprocal(x_scale_inv[:, :], x_scale[:, :])

        @block.gpsimd
        def _(pool):
            with pool.Fori(0, groups // 2) as i:
                for n in range(2):
                    group_rstd(nc, pool, g, i, lns[n])

        @block.tensor
        def _(pe):
            pe.wait_ge(weight_float, 1)
            nc.tensor.transpose(psum[:, 0, 0:P], raw[:, :], g.ident[:, :]).then_inc(weight_turned, 1)
            pe.wait_ge(lane_max_ready, 1)
            nc.tensor.transpose(psum[0:1, 1, 0:P], lane_max[:, 0:1], g.ident[:, :]).then_inc(lane_max_turned, 1)
            pe.wait_ge(scale_step, 2)
            nc.tensor.matmul(psum[:, 2, 0:1], g.ones_full[0:1, :], scale_one[0:1, 0:1], start=True, stop=True).then_inc(scale_spread, 1)

    width = STREAMS * P
    clipped = sb("clipped", [P, 2, width])
    shifted = sb("shifted", [P, 2, width])
    ints = sb("ints", [P, 2, width], BF16)
    ints_T = sb("ints_T", [P, 2, width], BF16)
    product = sb("product", [P, 2, width])
    biased = sb("biased", [P, 2, width])
    clipped_ready = sem("clipped_ready")
    shifted_ready = sem("shifted_ready")
    ints_ready = sem("ints_ready")
    ints_turned = sem("ints_turned")
    ints_kept = sem("ints_kept")
    dot_ready = sem("dot_ready")
    product_ready = sem("product_ready")
    biased_ready = sem("biased_ready")
    turn = [psum[:, 2 * b, 0:width // 2].bitcast(BF16) for b in range(2)]
    dot = [psum[:, 2 * b + 1, :] for b in range(2)]
    with nc.Block() as block:
        @block.vector
        def _(dve):
            with dve.Fori(0, groups // 2) as i:
                n0 = dve.snap(i * 2)
                for b in range(2):
                    t0 = (n0 + b) * STREAMS
                    source = normed_all[:, bass.ds(t0, STREAMS), :].rearrange("p t d -> p (t d)")
                    nc.vector.tensor_scalar(clipped[:, b, :], source, x_scale_inv[:, 0:1], 127.0, ALU.mult,
                                            ALU.min).then_inc(clipped_ready, 1)
                    dve.wait_ge(clipped_ready, n0 + (b + 1))
                    nc.vector.tensor_scalar(shifted[:, b, :], clipped[:, b, :], -128.0, ROUND, ALU.max,
                                            ALU.add).then_inc(shifted_ready, 1)
                    dve.wait_ge(shifted_ready, n0 + (b + 1))
                    nc.vector.tensor_scalar(ints[:, b, :], shifted[:, b, :], -ROUND, None, ALU.add).then_inc(ints_ready, 1)
                for b in range(2):
                    t0 = (n0 + b) * STREAMS
                    dve.wait_ge(dot_ready, n0 + (b + 1))
                    nc.vector.scalar_tensor_tensor(product[:, b, :].rearrange("p (t d) -> p t d", d=P),
                                                   dot[b].rearrange("p (t d) -> p t d", d=P), x_scale[:, 0:1],
                                                   bcast(scale_rows[:, :], [(0, STREAMS), (1, P)]), ALU.mult,
                                                   ALU.mult).then_inc(product_ready, 1)
                    dve.wait_ge(product_ready, n0 + (b + 1))
                    nc.vector.tensor_tensor(biased[:, b, :].rearrange("p (t d) -> p t d", d=P),
                                            product[:, b, :].rearrange("p (t d) -> p t d", d=P),
                                            bcast(bias_rows[:, :], [(0, STREAMS), (1, P)]), ALU.add).then_inc(biased_ready, 1)
                    dve.wait_ge(biased_ready, n0 + (b + 1))
                    row = g.x[:, bass.ds(t0, STREAMS), :].rearrange("p t d -> p (t d)")
                    nc.vector.tensor_tensor(row, row, biased[:, b, :], ALU.add)

        @block.tensor
        def _(pe):
            with pe.Fori(0, groups // 2) as i:
                n0 = pe.snap(i * 2)
                for b in range(2):
                    pe.wait_ge(ints_ready, n0 + (b + 1))
                    for s in range(STREAMS):
                        last = nc.tensor.transpose(turn[b][:, P * s:P * s + P], ints[:, b, P * s:P * s + P], g.ident_bf[:, :])
                    last.then_inc(ints_turned, 1)
                for b in range(2):
                    pe.wait_ge(ints_kept, n0 + (b + 1))
                    for s in range(STREAMS):
                        last = nc.tensor.matmul(dot[b][:, P * s:P * s + P], ints_T[:, b, P * s:P * s + P], weight_T[:, :],
                                                start=True, stop=True)
                    last.then_inc(dot_ready, 1)

        @block.scalar
        def _(act):
            with act.Fori(0, groups // 2) as i:
                n0 = act.snap(i * 2)
                for b in range(2):
                    act.wait_ge(ints_turned, n0 + (b + 1))
                    nc.scalar.copy(ints_T[:, b, :], turn[b]).then_inc(ints_kept, 1)

    ph.end()


def ternary_ffn_phase(nc, g, norm1_w, w1, act_scale, act_bias, norm2_w, w2):
    tiles = g.tiles
    groups = tiles // STREAMS
    hidden = w1.shape[0]
    chunks = hidden // P
    ph = Phase(nc, "l1f")
    sb, sem = ph.sb, ph.sem
    psum = ph.psum()
    raw = sb("raw", [P, 2, hidden])
    rounded_w = sb("rounded_w", [P, 2, hidden])
    ternary = sb("ternary", [P, 2, hidden], BF16)
    w1T = sb("w1T", [P, hidden], BF16)
    w2T = sb("w2T", [P, chunks, P], BF16)
    norm1_rows, norm2_rows = sb("norm1_rows", [P, P]), sb("norm2_rows", [P, hidden])
    act_scale_col, act_bias_col = sb("act_scale", [P, 1]), sb("act_bias", [P, 1])
    weight_sum = sb("weight_sum", [P, 2])
    weight_mean = sb("weight_mean", [P, 2])
    weight_mean_inv = sb("weight_mean_inv", [P, 2])
    transpose_weights(nc, ph, [(raw[:, 0, :].rearrange("p (c d) -> p c d", d=P), w1.rearrange("(c p) d -> p c d", p=P)),
                               (raw[:, 1, :], w2), (norm1_rows[:, :], row_on_all(norm1_w, P)),
                               (norm2_rows[:, :], row_on_all(norm2_w, hidden)), (act_scale_col[:, :], row_on_all(act_scale, 1)),
                               (act_bias_col[:, :], row_on_all(act_bias, 1))], [], g.ident, psum)
    weight_step = sem("weight_step")
    weight_summed = sem("weight_summed")
    ternary_turned = sem("ternary_turned")
    with nc.Block() as block:
        @block.vector
        def _(dve):
            nc.vector.tensor_reduce(weight_sum[:, :], raw[:, :, :], X, ALU.add, apply_absolute_value=True).then_inc(weight_step, 1)
            dve.wait_ge(weight_summed, 1)
            nc.vector.tensor_scalar(weight_mean[:, :], psum[:, 0, 0:2], 1.0 / (hidden * P), 1e-5, ALU.mult, ALU.max).then_inc(weight_step, 1)
            dve.wait_ge(weight_step, 2)
            nc.vector.reciprocal(weight_mean_inv[:, :], weight_mean[:, :]).then_inc(weight_step, 1)
            dve.wait_ge(weight_step, 3)
            for m in range(2):
                nc.vector.tensor_scalar(rounded_w[:, m, :], raw[:, m, :], weight_mean_inv[:, m:m + 1], ROUND, ALU.mult,
                                        ALU.add).then_inc(weight_step, 1)
            dve.wait_ge(weight_step, 5)
            nc.vector.tensor_scalar(raw[:, :, :], rounded_w[:, :, :], -ROUND, 1.0, ALU.add, ALU.min).then_inc(weight_step, 1)
            dve.wait_ge(weight_step, 6)
            nc.vector.tensor_scalar(ternary[:, :, :], raw[:, :, :], -1.0, None, ALU.max).then_inc(weight_step, 1)
            dve.wait_ge(ternary_turned, 1)
            nc.vector.tensor_copy(w1T[:, :], psum[:, 1, 0:hidden // 2].bitcast(BF16))
            nc.vector.tensor_copy(w2T[:, :, :].rearrange("p c d -> p (c d)"), psum[:, 2, 0:hidden // 2].bitcast(BF16))

        @block.tensor
        def _(pe):
            pe.wait_ge(weight_step, 1)
            nc.tensor.matmul(psum[:, 0, 0:2], g.ones_full[:, :], weight_sum[:, :], start=True, stop=True).then_inc(weight_summed, 1)
            pe.wait_ge(weight_step, 7)
            for m in range(2):
                for c in range(chunks):
                    last = nc.tensor.transpose(psum[:, 1 + m, 0:hidden // 2].bitcast(BF16)[:, P * c:P * c + P],
                                               ternary[:, m, P * c:P * c + P], g.ident_bf[:, :])
            last.then_inc(ternary_turned, 1)

    B = 2
    width = STREAMS * P
    ln = [LayernormState(ph, f"_{b}") for b in range(B)]
    normed = sb("normed", [P, B, STREAMS, P])
    squares = sb("squares", [P, B, STREAMS, P])
    square_sum = sb("square_sum", [P, B, STREAMS])
    mean_square = sb("mean_square", [P, B, STREAMS])
    rms_inv = sb("rms_inv", [P, B, STREAMS])
    rms_normed = sb("rms_normed", [P, B, STREAMS, P])
    top = sb("top", [P, B, STREAMS])
    top_kept = sb("top_kept", [P, B, STREAMS])
    top_inv = sb("top_inv", [P, B, STREAMS])
    to_int = sb("to_int", [P, B, STREAMS])
    from_int = sb("from_int", [P, B, STREAMS])
    rounded = sb("rounded", [P, B, STREAMS, P])
    lowered = sb("lowered", [P, B, STREAMS, P])
    ints = sb("ints", [P, B, width], BF16)
    ints_T = sb("ints_T", [P, B, width], BF16)
    act = sb("act", [P, B, STREAMS, hidden])
    work = sb("work", [P, B, STREAMS, hidden])
    square_sum2 = sb("square_sum2", [P, B, STREAMS])
    mean_square2 = sb("mean_square2", [P, B, STREAMS])
    rms_inv2 = sb("rms_inv2", [P, B, STREAMS])
    top2 = sb("top2", [P, B, STREAMS])
    top_kept2 = sb("top_kept2", [P, B, STREAMS])
    top_inv2 = sb("top_inv2", [P, B, STREAMS])
    to_int2 = sb("to_int2", [P, B, STREAMS])
    from_int2 = sb("from_int2", [P, B, STREAMS])
    hidden_ints = sb("hidden_ints", [P, B, STREAMS, hidden], BF16)
    hidden_T = sb("hidden_T", [P, B, STREAMS, hidden], BF16)
    normed_ready = sem("normed_ready")
    squares_ready = sem("squares_ready")
    mean_square_ready = sem("mean_square_ready")
    rms_ready = sem("rms_ready")
    rms_normed_ready = sem("rms_normed_ready")
    top_ready = sem("top_ready")
    top_kept_ready = sem("top_kept_ready")
    top_inv_ready = sem("top_inv_ready")
    to_int_ready = sem("to_int_ready")
    rounded_ready = sem("rounded_ready")
    lowered_ready = sem("lowered_ready")
    ints_ready = sem("ints_ready")
    ints_turned = sem("ints_turned")
    ints_kept = sem("ints_kept")
    hidden_ready = sem("hidden_ready")
    relu_ready = sem("relu_ready")
    squared_ready = sem("squared_ready")
    activated = sem("activated")
    hidden_squares_ready = sem("hidden_squares_ready")
    mean_square2_ready = sem("mean_square2_ready")
    rms2_ready = sem("rms2_ready")
    hidden_normed = sem("hidden_normed")
    top2_ready = sem("top2_ready")
    top_kept2_ready = sem("top_kept2_ready")
    top_inv2_ready = sem("top_inv2_ready")
    to_int2_ready = sem("to_int2_ready")
    hidden_rounded = sem("hidden_rounded")
    hidden_lowered = sem("hidden_lowered")
    hidden_ints_ready = sem("hidden_ints_ready")
    hidden_turned = sem("hidden_turned")
    hidden_kept = sem("hidden_kept")
    output_ready = sem("output_ready")
    streams, parities = range(STREAMS), range(B)
    rounds = groups // B

    def scales(dve, n, b, top, kept, inv, to_int, from_int, which, weight, ready):
        top_ready, kept_ready, inv_ready, scale_ready = ready
        dve.wait_ge(top_ready, which)
        nc.vector.tensor_scalar(kept[:, b, :], top[:, b, :], 1e-5, None, ALU.max).then_inc(kept_ready, 1)
        dve.wait_ge(kept_ready, n + (b + 1))
        nc.vector.reciprocal(inv[:, b, :], kept[:, b, :]).then_inc(inv_ready, 1)
        nc.vector.tensor_scalar(from_int[:, b, :], kept[:, b, :], 1.0 / 127.0, weight, ALU.mult, ALU.mult)
        dve.wait_ge(inv_ready, n + (b + 1))
        nc.vector.tensor_scalar(to_int[:, b, :], inv[:, b, :], 127.0, None, ALU.mult).then_inc(scale_ready, 1)

    with nc.Block() as block:
        @block.vector
        def _(dve):
            def normalize(i, c0, k0):
                for b in parities:
                    group_statistics(nc, dve, g, i, c0, ln[b], k0 + b * STREAMS)
                for b in parities:
                    dve.wait_ge(ln[b].rstd_ready, i + 1)
                    for s in streams:
                        last = nc.vector.tensor_scalar(normed[:, b, s, :], tile_of(g, k0 + (b * STREAMS + s)), ln[b].mean_var[:, s, 0:1],
                                                       ln[b].rstd[:, s:s + 1], ALU.subtract, ALU.mult)
                    last.then_inc(normed_ready, 1)

            def groups_at(i, n0, c0, k0, ahead):
                for b in parities:
                    dve.wait_ge(squares_ready, n0 + (b + 1))
                    nc.vector.tensor_scalar(mean_square[:, b, :], square_sum[:, b, :], 1.0 / P, 1e-8, ALU.mult,
                                            ALU.add).then_inc(mean_square_ready, 1)
                for b in parities:
                    dve.wait_ge(rms_ready, n0 + (b + 1))
                    for s in streams:
                        last = nc.vector.scalar_tensor_tensor(rms_normed[:, b, s, :], normed[:, b, s, :], rms_inv[:, b, s:s + 1],
                                                              norm1_rows[:, :], ALU.mult, ALU.mult)
                    last.then_inc(rms_normed_ready, 1)
                    dve.wait_ge(rms_normed_ready, n0 + (b + 1))
                    nc.vector.tensor_reduce(top[:, b, :], rms_normed[:, b, :, :], X, ALU.max, apply_absolute_value=True).then_inc(top_ready, 1)
                    scales(dve, n0, b, top, top_kept, top_inv, to_int, from_int, n0 + (b + 1), weight_mean[:, 0:1],
                           (top_ready, top_kept_ready, top_inv_ready, to_int_ready))
                    dve.wait_ge(to_int_ready, n0 + (b + 1))
                    for s in streams:
                        last = nc.vector.tensor_scalar(rounded[:, b, s, :], rms_normed[:, b, s, :], to_int[:, b, s:s + 1], ROUND,
                                                       ALU.mult, ALU.add)
                    last.then_inc(rounded_ready, 1)
                    dve.wait_ge(rounded_ready, n0 + (b + 1))
                    nc.vector.tensor_scalar(lowered[:, b, :, :], rounded[:, b, :, :], -ROUND, 127.0, ALU.add, ALU.min).then_inc(lowered_ready, 1)
                    dve.wait_ge(lowered_ready, n0 + (b + 1))
                    nc.vector.tensor_scalar(ints[:, b, :], lowered[:, b, :, :].rearrange("p s d -> p (s d)"), -128.0, None,
                                            ALU.max).then_inc(ints_ready, 1)
                if ahead:
                    normalize(i + 1, c0 + STREAMS, k0 + B * STREAMS)
                for b in parities:
                    for s in streams:
                        dve.wait_ge(hidden_ready, k0 + (b * STREAMS + s + 1))
                        nc.vector.tensor_scalar(act[:, b, s, :], psum[:, STREAMS * b + s, :], from_int[:, b, s:s + 1], 0.0, ALU.mult,
                                                ALU.max).then_inc(relu_ready, 1)
                for b in parities:
                    dve.wait_ge(hidden_squares_ready, n0 + (b + 1))
                    nc.vector.tensor_scalar(mean_square2[:, b, :], square_sum2[:, b, :], 1.0 / hidden, 1e-8, ALU.mult,
                                            ALU.add).then_inc(mean_square2_ready, 1)
                for b in parities:
                    dve.wait_ge(rms2_ready, n0 + (b + 1))
                    for s in streams:
                        last = nc.vector.scalar_tensor_tensor(work[:, b, s, :], act[:, b, s, :], rms_inv2[:, b, s:s + 1],
                                                              norm2_rows[:, :], ALU.mult, ALU.mult)
                    last.then_inc(hidden_normed, 1)
                    dve.wait_ge(hidden_normed, n0 + (b + 1))
                    nc.vector.tensor_reduce(top2[:, b, :], work[:, b, :, :], X, ALU.max, apply_absolute_value=True).then_inc(top2_ready, 1)
                    scales(dve, n0, b, top2, top_kept2, top_inv2, to_int2, from_int2, n0 + (b + 1), weight_mean[:, 1:2],
                           (top2_ready, top_kept2_ready, top_inv2_ready, to_int2_ready))
                    dve.wait_ge(to_int2_ready, n0 + (b + 1))
                    for s in streams:
                        last = nc.vector.tensor_scalar(act[:, b, s, :], work[:, b, s, :], to_int2[:, b, s:s + 1], ROUND,
                                                       ALU.mult, ALU.add)
                    last.then_inc(hidden_rounded, 1)
                    dve.wait_ge(hidden_rounded, n0 + (b + 1))
                    nc.vector.tensor_scalar(work[:, b, :, :], act[:, b, :, :], -ROUND, 127.0, ALU.add, ALU.min).then_inc(hidden_lowered, 1)
                    dve.wait_ge(hidden_lowered, n0 + (b + 1))
                    nc.vector.tensor_scalar(hidden_ints[:, b, :, :], work[:, b, :, :], -128.0, None, ALU.max).then_inc(hidden_ints_ready, 1)
                for b in parities:
                    for s in streams:
                        dve.wait_ge(output_ready, k0 + (b * STREAMS + s + 1))
                        row = tile_of(g, k0 + (b * STREAMS + s))
                        nc.vector.scalar_tensor_tensor(row, psum[:, STREAMS * b + s, 256:256 + P], from_int2[:, b, s:s + 1], row,
                                                       ALU.mult, ALU.add)

            normalize(0, 0, 0)
            with dve.Fori(0, rounds - 1) as i:
                groups_at(i, dve.snap(i * B), dve.snap(i * STREAMS), dve.snap(i * (B * STREAMS)), True)
            groups_at(rounds - 1, (rounds - 1) * B, (rounds - 1) * STREAMS, (rounds - 1) * B * STREAMS, False)

        @block.gpsimd
        def _(pool):
            def rstd(i):
                for b in parities:
                    group_rstd(nc, pool, g, i, ln[b])

            def groups_at(i, n0, ahead):
                for b in parities:
                    pool.wait_ge(mean_square_ready, n0 + (b + 1))
                    nc.gpsimd.tensor_tensor(rms_inv[:, b, :], mean_square[:, b, :], g.minus_half[:, 0:STREAMS], ALU.pow).then_inc(rms_ready, 1)
                if ahead:
                    rstd(i + 1)
                for b in parities:
                    pool.wait_ge(mean_square2_ready, n0 + (b + 1))
                    nc.gpsimd.tensor_tensor(rms_inv2[:, b, :], mean_square2[:, b, :], g.minus_half[:, 0:STREAMS], ALU.pow).then_inc(rms2_ready, 1)

            rstd(0)
            with pool.Fori(0, rounds - 1) as i:
                groups_at(i, pool.snap(i * B), True)
            groups_at(rounds - 1, (rounds - 1) * B, False)

        @block.tensor
        def _(pe):
            with pe.Fori(0, groups // B) as i:
                n0 = pe.snap(i * B)
                k0 = pe.snap(i * (B * STREAMS))
                for b in parities:
                    turned = psum[:, STREAMS * b, 0:width // 2].bitcast(BF16)
                    pe.wait_ge(ints_ready, n0 + (b + 1))
                    for s in streams:
                        last = nc.tensor.transpose(turned[:, P * s:P * s + P], ints[:, b, P * s:P * s + P], g.ident_bf[:, :])
                    last.then_inc(ints_turned, 1)
                for b in parities:
                    pe.wait_ge(ints_kept, n0 + (b + 1))
                    for s in streams:
                        nc.tensor.matmul(psum[:, STREAMS * b + s, :], ints_T[:, b, P * s:P * s + P], w1T[:, :],
                                         start=True, stop=True).then_inc(hidden_ready, 1)
                for b in parities:
                    pe.wait_ge(hidden_ints_ready, n0 + (b + 1))
                    for s in streams:
                        turned = psum[:, STREAMS * b + s, 0:hidden // 2].bitcast(BF16)
                        for c in range(chunks):
                            last = nc.tensor.transpose(turned[:, P * c:P * c + P], hidden_ints[:, b, s, P * c:P * c + P], g.ident_bf[:, :])
                        last.then_inc(hidden_turned, 1)
                for b in parities:
                    for s in streams:
                        pe.wait_ge(hidden_kept, k0 + (b * STREAMS + s + 1))
                        for c in range(chunks):
                            last = nc.tensor.matmul(psum[:, STREAMS * b + s, 256:256 + P], hidden_T[:, b, s, P * c:P * c + P], w2T[:, c, :],
                                                    start=c == 0, stop=c == chunks - 1)
                        last.then_inc(output_ready, 1)

        @block.scalar
        def _(acte):
            with acte.Fori(0, groups // B) as i:
                n0 = acte.snap(i * B)
                k0 = acte.snap(i * (B * STREAMS))
                for b in parities:
                    acte.wait_ge(normed_ready, n0 + (b + 1))
                    for s in streams:
                        last = nc.scalar.activation(squares[:, b, s, :], normed[:, b, s, :], ACT.Square, accum_out=square_sum[:, b, s:s + 1])
                    last.then_inc(squares_ready, 1)
                for b in parities:
                    acte.wait_ge(ints_turned, n0 + (b + 1))
                    nc.scalar.copy(ints_T[:, b, :], psum[:, STREAMS * b, 0:width // 2].bitcast(BF16)).then_inc(ints_kept, 1)
                for b in parities:
                    for s in streams:
                        acte.wait_ge(relu_ready, k0 + (b * STREAMS + s + 1))
                        nc.scalar.activation(work[:, b, s, :], act[:, b, s, :], ACT.Square).then_inc(squared_ready, 1)
                for b in parities:
                    acte.wait_ge(squared_ready, k0 + (b * STREAMS + STREAMS))
                    for s in streams:
                        nc.scalar.activation(act[:, b, s, :], work[:, b, s, :], ACT.Identity, bias=act_bias_col[:, 0:1],
                                             scale=act_scale_col[:, 0:1]).then_inc(activated, 1)
                for b in parities:
                    acte.wait_ge(activated, k0 + (b * STREAMS + STREAMS))
                    for s in streams:
                        last = nc.scalar.activation(work[:, b, s, :], act[:, b, s, :], ACT.Square, accum_out=square_sum2[:, b, s:s + 1])
                    last.then_inc(hidden_squares_ready, 1)
                for b in parities:
                    for s in streams:
                        acte.wait_ge(hidden_turned, k0 + (b * STREAMS + s + 1))
                        nc.scalar.copy(hidden_T[:, b, s, :], psum[:, STREAMS * b + s, 0:hidden // 2].bitcast(BF16)).then_inc(hidden_kept, 1)

    ph.end()


def takes_the_wait(nc, g, column):
    nc.tensor.matmul(column, g.ones_full[0:1, :], g.ones_full[0:1, 0:1], start=True, stop=True)


def box_attention_phase(nc, g, boxes, context, wq, bq, wk, bk, wv, bv, wo, bo, wg, bg, constants):
    tiles = g.tiles
    wide = wq.shape[0]
    heads_dim = wide // HEADS
    pairs = HEADS // 2
    scale = heads_dim ** -0.5
    kinds, trigs = 4, 2
    features = kinds * trigs
    keys_at_once = P // features
    blocks = SEQ // keys_at_once
    turns = 100.0 / (2 * 3.141592653589793)
    T = 2
    ph = Phase(nc, "l2x")
    sb, sem = ph.sb, ph.sem
    psum = ph.psum()
    ps = [psum[:, 4 * b:4 * b + 4, :].rearrange("p b n -> p (b n)") for b in range(T)]
    wqT, wkT, wvT = sb("wqT", [P, wide]), sb("wkT", [P, wide]), sb("wvT", [P, wide])
    woT = sb("woT", [P, pairs, P])
    raw = sb("raw", [P, 4, wide])
    bq_cols, bk_cols, bv_cols = sb("bq", [P, pairs]), sb("bk", [P, pairs]), sb("bv", [P, pairs])
    bo_row, out_bias = sb("bo", [1, P]), sb("out_bias", [1, P])
    boxes_all = sb("boxes_all", [P, tiles, 4])
    box_features = sb("box_features", [P, tiles, 4, kinds])
    gate_cols = sb("gate_cols", [P, HEADS])
    gate_weights = sb("gate_weights", [P, HEADS, keys_at_once])
    bg_row, gate_bias = sb("bg", [1, HEADS]), sb("gate_bias", [1, HEADS * keys_at_once])
    same_key, block_of, diagonal, floor_phase = (sb("same_key", [P, P]), sb("block_of", [P, PAIR * blocks]),
                                                 sb("diagonal", [P, keys_at_once]), sb("floor_phase", [P, 2]))
    loads = [(raw[:, m, :].rearrange("p (c d) -> p c d", d=P), w.rearrange("(c p) d -> p c d", p=P)) for m, w in enumerate((wq, wk, wv))]
    loads += [(raw[:, 3, :], wo)]
    loads += [(t[:, :], bass.AP(b.tensor, b.offset, [[1, P], [P, pairs]])) for t, b in ((bq_cols, bq), (bk_cols, bk), (bv_cols, bv))]
    loads += [(bo_row[:, :], row_on_all(bo, P, 1)), (bg_row[:, :], row_on_all(bg, HEADS, 1))]
    loads += [(boxes_all[:, :, :], boxes)]
    loads += [(gate_cols[features * k:features * (k + 1), :], wg.rearrange("h d -> d h")) for k in range(keys_at_once)]
    loads += [(same_key[:, :], constants["same_key"]), (block_of[:, :], constants["block_of"]),
              (diagonal[:, :], constants["diagonal"]), (floor_phase[:, :], constants["floor_phase"])]
    turned = [(dst[:, P * c:P * c + P], raw[:, m, P * c:P * c + P]) for m, dst in enumerate((wqT, wkT, wvT)) for c in range(pairs)]
    turned += [(woT[:, c, :], raw[:, 3, P * c:P * c + P]) for c in range(pairs)]
    transpose_weights(nc, ph, loads, turned, g.ident, psum)

    prepare = sem("prepare")
    bias_summed = sem("bias_summed")
    gate_bias_parts = ExactParts(ph, "gate_bias", HEADS * keys_at_once)
    out_bias_parts = ExactParts(ph, "out_bias", P)
    with nc.Block() as block:
        @block.vector
        def _(dve):
            size, center = box_features[:, :, 0, 2:4], box_features[:, :, 0, 0:2]
            nc.vector.memset(box_features[:, :, 1:4, :].rearrange("p t m k -> p t (m k)"), 1.0).then_inc(prepare, 1)
            nc.vector.tensor_tensor(center, boxes_all[:, :, 0:2], boxes_all[:, :, 2:4], ALU.add)
            nc.vector.tensor_tensor(size, boxes_all[:, :, 2:4], boxes_all[:, :, 0:2], ALU.subtract).then_inc(prepare, 1)
            dve.wait_ge(prepare, 2)
            nc.vector.tensor_scalar(size, size, 1.0, None, ALU.add)
            nc.vector.tensor_scalar(center, center, 0.5, None, ALU.mult).then_inc(prepare, 1)
            dve.wait_ge(prepare, 3)
            nc.vector.reciprocal(box_features[:, :, 1, 0:2], size)
            nc.vector.memset(box_features[:, :, 2, 2:4], 0.0)
            nc.vector.tensor_copy(box_features[:, :, 2, 0:2], center).then_inc(prepare, 1)
            dve.wait_ge(prepare, 4)
            nc.vector.tensor_copy(box_features[:, :, 3, 2:4], box_features[:, :, 1, 0:2])
            nc.vector.tensor_tensor(gate_weights[:, :, :], bcast(gate_cols[:, :], [(1, HEADS), (0, keys_at_once)]),
                                    bcast(diagonal[:, :], [(0, HEADS), (1, keys_at_once)]), ALU.mult)
            nc.vector.tensor_copy(gate_bias[:, :].rearrange("p (h k) -> p h k", k=keys_at_once),
                                  bcast(bg_row[:, :], [(1, HEADS), (0, keys_at_once)])).then_inc(gate_bias_parts.step, 1)
            gate_bias_parts.split(nc, dve, gate_bias[0:1, :])
            dve.wait_ge(bias_summed, 1)
            nc.vector.tensor_tensor(out_bias[:, :], psum[0:1, 0, 0:P], bo_row[:, :], ALU.add).then_inc(out_bias_parts.step, 1)
            out_bias_parts.split(nc, dve, out_bias[0:1, :])

        @block.tensor
        def _(pe):
            for c in range(pairs):
                last = nc.tensor.matmul(psum[0:1, 0, 0:P], bv_cols[:, c:c + 1], woT[:, c, :], start=c == 0, stop=c == pairs - 1)
            last.then_inc(bias_summed, 1)

    ln = LayernormState(ph, n=1)
    normed = sb("normed", [P, T, P])
    context_in = sb("context_in", [P, T, P])
    inputs_T = sb("inputs_T", [P, T, 2, P])
    query_boxes = sb("query_boxes", [P, T, 2, P])
    key_boxes = sb("key_boxes", [P, T, 2, P])
    spread = sb("spread", [P, T, 2 * P + 2 * PAIR * blocks])
    relation = sb("relation", [P, T, 2, blocks * P])
    embedding = sb("embedding", [P, T, blocks * P])
    queries_T = sb("queries_T", [P, T, pairs, P])
    keys_T = sb("keys_T", [P, T, pairs, P])
    values = sb("values", [P, T, PAIR, pairs, heads_dim])
    probs = sb("probs", [P, T, HEADS * SEQ])
    gated = sb("gated", [P, T, HEADS * SEQ])
    probs_T = sb("probs_T", [P, T, pairs, P])
    attended_T = sb("attended_T", [P, T, pairs, P])
    negmax = sb("negmax", [P, T, HEADS])
    total = sb("total", [P, T, HEADS])
    recip = sb("recip", [P, T, HEADS])
    context_loaded = [sem(f"context_loaded_{b}") for b in range(T)]
    tile_done = sem("tile_done")
    normed_ready = sem("normed_ready")
    boxes_spread = sem("boxes_spread")
    inputs_turned = sem("inputs_turned")
    inputs_ready = sem("inputs_ready")
    spread_ready = sem("spread_ready")
    difference_ready = sem("difference_ready")
    scaled_once = sem("scaled_once")
    relation_ready = sem("relation_ready")
    magnitude_ready = sem("magnitude_ready")
    floored_ready = sem("floored_ready")
    logs_ready = sem("logs_ready")
    turns_ready = sem("turns_ready")
    rounded_ready = sem("rounded_ready")
    fraction_ready = sem("fraction_ready")
    embedding_ready = sem("embedding_ready")
    queries_projected = sem("queries_projected")
    keys_projected = sem("keys_projected")
    queries_ready = sem("queries_ready")
    keys_ready = sem("keys_ready")
    values_projected = sem("values_projected")
    values_ready = sem("values_ready")
    gates_ready = sem("gates_ready")
    scores_half = sem("scores_half")
    scores_ready = sem("scores_ready")
    negmax_ready = sem("negmax_ready")
    shifted_scores = sem("shifted_scores")
    exp_ready = sem("exp_ready")
    gated_ready = sem("gated_ready")
    total_ready = sem("total_ready")
    recip_ready = sem("recip_ready")
    probs_ready = sem("probs_ready")
    probs_turned = sem("probs_turned")
    probs_kept = sem("probs_kept")
    attended_ready = sem("attended_ready")
    attended_kept = sem("attended_kept")
    output_ready = sem("output_ready")
    parts = (1, 0, -1)
    with nc.Block() as block:
        @block.sync
        def _(sp):
            def load(tile):
                sp.dma_start(context_in[:, tile.stream, :],
                             context[bass.ds(tile.t, 1), :, :].rearrange("o p d -> p (o d)")).then_inc(context_loaded[tile.stream], 16)

            for b in range(T):
                load(Tile(0, b, 0, T))
            with sp.Fori(0, tiles // T - 1) as i:
                t0 = sp.snap(i * T)
                for b in range(T):
                    sp.wait_ge(inputs_turned, t0 + (b + 1))
                    load(Tile(t0, T + b, 0, T))

        @block.gpsimd
        def _(pool):
            def spread_boxes(tile):
                b = tile.stream
                f = box_features[:, bass.ds(tile.t, 1), :, :].rearrange("p a m k -> p (a m k)")
                nc.gpsimd.tensor_copy(query_boxes[:, b, :, :].rearrange("p m (r k) -> p m r k", k=kinds),
                                      bcast(f[:, 0:2 * kinds], [(kinds, 2), (0, P // kinds), (1, kinds)]))
                nc.gpsimd.tensor_tensor(key_boxes[:, b, :, :].rearrange("p m (r k) -> p m r k", k=kinds),
                                        bcast(f[:, 2 * kinds:4 * kinds], [(kinds, 2), (0, P // kinds), (1, kinds)]),
                                        bcast(same_key[:, :], [(0, 2), (kinds, P // kinds), (1, kinds)]), ALU.mult).then_inc(boxes_spread, 1)

            def relate(tile):
                b = tile.stream
                pool.wait_ge(spread_ready, tile.t + 1)
                nc.gpsimd.tensor_tensor(relation[:, b, 0, :].rearrange("p (c s n) -> p c s n", s=PAIR, n=SEQ),
                                        bcast(spread[:, b, 0:P], [(0, blocks), (SEQ, PAIR), (1, SEQ)]),
                                        bcast(spread[:, b, 2 * P:2 * P + 8], [(1, blocks), (blocks, PAIR), (0, SEQ)]),
                                        ALU.subtract).then_inc(difference_ready, 1)
                pool.wait_ge(difference_ready, tile.t + 1)
                nc.gpsimd.tensor_tensor(relation[:, b, 1, :].rearrange("p (c n) -> p c n", n=P),
                                        relation[:, b, 0, :].rearrange("p (c n) -> p c n", n=P),
                                        bcast(spread[:, b, P:2 * P], [(0, blocks), (1, P)]), ALU.mult).then_inc(scaled_once, 1)
                pool.wait_ge(scaled_once, tile.t + 1)
                nc.gpsimd.tensor_tensor(relation[:, b, 0, :].rearrange("p (c s n) -> p c s n", s=PAIR, n=SEQ),
                                        relation[:, b, 1, :].rearrange("p (c s n) -> p c s n", s=PAIR, n=SEQ),
                                        bcast(spread[:, b, 2 * P + 8:2 * P + 16], [(1, blocks), (blocks, PAIR), (0, SEQ)]),
                                        ALU.mult).then_inc(relation_ready, 1)

            def fraction(tile):
                b = tile.stream
                pool.wait_ge(rounded_ready, tile.t + 1)
                nc.gpsimd.tensor_tensor(embedding[:, b, :], relation[:, b, 0, :], relation[:, b, 1, :],
                                        ALU.subtract).then_inc(fraction_ready, 1)

            def divide(tile):
                b = tile.stream
                pool.wait_ge(recip_ready, tile.t + 1)
                nc.gpsimd.tensor_tensor(probs[:, b, :].rearrange("p (h k) -> p h k", k=SEQ),
                                        gated[:, b, :].rearrange("p (h k) -> p h k", k=SEQ),
                                        bcast(recip[:, b, :], [(1, HEADS), (0, SEQ)]), ALU.mult).then_inc(probs_ready, 1)

            def step(ahead, a, c):
                if a:
                    relate(a)
                if ahead:
                    spread_boxes(ahead)
                    tile_rstd(nc, pool, g, ahead, ln)
                if a:
                    fraction(a)
                    divide(a)

            first = Tile(0, 0, 0, T)
            spread_boxes(first)
            tile_rstd(nc, pool, g, first, ln)
            run_tiles(pool, tiles, T, parts, step)

        @block.vector
        def _(dve):
            nc.vector.memset(negmax[:, 0, 0:1], 0.0).then_inc(tile_done, T)

            def add_biases(tile):
                b = tile.stream
                dve.wait_ge(queries_projected, tile.t + 1)
                nc.vector.tensor_tensor(queries_T[:, b, :, :], ps[b][:, 0:1024].rearrange("p (c n) -> p c n", n=P),
                                        bcast(bq_cols[:, :], [(1, pairs), (0, P)]), ALU.add).then_inc(queries_ready, 1)
                dve.wait_ge(keys_projected, tile.t + 1)
                nc.vector.tensor_tensor(keys_T[:, b, :, :], ps[b][:, 1024:2048].rearrange("p (c n) -> p c n", n=P),
                                        bcast(bk_cols[:, :], [(1, pairs), (0, P)]), ALU.add).then_inc(keys_ready, 1)

            def floor(tile):
                b = tile.stream
                dve.wait_ge(magnitude_ready, tile.t + 1)
                nc.vector.tensor_scalar(relation[:, b, 1, :], relation[:, b, 0, :], floor_phase[:, 0:1], None,
                                        ALU.max).then_inc(floored_ready, 1)

            def whole_turns(tile):
                b = tile.stream
                dve.wait_ge(logs_ready, tile.t + 1)
                nc.vector.tensor_scalar(relation[:, b, 0, :], relation[:, b, 1, :], turns, floor_phase[:, 1:2], ALU.mult,
                                        ALU.add).then_inc(turns_ready, 1)
                dve.wait_ge(turns_ready, tile.t + 1)
                nc.vector.tensor_scalar(relation[:, b, 1, :], relation[:, b, 0, :], ROUND, -ROUND, ALU.add,
                                        ALU.add).then_inc(rounded_ready, 1)

            def shift_scores(tile):
                b = tile.stream
                dve.wait_ge(scores_ready, tile.t + 1)
                scores = ps[b][:, 0:1024].rearrange("p (h k) -> p h k", k=SEQ)
                nc.vector.tensor_reduce(negmax[:, b, :], scores, X, ALU.max, negate=True).then_inc(negmax_ready, 1)
                dve.wait_ge(negmax_ready, tile.t + 1)
                nc.vector.tensor_tensor(probs[:, b, :].rearrange("p (h k) -> p h k", k=SEQ), scores,
                                        bcast(negmax[:, b, :], [(1, HEADS), (0, SEQ)]), ALU.add).then_inc(shifted_scores, 1)

            def gate(tile):
                b = tile.stream
                dve.wait_ge(exp_ready, tile.t + 1)
                dve.wait_ge(gates_ready, tile.t + 1)
                nc.vector.scalar_tensor_tensor(gated[:, b, :], ps[b][:, 1024:2048], 1e-6, probs[:, b, :], ALU.max,
                                               ALU.mult).then_inc(gated_ready, 1)
                dve.wait_ge(gated_ready, tile.t + 1)
                nc.vector.tensor_reduce(total[:, b, :], gated[:, b, :].rearrange("p (h k) -> p h k", k=SEQ), X,
                                        ALU.add).then_inc(total_ready, 1)
                dve.wait_ge(total_ready, tile.t + 1)
                nc.vector.reciprocal(recip[:, b, :], total[:, b, :]).then_inc(recip_ready, 1)

            def add_output(tile):
                dve.wait_ge(output_ready, tile.t + 1)
                row = tile_of(g, tile.t)
                nc.vector.tensor_tensor(row, row, ps[tile.stream][:, 1024:1024 + P], ALU.add).then_inc(tile_done, 1)

            def step(ahead, a, c):
                if ahead:
                    tile_statistics(nc, g, ahead, ln)
                if a:
                    add_biases(a)
                    floor(a)
                if ahead:
                    tile_moments(nc, dve, ahead, ln)
                if a:
                    whole_turns(a)
                if ahead:
                    norm_tile(nc, dve, g, ahead, ln, normed, normed_ready)
                if a:
                    shift_scores(a)
                    gate(a)
                if c:
                    add_output(c)

            first = Tile(0, 0, 0, T)
            tile_statistics(nc, g, first, ln)
            tile_moments(nc, dve, first, ln)
            norm_tile(nc, dve, g, first, ln, normed, normed_ready)
            run_tiles(dve, tiles, T, parts, step)

        @block.scalar
        def _(act):
            def keep_inputs(tile):
                b = tile.stream
                act.wait_ge(inputs_turned, tile.t + 1)
                nc.scalar.copy(spread[:, b, :], ps[b][:, 512:512 + 2 * P + 16]).then_inc(spread_ready, 1)
                nc.scalar.copy(inputs_T[:, b, :, :].rearrange("p a n -> p (a n)"), ps[b][:, 0:2 * P]).then_inc(inputs_ready, 1)

            def keep_values(tile):
                b = tile.stream
                act.wait_ge(values_projected, tile.t + 1)
                for s in range(PAIR):
                    for h in range(2):
                        last = nc.scalar.copy(values[SEQ * h:SEQ * h + SEQ, b, s, :, :],
                                              ps[b][SEQ * s:SEQ * s + SEQ, 0:1024].rearrange("p (c h d) -> p c h d", h=2, d=heads_dim)[:, :, h, :])
                last.then_inc(values_ready, 1)

            def magnitude(tile):
                b = tile.stream
                act.wait_ge(relation_ready, tile.t + 1)
                nc.scalar.activation(relation[:, b, 0, :], relation[:, b, 0, :], ACT.Abs).then_inc(magnitude_ready, 1)

            def logs(tile):
                b = tile.stream
                act.wait_ge(floored_ready, tile.t + 1)
                nc.scalar.activation(relation[:, b, 1, :], relation[:, b, 1, :], ACT.Ln).then_inc(logs_ready, 1)

            def sines(tile):
                b = tile.stream
                act.wait_ge(fraction_ready, tile.t + 1)
                nc.scalar.activation(embedding[:, b, :], embedding[:, b, :], ACT.Sin, scale=6.283185).then_inc(embedding_ready, 1)

            def exponentials(tile):
                b = tile.stream
                act.wait_ge(shifted_scores, tile.t + 1)
                nc.scalar.activation(probs[:, b, :], probs[:, b, :], ACT.Exp, scale=scale).then_inc(exp_ready, 1)

            def keep_turned(tile):
                b = tile.stream
                act.wait_ge(probs_turned, tile.t + 1)
                nc.scalar.copy(probs_T[:, b, :, :].rearrange("p c n -> p (c n)"), ps[b][:, 1024:2048]).then_inc(probs_kept, 1)

            def keep_attended(tile):
                b = tile.stream
                act.wait_ge(attended_ready, tile.t + 1)
                nc.scalar.copy(attended_T[:, b, :, :].rearrange("p c n -> p (c n)"), ps[b][:, 0:1024]).then_inc(attended_kept, 1)

            def step(ahead, a, c):
                if a:
                    keep_inputs(a)
                    magnitude(a)
                if c:
                    keep_turned(c)
                if a:
                    logs(a)
                    keep_values(a)
                    sines(a)
                if c:
                    keep_attended(c)
                if a:
                    exponentials(a)

            run_tiles(act, tiles, T, parts, step)

        @block.tensor
        def _(pe):
            def turn_inputs(tile):
                b = tile.stream
                pe.wait_ge(normed_ready, tile.t + 1)
                nc.tensor.transpose(ps[b][:, 0:P], normed[:, b, :], g.ident[:, :])
                pe.wait_ge(context_loaded[b], tile.loads + 16)
                nc.tensor.transpose(ps[b][:, P:2 * P], context_in[:, b, :], g.ident[:, :])
                pe.wait_ge(boxes_spread, tile.t + 1)
                for m in range(2):
                    nc.tensor.transpose(ps[b][:, 512 + P * m:512 + P * m + P], query_boxes[:, b, m, :], g.ident[:, :])
                for m in range(2):
                    last = nc.tensor.matmul(ps[b][:, 768 + 8 * m:768 + 8 * m + 8], key_boxes[:, b, m, :], block_of[:, :],
                                            start=True, stop=True)
                last.then_inc(inputs_turned, 1)

            def project_queries_and_keys(tile):
                b = tile.stream
                pe.wait_ge(inputs_ready, tile.t + 1)
                pe.wait_ge(spread_ready, tile.t + 1)
                for c in range(pairs):
                    last = nc.tensor.matmul(ps[b][:, P * c:P * c + P], wqT[:, P * c:P * c + P], inputs_T[:, b, 0, :], start=True, stop=True)
                last.then_inc(queries_projected, 1)
                pe.wait_ge(tile_done, tile.t + 1)
                for c in range(pairs):
                    last = nc.tensor.matmul(ps[b][:, 1024 + P * c:1024 + P * c + P], wkT[:, P * c:P * c + P], inputs_T[:, b, 1, :],
                                            start=True, stop=True)
                last.then_inc(keys_projected, 1)

            def project_values(tile):
                b = tile.stream
                pe.wait_ge(queries_ready, tile.t + 1)
                for c in range(2):
                    last = nc.tensor.matmul(ps[b][:, 512 * c:512 * c + 512], inputs_T[:, b, 1, :], wvT[:, 512 * c:512 * c + 512],
                                            start=True, stop=True)
                last.then_inc(values_projected, 1)

            def score(tile, turn):
                b = tile.stream
                if turn == 0:
                    pe.wait_ge(keys_ready, tile.t + 1)
                    pe.wait_ge(values_ready, tile.t + 1)
                else:
                    pe.wait_ge(scores_half, tile.t + 1)
                takes_the_wait(nc, g, ps[b][:, 0:1])
                for c in range(pairs):
                    for h in range(2):
                        rows, s = slice(SEQ * h, SEQ * h + SEQ), (h + turn) % PAIR
                        cols = slice(SEQ * s, SEQ * s + SEQ)
                        last = nc.tensor.matmul(ps[b][cols, P * c + SEQ * h:P * c + SEQ * h + SEQ], queries_T[rows, b, c, cols],
                                                keys_T[rows, b, c, cols], start=True, stop=True)
                last.then_inc(scores_ready if turn else scores_half, 1)

            def make_gates(tile):
                b = tile.stream
                pe.wait_ge(embedding_ready, tile.t + 1)
                gates = ps[b][:, 1024:2048].rearrange("p (h k) -> p h k", k=SEQ)
                for c in range(blocks):
                    for half in range(2):
                        hs = slice(8 * half, 8 * half + 8)
                        out = gates[:, hs, keys_at_once * c:keys_at_once * (c + 1)]
                        nc.tensor.matmul(out, g.ones_bf[0:3 * 32, :], gate_bias_parts.rows[:, P * half:P * half + P], start=True, stop=False,
                                         skip_group_check=True)
                        last = nc.tensor.matmul(out, embedding[:, b, P * c:P * c + P], gate_weights[:, hs, :], start=False, stop=True,
                                                skip_group_check=True)
                last.then_inc(gates_ready, 1)

            def turn_probs(tile):
                b = tile.stream
                pe.wait_ge(probs_ready, tile.t + 1)
                for c in range(pairs):
                    last = nc.tensor.transpose(ps[b][:, 1024 + P * c:1024 + P * c + P], probs[:, b, P * c:P * c + P], g.ident[:, :])
                last.then_inc(probs_turned, 1)

            def attend(tile):
                b = tile.stream
                pe.wait_ge(probs_kept, tile.t + 1)
                takes_the_wait(nc, g, ps[b][:, 0:1])
                for c in range(pairs):
                    for s in range(PAIR):
                        for h in range(2):
                            rows, cols = slice(SEQ * h, SEQ * h + SEQ), slice(SEQ * s, SEQ * s + SEQ)
                            last = nc.tensor.matmul(ps[b][rows, P * c + SEQ * s:P * c + SEQ * s + SEQ], values[rows, b, s, c, :],
                                                    probs_T[rows, b, c, cols], start=True, stop=True)
                last.then_inc(attended_ready, 1)

            def put_out(tile):
                b = tile.stream
                pe.wait_ge(attended_kept, tile.t + 1)
                out = ps[b][:, 1024:1024 + P]
                nc.tensor.matmul(out, g.ones_bf[0:3 * 32, :], out_bias_parts.rows[:, :], start=True, stop=False)
                for c in range(pairs):
                    last = nc.tensor.matmul(out, attended_T[:, b, c, :], woT[:, c, :], start=False, stop=c == pairs - 1)
                last.then_inc(output_ready, 1)

            def step(ahead, a, c):
                if a:
                    turn_inputs(a)
                    project_queries_and_keys(a)
                if c:
                    turn_probs(c)
                if a:
                    project_values(a)
                if c:
                    attend(c)
                if a:
                    score(a, 0)
                    score(a, 1)
                    make_gates(a)
                if c:
                    put_out(c)

            run_tiles(pe, tiles, T, parts, step)

    ph.end()


EXPERTS = 8


def route(nc, ph, g, psum, normed_T, weights, gate_T, capacity, constants, ln_rows=None):
    sb, sem = ph.sb, ph.sem
    tiles = g.tiles
    groups = tiles // STREAMS
    affine = ln_rows is not None
    lns = [LayernormState(ph, f"_{n}") for n in range(2)]
    normed = sb("normed", [P, 2, STREAMS, P])
    route_T = sb("route_T", [P, 2, STREAMS, P])
    logits = sb("logits", [P, tiles, EXPERTS])
    normed_ready = sem("normed_ready")
    scaled_ready = sem("scaled_ready")
    shifted_ready = sem("shifted_ready")
    tokens_turned = sem("tokens_turned")
    tokens_kept = sem("tokens_kept")
    logits_ready = sem("logits_ready")
    logits_kept = sem("logits_kept")
    norm_ready = shifted_ready if affine else normed_ready
    turned = [psum[:, b, :] for b in range(2)]
    logit_bank = [psum[:, 2 + b, 0:STREAMS * EXPERTS] for b in range(2)]
    with nc.Block() as block:
        @block.vector
        def _(dve):
            def norm(i, b):
                n0 = i * 2
                dve.wait_ge(logits_kept, n0 + (b + 1))
                dve.wait_ge(lns[b].rstd_ready, i + 1)
                for s in range(STREAMS):
                    last = nc.vector.tensor_scalar(normed[:, b, s, :], tile_of(g, (n0 + b) * STREAMS + s), lns[b].mean_var[:, s, 0:1],
                                                   lns[b].rstd[:, s:s + 1], ALU.subtract, ALU.mult)
                last.then_inc(normed_ready, 1)

            nc.vector.memset(logits[:, 0, 0:1], 0.0).then_inc(logits_kept, 2)
            norm_groups(nc, dve, g, lns, norm)

        @block.gpsimd
        def _(pool):
            with pool.Fori(0, groups // 2) as i:
                n0 = pool.snap(i * 2)
                for b in range(2):
                    group_rstd(nc, pool, g, i, lns[b])
                    if affine:
                        pool.wait_ge(normed_ready, n0 + (b + 1))
                        nc.gpsimd.tensor_tensor(normed[:, b, :, :], normed[:, b, :, :], bcast(ln_rows[0][:, :], [(0, STREAMS), (1, P)]),
                                                ALU.mult).then_inc(scaled_ready, 1)
                        pool.wait_ge(scaled_ready, n0 + (b + 1))
                        nc.gpsimd.tensor_tensor(normed[:, b, :, :], normed[:, b, :, :], bcast(ln_rows[1][:, :], [(0, STREAMS), (1, P)]),
                                                ALU.add).then_inc(shifted_ready, 1)

        @block.tensor
        def _(pe):
            with pe.Fori(0, groups // 2) as i:
                n0 = pe.snap(i * 2)
                for b in range(2):
                    pe.wait_ge(norm_ready, n0 + (b + 1))
                    for s in range(STREAMS):
                        last = nc.tensor.transpose(turned[b][:, P * s:P * s + P], normed[:, b, s, :], g.ident[:, :])
                    last.then_inc(tokens_turned, 1)
                for b in range(2):
                    pe.wait_ge(tokens_kept, n0 + (b + 1))
                    for s in range(STREAMS):
                        last = nc.tensor.matmul(logit_bank[b][:, EXPERTS * s:EXPERTS * s + EXPERTS],
                                                route_T[:, b, s, :], gate_T[:, :], start=True, stop=True)
                    last.then_inc(logits_ready, 1)

        @block.scalar
        def _(act):
            with act.Fori(0, groups // 2) as i:
                n0 = act.snap(i * 2)
                for b in range(2):
                    act.wait_ge(tokens_turned, n0 + (b + 1))
                    nc.scalar.copy(route_T[:, b, :, :].rearrange("p s n -> p (s n)"), turned[b])
                    nc.scalar.copy(normed_T[:, bass.ds((n0 + b) * STREAMS, STREAMS), :].rearrange("p s n -> p (s n)"),
                                   turned[b]).then_inc(tokens_kept, 1)
                for b in range(2):
                    act.wait_ge(logits_ready, n0 + (b + 1))
                    nc.scalar.copy(logits[:, bass.ds((n0 + b) * STREAMS, STREAMS), :].rearrange("p t e -> p (t e)"),
                                   logit_bank[b]).then_inc(logits_kept, 1)

    order = sb("order", [P, EXPERTS])
    before = sb("before", [P, P])
    loaded, step, exp_step, counted = sem("rank_loaded"), sem("rank_step"), sem("rank_exp"), sem("rank_counted")
    best = [sb(f"best_{j}", [P, tiles]) for j in range(2)]
    first = [sb(f"first_{j}", [P, tiles]) for j in range(2)]
    chosen = [sb(f"chosen_{j}", [P, tiles, EXPERTS]) for j in range(2)]
    hit = sb("hit", [P, tiles, EXPERTS])
    ranked = sb("ranked", [P, tiles, EXPERTS])
    gap = sb("gap", [P, tiles])
    gate = [sb(f"gate_{j}", [P, tiles]) for j in range(2)]
    ones_row = sb("scan_ones", [P, tiles])
    counts = sb("counts", [P, tiles, EXPERTS])
    passed = [sb(f"passed_{j}", [P, tiles + 1, EXPERTS]) for j in range(2)]
    place = sb("place", [P, tiles, EXPERTS])
    flat = lambda t: t[:, :, :].rearrange("p t e -> p (t e)")
    over = lambda t: bcast(t[:, :], [(1, tiles), (0, EXPERTS)])
    with nc.Block() as block:
        @block.sync
        def _(sp):
            sp.dma_start(order[:, :], constants["order"]).then_inc(loaded, 16)
            sp.dma_start(before[:, :], constants["before"]).then_inc(loaded, 16)
            sp.wait_ge(loaded, 32)

        @block.scalar
        def _(act):
            act.wait_ge(exp_step, 1)
            nc.scalar.activation(gap[:, :], gap[:, :], ACT.Exp).then_inc(exp_step, 1)

        @block.tensor
        def _(pe):
            if capacity is not None:
                pe.wait_ge(loaded, 32)
                pe.wait_ge(counted, 1)
                for j in range(2):
                    nc.tensor.matmul(psum[:, 2 * j, 0:tiles * EXPERTS], before[:, :], flat(chosen[j]), start=True, stop=True)
                    last = nc.tensor.matmul(psum[:, 2 * j + 1, 0:tiles * EXPERTS], g.ones_full[:, :], flat(chosen[j]), start=True, stop=True)
                last.then_inc(counted, 1)

        @block.vector
        def _(dve):
            done = [0]

            def then(instruction):
                done[0] += 1
                instruction.then_inc(step, 1)
                dve.wait_ge(step, done[0])

            dve.wait_ge(loaded, 32)
            source = logits
            for j in range(2):
                then(nc.vector.tensor_reduce(best[j][:, :], source[:, :, :], X, ALU.max))
                then(nc.vector.tensor_tensor(hit[:, :, :], source[:, :, :], over(best[j]), ALU.is_equal))
                then(nc.vector.tensor_tensor(hit[:, :, :], hit[:, :, :], bcast(order[:, :], [(0, tiles), (1, EXPERTS)]), ALU.mult))
                then(nc.vector.tensor_reduce(first[j][:, :], hit[:, :, :], X, ALU.max))
                then(nc.vector.tensor_tensor(chosen[j][:, :, :], hit[:, :, :], over(first[j]), ALU.is_equal))
                if j == 0:
                    then(nc.vector.scalar_tensor_tensor(flat(ranked), flat(chosen[0]), MASKED, flat(logits), ALU.mult, ALU.add))
                    source = ranked
            nc.vector.tensor_tensor(gap[:, :], best[1][:, :], best[0][:, :], ALU.subtract).then_inc(exp_step, 1)
            dve.wait_ge(exp_step, 2)
            then(nc.vector.tensor_scalar(gate[0][:, :], gap[:, :], 1.0, None, ALU.add))
            then(nc.vector.reciprocal(gate[0][:, :], gate[0][:, :]))
            then(nc.vector.tensor_tensor(gate[1][:, :], gate[0][:, :], gap[:, :], ALU.mult))
            if capacity is not None:
                then(nc.vector.memset(ones_row[:, :], 1.0))
                nc.vector.memset(passed[0][:, 0:1, :], 0.0).then_inc(counted, 1)
                dve.wait_ge(counted, 2)
                for j in range(2):
                    then(nc.vector.tensor_copy(flat(counts), psum[:, 2 * j + 1, 0:tiles * EXPERTS]))
                    if j == 1:
                        then(nc.vector.tensor_copy(passed[1][:, 0:1, :], passed[0][:, tiles:tiles + 1, :]))
                    for e in range(EXPERTS):
                        last = nc.vector.tensor_tensor_scan(passed[j][:, 1:tiles + 1, e], ones_row[:, :], counts[:, :, e],
                                                            passed[j][:, 0:1, e], ALU.mult, ALU.add)
                    then(last)
                    then(nc.vector.tensor_tensor(flat(place), psum[:, 2 * j, 0:tiles * EXPERTS],
                                                 passed[j][:, 0:tiles, :].rearrange("p t e -> p (t e)"), ALU.add))
                    then(nc.vector.scalar_tensor_tensor(flat(chosen[j]), flat(place), float(capacity), flat(chosen[j]), ALU.is_lt, ALU.mult))
            then(nc.vector.tensor_tensor(hit[:, :, :], chosen[0][:, :, :], over(gate[0]), ALU.mult))
            then(nc.vector.tensor_tensor(ranked[:, :, :], chosen[1][:, :, :], over(gate[1]), ALU.mult))
            nc.vector.tensor_tensor(weights[:, :, :], hit[:, :, :], ranked[:, :, :], ALU.add)


def capacity_experts_phase(nc, g, gate_w, fc1_w, fc1_b, fc2_w, fc2_b, constants):
    tiles = g.tiles
    groups = tiles // STREAMS
    hidden = fc1_w.shape[1]
    chunks = hidden // P
    tokens = tiles * P
    capacity = 2 * ((tokens + EXPERTS - 1) // EXPERTS)
    width = STREAMS * P
    ph = Phase(nc, "l2f")
    sb, sem = ph.sb, ph.sem
    psum = ph.psum()
    normed_T = sb("normed_T", [P, tiles, P])
    weights = sb("weights", [P, tiles, EXPERTS])
    fc1_T = sb("fc1_T", [P, EXPERTS, chunks, P])
    fc2 = sb("fc2", [P, EXPERTS, chunks, P])
    raw = sb("raw", [P, EXPERTS, chunks, P])
    fc1_bias = sb("fc1_bias", [P, EXPERTS, chunks])
    gate_raw, gate_T = sb("gate_raw", [EXPERTS, P]), sb("gate_T", [P, EXPERTS])
    out_bias = sb("out_bias", [STREAMS * EXPERTS, STREAMS, P])
    spread_bias = sb("spread_bias", [STREAMS * EXPERTS, STREAMS, P])
    own_tile = sb("own_tile", [STREAMS * EXPERTS, STREAMS])
    loads = [(raw[:, :, :, :].rearrange("p e c d -> p (e c) d"), fc1_w.rearrange("e (c p) d -> p (e c) d", p=P)),
             (fc2[:, :, :, :].rearrange("p e c d -> p (e c) d"), fc2_w.rearrange("e (c p) d -> p (e c) d", p=P)),
             (fc1_bias[:, :, :].rearrange("p e c -> p (e c)"), fc1_b.rearrange("e o (c p) -> p (e o c)", p=P)),
             (gate_raw[:, :], gate_w), (own_tile[:, :], constants["own_tile"])]
    for s in range(STREAMS):
        for r in range(STREAMS):
            loads.append((out_bias[EXPERTS * s:EXPERTS * s + EXPERTS, r, :], fc2_b.rearrange("e o d -> (e o) d")))
    turned = [(fc1_T[:, e, c, :], raw[:, e, c, :]) for e in range(EXPERTS) for c in range(chunks)]
    turned.append((gate_T[:, :], gate_raw[:, :]))
    transpose_weights(nc, ph, loads, turned, g.ident, psum)
    route(nc, ph, g, psum, normed_T, weights, gate_T, capacity, constants)

    items = EXPERTS * chunks
    hidden_buf = sb("hidden_buf", [P, 4, width])
    group_weights = sb("group_weights", [P, STREAMS * EXPERTS])
    group_weights_T = sb("group_weights_T", [STREAMS * EXPERTS, P])
    bias_spread = sem("bias_spread")
    banks_free = sem("banks_free")
    group_weights_ready = sem("group_weights_ready")
    weights_turned = sem("weights_turned")
    weights_kept = sem("weights_kept")
    bias_ready = sem("bias_ready")
    bias_added = sem("bias_added")
    hidden_raw = sem("hidden_raw")
    hidden_ready = sem("hidden_ready")
    expert_ready = sem("expert_ready")
    raw_bank = [psum[:, n, :] for n in range(4)]
    sum_bank = [psum[:, 4 + n, :] for n in range(2)]
    bias_bank, turn_bank = psum[:, 6, :], psum[:, 7, :]
    rows = slice(0, STREAMS * EXPERTS)
    with nc.Block() as block:
        @block.vector
        def _(dve):
            nc.vector.tensor_tensor(spread_bias[:, :, :], out_bias[:, :, :], bcast(own_tile[:, :], [(1, STREAMS), (0, P)]),
                                    ALU.mult).then_inc(bias_spread, 1)
            dve.wait_ge(bias_spread, 1)
            nc.vector.memset(group_weights[:, :], 0.0).then_inc(banks_free, 2)
            dve.wait_ge(banks_free, 2)
            with dve.Fori(0, groups) as i:
                t0 = dve.snap(i * STREAMS)
                e0 = dve.snap(i * EXPERTS)
                dve.wait_ge(banks_free, e0 + 2)
                nc.vector.tensor_copy(group_weights[:, :], weights[:, bass.ds(t0, STREAMS), :].rearrange("p t e -> p (t e)")).then_inc(group_weights_ready, 1)
                dve.wait_ge(bias_ready, i + 1)
                row = g.x[:, bass.ds(t0, STREAMS), :].rearrange("p t d -> p (t d)")
                nc.vector.tensor_tensor(row, row, bias_bank, ALU.add).then_inc(bias_added, 1)
                dve.wait_ge(bias_added, i + 1)
                for e in range(EXPERTS):
                    dve.wait_ge(expert_ready, e0 + (e + 1))
                    dve.wait_ge(banks_free, e0 + (e + 2))
                    for s in range(STREAMS):
                        row = tile_of(g, t0 + s)
                        c = EXPERTS * s + e
                        last = nc.vector.scalar_tensor_tensor(row, sum_bank[e % 2][:, P * s:P * s + P], group_weights[:, c:c + 1], row,
                                                              ALU.mult, ALU.add)
                    last.then_inc(banks_free, 1)

        @block.scalar
        def _(act):
            with act.Fori(0, groups) as i:
                n0 = act.snap(i * items)
                act.wait_ge(weights_turned, i + 1)
                nc.scalar.copy(group_weights_T[:, :], turn_bank[rows, 0:P]).then_inc(weights_kept, 1)
                for n in range(items):
                    e, c = n // chunks, n % chunks
                    act.wait_ge(hidden_raw, n0 + (n + 1))
                    nc.scalar.activation(hidden_buf[:, n % 4, :], raw_bank[n % 4], ACT.Relu, bias=fc1_bias[:, e, c:c + 1]).then_inc(hidden_ready, 1)

        @block.tensor
        def _(pe):
            pe.wait_ge(bias_spread, 1)
            with pe.Fori(0, groups) as i:
                t0 = pe.snap(i * STREAMS)
                n0 = pe.snap(i * items)
                e0 = pe.snap(i * EXPERTS)
                tokens_T = normed_T[:, bass.ds(t0, STREAMS), :].rearrange("p t n -> p (t n)")
                pe.wait_ge(group_weights_ready, i + 1)
                nc.tensor.transpose(turn_bank[rows, 0:P], group_weights[:, :], g.ident[:, :]).then_inc(weights_turned, 1)
                for n in range(items + 2):
                    if n < items:
                        nc.tensor.matmul(raw_bank[n % 4], fc1_T[:, n // chunks, n % chunks, :], tokens_T, start=True, stop=True).then_inc(hidden_raw, 1)
                    if n == 0:
                        pe.wait_ge(weights_kept, i + 1)
                        nc.tensor.matmul(bias_bank, group_weights_T[:, :], spread_bias[:, :, :].rearrange("p s d -> p (s d)"),
                                         start=True, stop=True).then_inc(bias_ready, 1)
                    if n >= 2:
                        m = n - 2
                        e, c = m // chunks, m % chunks
                        pe.wait_ge(hidden_ready, n0 + (m + 1))
                        if c == 0:
                            pe.wait_ge(banks_free, e0 + (e + 1))
                        for s in range(STREAMS):
                            last = nc.tensor.matmul(sum_bank[e % 2][:, P * s:P * s + P], hidden_buf[:, m % 4, P * s:P * s + P], fc2[:, e, c, :],
                                                    start=c == 0 and s == 0, stop=c == chunks - 1, skip_group_check=True)
                        if c == chunks - 1:
                            last.then_inc(expert_ready, 1)

    ph.end()


def normalize_phase(nc, g):
    ph = Phase(nc, "norm")
    lns = [LayernormState(ph, f"_{n}") for n in range(2)]
    x_normed = ph.sem("x_normed")
    with nc.Block() as block:
        @block.gpsimd
        def _(pool):
            with pool.Fori(0, g.tiles // STREAMS // 2) as i:
                for n in range(2):
                    group_rstd(nc, pool, g, i, lns[n])

        @block.vector
        def _(dve):
            def norm(i, n):
                dve.wait_ge(lns[n].rstd_ready, i + 1)
                for s in range(STREAMS):
                    row = tile_of(g, (i * 2 + n) * STREAMS + s)
                    nc.vector.tensor_scalar(row, row, lns[n].mean_var[:, s, 0:1], lns[n].rstd[:, s:s + 1],
                                            ALU.subtract, ALU.mult).then_inc(x_normed, 1)

            norm_groups(nc, dve, g, lns, norm)

    ph.end()


def gated_experts_phase(nc, g, x_before, ln_scale, ln_shift, gate_w, w1, w2, w3, constants):
    tiles = g.tiles
    groups = tiles // STREAMS
    hidden = w1.shape[2]
    chunks = hidden // P
    width = STREAMS * P
    ph = Phase(nc, "l3e")
    sb, sem = ph.sb, ph.sem
    psum = ph.psum()
    normed_T = sb("normed_T", [P, tiles, P])
    weights = sb("weights", [P, tiles, EXPERTS])
    w1_in, w2_in = sb("w1_in", [P, EXPERTS, hidden]), sb("w2_in", [P, EXPERTS, hidden])
    w3_in = sb("w3_in", [P, EXPERTS, chunks, P])
    gate_T = sb("gate_T", [P, EXPERTS])
    ln_rows = (sb("ln_scale", [P, P]), sb("ln_shift", [P, P]))
    loads = [(w1_in[:, :, :], w1.rearrange("e d h -> d e h")), (w2_in[:, :, :], w2.rearrange("e d h -> d e h")),
             (w3_in[:, :, :, :].rearrange("p e c d -> p (e c) d"), w3.rearrange("e (c p) d -> p (e c) d", p=P)), (gate_T[:, :], gate_w),
             (ln_rows[0][:, :], row_on_all(ln_scale, P)), (ln_rows[1][:, :], row_on_all(ln_shift, P))]
    transpose_weights(nc, ph, loads, [], g.ident, psum)
    route(nc, ph, g, psum, normed_T, weights, gate_T, None, constants, ln_rows)

    items = EXPERTS * chunks
    act_buf = sb("act_buf", [P, 2, width])
    hidden_buf = sb("hidden_buf", [P, 2, width])
    before_added = sem("before_added")
    banks_free = sem("banks_free")
    gate_raw = sem("gate_raw")
    up_raw = sem("up_raw")
    act_ready = sem("act_ready")
    hidden_ready = sem("hidden_ready")
    expert_ready = sem("expert_ready")
    gate_bank = [psum[:, n, :] for n in range(2)]
    up_bank = [psum[:, 2 + n, :] for n in range(2)]
    sum_bank = [psum[:, 4 + n, :] for n in range(2)]
    with nc.Block() as block:
        @block.vector
        def _(dve):
            nc.vector.memset(act_buf[:, 0, 0:1], 0.0).then_inc(banks_free, 2)
            with dve.Fori(0, groups) as i:
                t0 = dve.snap(i * STREAMS)
                e0 = dve.snap(i * EXPERTS)
                n0 = dve.snap(i * items)

                row = g.x[:, bass.ds(t0, STREAMS), :].rearrange("p t d -> p (t d)")
                nc.vector.tensor_tensor(row, row, x_before[:, bass.ds(t0, STREAMS), :].rearrange("p t d -> p (t d)"),
                                        ALU.add).then_inc(before_added, 1)
                dve.wait_ge(before_added, i + 1)

                def add(e):
                    dve.wait_ge(expert_ready, e0 + (e + 1))
                    dve.wait_ge(banks_free, e0 + (e + 2))
                    for s in range(STREAMS):
                        row = tile_of(g, t0 + s)
                        last = nc.vector.scalar_tensor_tensor(row, sum_bank[e % 2][:, P * s:P * s + P],
                                                              weights[:, bass.ds(t0 + s, 1), e:e + 1].rearrange("p a e -> p (a e)"), row,
                                                              ALU.mult, ALU.add)
                    last.then_inc(banks_free, 1)

                for n in range(items):
                    dve.wait_ge(act_ready, n0 + (n + 1))
                    dve.wait_ge(up_raw, n0 + (n + 1))
                    nc.vector.tensor_tensor(hidden_buf[:, n % 2, :], act_buf[:, n % 2, :], up_bank[n % 2], ALU.mult).then_inc(hidden_ready, 1)
                    if n % chunks == 1 and n >= chunks:
                        add(n // chunks - 1)
                add(EXPERTS - 1)

        @block.scalar
        def _(act):
            act.wait_ge(banks_free, 2)
            with act.Fori(0, groups) as i:
                n0 = act.snap(i * items)
                for n in range(items):
                    act.wait_ge(gate_raw, n0 + (n + 1))
                    nc.scalar.activation(act_buf[:, n % 2, :], gate_bank[n % 2], ACT.Silu).then_inc(act_ready, 1)

        @block.tensor
        def _(pe):
            with pe.Fori(0, groups) as i:
                t0 = pe.snap(i * STREAMS)
                n0 = pe.snap(i * items)
                e0 = pe.snap(i * EXPERTS)
                tokens_T = normed_T[:, bass.ds(t0, STREAMS), :].rearrange("p t n -> p (t n)")
                for n in range(items + 1):
                    if n < items:
                        cols = slice(P * (n % chunks), P * (n % chunks) + P)
                        nc.tensor.matmul(gate_bank[n % 2], w1_in[:, n // chunks, cols], tokens_T, start=True, stop=True).then_inc(gate_raw, 1)
                        nc.tensor.matmul(up_bank[n % 2], w2_in[:, n // chunks, cols], tokens_T, start=True, stop=True).then_inc(up_raw, 1)
                    if n >= 1:
                        m = n - 1
                        e, c = m // chunks, m % chunks
                        pe.wait_ge(hidden_ready, n0 + (m + 1))
                        if c == 0:
                            pe.wait_ge(banks_free, e0 + (e + 1))
                        for s in range(STREAMS):
                            last = nc.tensor.matmul(sum_bank[e % 2][:, P * s:P * s + P], hidden_buf[:, m % 2, P * s:P * s + P], w3_in[:, e, c, :],
                                                    start=c == 0 and s == 0, stop=c == chunks - 1, skip_group_check=True)
                        if c == chunks - 1:
                            last.then_inc(expert_ready, 1)

    ph.end()



def program(nc, d, out):
    tokens, width = d["x"].shape[0] * d["x"].shape[1], d["x"].shape[2]
    tiles = tokens // P
    x_tiles = d["x"].rearrange("(t a) s d -> (a s) t d", a=PAIR)
    out_tiles = out.rearrange("(t a) s d -> (a s) t d", a=PAIR)
    context = d["ctx_1024"].rearrange("(t a) s d -> t (a s) d", a=PAIR)
    key_mask = d["mask_BxS2_ik0"].rearrange("(t a) k -> t a k", a=PAIR)
    with ExitStack() as ctx:
        def sb(label, shape, dt=F32):
            return ctx.enter_context(nc.sbuf_tensor(label, shape, dt))

        g = Resident(sb, tiles)
        x_loaded = ctx.enter_context(nc.semaphore("x_loaded"))
        ident_ready = ctx.enter_context(nc.semaphore("ident_ready"))
        out_stored = ctx.enter_context(nc.semaphore("out_stored"))
        with nc.Block() as block:
            @block.sync
            def _(sp):
                sp.dma_start(g.ident[:, :], d["const_ident"]).then_inc(ident_ready, 16)
                sp.dma_start(g.group_mask[:, :], d["const_group_mask"]).then_inc(x_loaded, 16)
                sp.dma_start(g.x[:, :, :], x_tiles).then_inc(x_loaded, 16)
                sp.wait_ge(x_loaded, 32)

            @block.vector
            def _(dve):
                nc.vector.memset(g.ones_bf[:, :], 1.0)
                nc.vector.memset(g.ones_full[:, :], 1.0)
                nc.vector.memset(g.minus_half[:, :], -0.5)
                dve.wait_ge(ident_ready, 16)
                nc.vector.tensor_copy(g.ident_bf[:, :], g.ident[:, :])

        def w(layer, key):
            return d[f"{layer}_{key}"]

        attention_phase(nc, "l0x", g, *[w("L0_xattn", k) for k in ("Wq", "bq", "Wk", "bk", "Wv", "bv", "Wo", "bo")],
                        context=context, key_mask=key_mask)
        int8_ffn_phase(nc, g, *[w("L0_ffn", k) for k in ("weight_int8", "weight_scale", "bias")])
        attention_phase(nc, "l1x", g, wo=w("L1_xattn", "Wo"), context=context)

        ternary_ffn_phase(nc, g, *[w("L1_ffn", k) for k in ("norm1_w", "w1", "act_scale", "act_bias", "norm2_w", "w2")])

        box_attention_phase(nc, g, d["fside_BxSx4_0"].rearrange("(t a) s d -> (a s) t d", a=PAIR),
                            context,
                            *[w("L2_xattn", k) for k in ("Wq", "bq", "Wk", "bk", "Wv", "bv", "Wo", "bo", "Wg", "bg")],
                            {k: d["const_" + k] for k in ("same_key", "block_of", "diagonal", "floor_phase")})

        ranking = {k: d["const_" + k] for k in ("order", "before", "own_tile")}
        capacity_experts_phase(nc, g, *[w("L2_ffn", k) for k in ("gate_w", "fc1_w", "fc1_b", "fc2_w", "fc2_b")], ranking)
        attention_phase(nc, "l3x", g, *[w("L3_xattn", k) for k in ("Wq", "bq", "Wk", "bk", "Wv", "bv", "Wo", "bo")],
                        context=context, score_mask=d["mask_1x1xSxS2_ff0"].rearrange("a b q k -> (a b q) k"))
        x_before = sb("x_before", [P, tiles, P])
        with nc.Block() as block:
            @block.vector
            def _(dve):
                nc.vector.tensor_copy(x_before[:, :, :], g.x[:, :, :])
        normalize_phase(nc, g)

        attention_phase(nc, "l3a", g, wq=w("L3_ffn", "wq"), wk=w("L3_ffn", "wk"), wv=w("L3_ffn", "wv"), wo=w("L3_ffn", "wo"),
                        bo=w("L3_ffn", "bo"), weights_turned=True, score_mask=d["const_causal"],
                        ln_scale=w("L3_ffn", "ln1_scale"), ln_shift=w("L3_ffn", "ln1_shift"))
        gated_experts_phase(nc, g, x_before, *[w("L3_ffn", k) for k in ("ln2_scale", "ln2_shift", "gate_w", "w1", "w2", "w3")],
                            ranking)

        with nc.Block() as block:
            @block.sync
            def _(sp):
                sp.dma_start(out_tiles, g.x[:, :, :]).then_inc(out_stored, 16)
                sp.wait_ge(out_stored, 16)



def kernel(**inputs):
    import numpy as np
    import concourse.bacc as bacc
    from concourse.bass_utils import run_bass_kernel_spmd

    p = np.arange(P)
    constants = {
        "const_ident": np.eye(P, dtype=np.float32),
        "const_group_mask": (p[:, None] % 32 // HD == np.arange(GROUP)[None, :]).astype(np.float32),
    }
    key, feature = p // 8, p % 8
    constants["const_same_key"] = (p[:, None] % 16 == key[None, :]).astype(np.float32)
    constants["const_block_of"] = (p[:, None] // 16 == np.arange(8)[None, :]).astype(np.float32)
    constants["const_diagonal"] = (key[:, None] == np.arange(16)[None, :]).astype(np.float32)
    constants["const_floor_phase"] = np.stack([np.where(feature % 4 < 2, 1e-3, 0.0), np.where(feature < 4, 0.0, 0.25)], 1).astype(np.float32)
    constants["const_causal"] = np.where(np.arange(SEQ)[:, None] < np.arange(SEQ)[None, :], MASKED, 0.0).astype(np.float32)
    constants["const_order"] = np.broadcast_to(np.arange(EXPERTS, 0, -1, dtype=np.float32), (P, EXPERTS)).copy()
    constants["const_before"] = (p[:, None] < p[None, :]).astype(np.float32)
    constants["const_own_tile"] = (np.arange(STREAMS * EXPERTS)[:, None] // EXPERTS == np.arange(STREAMS)[None, :]).astype(np.float32)
    nc = bacc.Bacc("TRN2", target_bir_lowering=False, num_devices=1)
    arrays, d = {}, {}
    for name, a in list(inputs.items()) + list(constants.items()):
        a = np.ascontiguousarray(a)
        if a.dtype.kind in "iu":
            a = a.astype(np.int32)
        arrays[name] = a
        d[name] = nc.dram_tensor(name, a.shape, mybir.dt.from_np(a.dtype), kind="ExternalInput").ap()
    out = nc.dram_tensor("out", inputs["x"].shape, F32, kind="ExternalOutput").ap()
    program(nc, d, out)
    result = run_bass_kernel_spmd(nc, [arrays], core_ids=[0])
    return result.results[0]["out"]
```
